# Optimizing a Trainium2 kernel written in Bass

```python
import numpy as np
import jax
import jax.numpy as jnp

def _softmax(x, axis=-1):
    return jax.nn.softmax(x, axis=axis)

def _gelu(x):
    return jax.nn.gelu(x, approximate=True)

def _silu(x):
    return jax.nn.silu(x)

def _sigmoid(x):
    return jax.nn.sigmoid(x)

def _layernorm(x, axis=-1, eps=1e-05):
    m = jnp.mean(x, axis=axis, keepdims=True)
    v = jnp.var(x, axis=axis, keepdims=True)
    return (x - m) / jnp.sqrt(v + eps)

def _scatter_add(tgt, idx, src, axis=0):
    return tgt.at[idx].add(src)

def _segment_sum(src, seg, n):
    return jax.ops.segment_sum(src, seg, n)
kernel_name = 'mk_audio_tower_d2_tok_audfeat512_r4_2c2135'

def setup_inputs(seed: int=0):
    np.random.seed(seed)
    _w = jnp.asarray

    def _rec_inputs():
        import jax
        import jax.numpy as jnp
        _rk = jax.random.key(seed)
        x = -7.10856e-05 + 0.999911 * jax.random.normal(jax.random.fold_in(_rk, 1), (16, 256, 128), jnp.float32)
        return x
    x = _rec_inputs()

    def _L0_tok_setup():
        import jax, jax.numpy as jnp
        import numpy as np
        EPS = 1e-05

        def conv1d(x, w, b, stride=1, padding=0):
            out = jax.lax.conv_general_dilated(x, w, window_strides=(stride,), padding=[(padding, padding)], dimension_numbers=('NCH', 'OIH', 'NCH'))
            return out + b[None, :, None]

        def layer_norm(x, g, b):
            mu = jnp.mean(x, axis=-1, keepdims=True)
            var = jnp.mean(jnp.square(x - mu), axis=-1, keepdims=True)
            return (x - mu) * jax.lax.rsqrt(var + EPS) * g + b
        key = jax.random.key(seed)
        ks = jax.random.split(key, 16)
        B, T, H = (64, 512, 128)
        Bn = H // 2
        s = 0.02
        return {'x': jax.random.normal(ks[0], (B, T, H), dtype=jnp.float32), 'w_compress': jax.random.normal(ks[1], (Bn, H, 1), dtype=jnp.float32) * s, 'b_compress': jnp.zeros((Bn,), dtype=jnp.float32), 'w_main': jax.random.normal(ks[2], (Bn, Bn, 3), dtype=jnp.float32) * s, 'b_main': jnp.zeros((Bn,), dtype=jnp.float32), 'w_expand': jax.random.normal(ks[3], (H, Bn, 1), dtype=jnp.float32) * s, 'b_expand': jnp.zeros((H,), dtype=jnp.float32), 'g_conv_norm': jnp.ones((H,), dtype=jnp.float32), 'b_conv_norm': jnp.zeros((H,), dtype=jnp.float32), 'w_ff1': jax.random.normal(ks[4], (Bn, H), dtype=jnp.float32) * s, 'b_ff1': jnp.zeros((Bn,), dtype=jnp.float32), 'w_ff2': jax.random.normal(ks[5], (H, Bn), dtype=jnp.float32) * s, 'b_ff2': jnp.zeros((H,), dtype=jnp.float32), 'g_ff_norm': jnp.ones((H,), dtype=jnp.float32), 'b_ff_norm': jnp.zeros((H,), dtype=jnp.float32)}
    _L0_tok_all = _L0_tok_setup()
    _L0_tok_in = {k: v for k, v in _L0_tok_all.items() if k in ('w_compress', 'b_compress', 'w_main', 'b_main', 'w_expand', 'b_expand', 'g_conv_norm', 'b_conv_norm', 'w_ff1', 'b_ff1', 'w_ff2', 'b_ff2', 'g_ff_norm', 'b_ff_norm')}
    del _L0_tok_all

    def _L0_attn_setup():
        import jax, jax.numpy as jnp
        import numpy as np
        B, L, D_MODEL = (8, 512, 128)
        S_EA = 128
        EXPAND = 2
        D_INNER = EXPAND * D_MODEL
        D_STATE = 16
        D_CONV = 4
        DT_RANK = (D_MODEL + 15) // 16

        def _layernorm(x, g, b, eps=1e-05):
            mu = jnp.mean(x, axis=-1, keepdims=True)
            var = jnp.var(x, axis=-1, keepdims=True)
            return (x - mu) * jax.lax.rsqrt(var + eps) * g + b

        def _mamba(x, in_proj_w, conv_w, conv_b, x_proj_w, dt_proj_w, dt_proj_b, A_log, Dp, out_proj_w):
            b, l, _ = x.shape
            xz = jnp.einsum('bld,ed->ble', x, in_proj_w)
            xin, z = jnp.split(xz, 2, axis=-1)
            xc = jnp.transpose(xin, (0, 2, 1))
            xc = jax.lax.conv_general_dilated(xc, conv_w[:, None, :], window_strides=(1,), padding=[(D_CONV - 1, 0)], dimension_numbers=('NCH', 'OIH', 'NCH'), feature_group_count=D_INNER)
            xc = xc + conv_b[None, :, None]
            xact = jax.nn.silu(jnp.transpose(xc, (0, 2, 1)))
            x_dbl = jnp.einsum('bld,ed->ble', xact, x_proj_w)
            dt = x_dbl[..., :DT_RANK]
            Bmat = x_dbl[..., DT_RANK:DT_RANK + D_STATE]
            Cmat = x_dbl[..., DT_RANK + D_STATE:]
            dt = jax.nn.softplus(jnp.einsum('blr,dr->bld', dt, dt_proj_w) + dt_proj_b)
            A = -jnp.exp(A_log)

            def step(h, t):
                dt_t, B_t, C_t, x_t = t
                dA = jnp.exp(dt_t[:, :, None] * A[None])
                dBx = (dt_t * x_t)[:, :, None] * B_t[:, None, :]
                h = h * dA + dBx
                y = jnp.einsum('bds,bs->bd', h, C_t)
                return (h, y)
            h0 = jnp.zeros((b, D_INNER, D_STATE), x.dtype)
            xs = (jnp.swapaxes(dt, 0, 1), jnp.swapaxes(Bmat, 0, 1), jnp.swapaxes(Cmat, 0, 1), jnp.swapaxes(xact, 0, 1))
            _, ys = jax.lax.scan(step, h0, xs)
            y = jnp.swapaxes(ys, 0, 1) + xact * Dp
            y = y * jax.nn.silu(z)
            return jnp.einsum('ble,de->bld', y, out_proj_w)
        key = jax.random.key(seed)
        ks = jax.random.split(key, 12)
        s = 0.02
        inp = {'x': jax.random.normal(ks[0], (B, L, D_MODEL), jnp.float32), 'mk_w': jax.random.normal(ks[1], (S_EA, D_MODEL), jnp.float32) * s, 'mv_w': jax.random.normal(ks[2], (D_MODEL, S_EA), jnp.float32) * s, 'ln_g': jnp.ones((D_MODEL,), jnp.float32), 'ln_b': jnp.zeros((D_MODEL,), jnp.float32), 'in_proj_w': jax.random.normal(ks[3], (2 * D_INNER, D_MODEL), jnp.float32) * s, 'conv_w': jax.random.normal(ks[4], (D_INNER, D_CONV), jnp.float32) * s, 'conv_b': jnp.zeros((D_INNER,), jnp.float32), 'x_proj_w': jax.random.normal(ks[5], (DT_RANK + 2 * D_STATE, D_INNER), jnp.float32) * s, 'dt_proj_w': jax.random.normal(ks[6], (D_INNER, DT_RANK), jnp.float32) * s, 'dt_proj_b': jax.random.normal(ks[7], (D_INNER,), jnp.float32) * s, 'A_log': jnp.log(jnp.tile(jnp.arange(1, D_STATE + 1, dtype=jnp.float32), (D_INNER, 1))), 'D': jnp.ones((D_INNER,), jnp.float32), 'out_proj_w': jax.random.normal(ks[8], (D_MODEL, D_INNER), jnp.float32) * s}
        return inp
    _L0_attn_all = _L0_attn_setup()
    _L0_attn_in = {k: v for k, v in _L0_attn_all.items() if k in ('mk_w', 'mv_w', 'ln_g', 'ln_b', 'in_proj_w', 'conv_w', 'conv_b', 'x_proj_w', 'dt_proj_w', 'dt_proj_b', 'A_log', 'D', 'out_proj_w')}
    del _L0_attn_all

    def _L0_ffn_setup():
        import jax, jax.numpy as jnp
        import numpy as np
        TOP_K = 2

        def quick_gelu(x):
            return x * jax.nn.sigmoid(1.702 * x)
        key = jax.random.key(seed)
        ks = jax.random.split(key, 6)
        B, S, H, I, E = (8, 1024, 128, 256, 8)
        s_h = 1.0 / np.sqrt(H).astype(np.float32)
        s_i = 1.0 / np.sqrt(I).astype(np.float32)
        return {'hidden_states': jax.random.normal(ks[0], (B, S, H), jnp.float32), 'router_w': jax.random.normal(ks[1], (H, E), jnp.float32) * s_h, 'router_b': jnp.zeros((E,), jnp.float32), 'gate_up_proj': jax.random.normal(ks[2], (E, H, 2 * I), jnp.float32) * s_h, 'gate_up_proj_bias': jnp.zeros((E, 2 * I), jnp.float32), 'down_proj': jax.random.normal(ks[3], (E, I, H), jnp.float32) * s_i, 'down_proj_bias': jnp.zeros((E, H), jnp.float32)}
    _L0_ffn_all = _L0_ffn_setup()
    _L0_ffn_in = {k: v for k, v in _L0_ffn_all.items() if k in ('router_w', 'router_b', 'gate_up_proj', 'gate_up_proj_bias', 'down_proj', 'down_proj_bias')}
    del _L0_ffn_all

    def _L1_attn_setup():
        import jax, jax.numpy as jnp
        import numpy as np
        B, S, IN, HID, H, D, FF = (8, 512, 128, 128, 8, 64, 512)
        EPS = 1e-05

        def layer_norm(x, g, b):
            m = jnp.mean(x, axis=-1, keepdims=True)
            v = jnp.mean(jnp.square(x - m), axis=-1, keepdims=True)
            return (x - m) * jax.lax.rsqrt(v + EPS) * g + b

        def delta_rule(q, k, v, beta):

            def step(W, inp):
                qt, kt, vt, bt = inp
                wk = jnp.einsum('bhde,bhe->bhd', W, kt)
                v_new = bt * (vt - wk)
                W = W + jnp.einsum('bhd,bhe->bhde', v_new, kt)
                out = jnp.einsum('bhde,bhe->bhd', W, qt)
                return (W, out)
            bsz = q.shape[1]
            W0 = jnp.zeros((bsz, H, D, D), dtype=q.dtype)
            _, outs = jax.lax.scan(step, W0, (q, k, v, beta))
            return outs

        def fast_ff(x, ln_g, ln_b, slow_w, out_w):
            slen, bsz, _ = x.shape
            h = layer_norm(x, ln_g, ln_b)
            qkvb = jnp.einsum('sbi,oi->sbo', h, slow_w).reshape(slen, bsz, H, 3 * D + 1)
            q, k, v, beta = jnp.split(qkvb, [D, 2 * D, 3 * D], axis=-1)
            q = jax.nn.softmax(q, axis=-1)
            k = jax.nn.softmax(k, axis=-1)
            beta = jax.nn.sigmoid(beta)
            attn = delta_rule(q, k, v, beta)
            o = jnp.einsum('sbd,od->sbo', attn.reshape(slen, bsz, H * D), out_w)
            return x + o

        def ffn(x, ln_g, ln_b, w1, b1, w2, b2):
            h = layer_norm(x, ln_g, ln_b)
            h = jax.nn.relu(jnp.einsum('sbi,fi->sbf', h, w1) + b1)
            return x + jnp.einsum('sbf,of->sbo', h, w2) + b2
        key = jax.random.key(seed)
        ks = jax.random.split(key, 8)
        s = 0.02
        return {'x': jax.random.normal(ks[0], (B, S, IN), jnp.float32), 'ip_w': s * jax.random.normal(ks[1], (HID, IN), jnp.float32), 'ip_b': jnp.zeros((HID,), jnp.float32), 'fw_ln_g': jnp.ones((2, HID), jnp.float32), 'fw_ln_b': jnp.zeros((2, HID), jnp.float32), 'fw_slow_w': s * jax.random.normal(ks[2], (2, H * (3 * D + 1), HID), jnp.float32), 'fw_out_w': s * jax.random.normal(ks[3], (2, HID, H * D), jnp.float32), 'ff_ln_g': jnp.ones((HID,), jnp.float32), 'ff_ln_b': jnp.zeros((HID,), jnp.float32), 'ff_w1': s * jax.random.normal(ks[4], (FF, HID), jnp.float32), 'ff_b1': jnp.zeros((FF,), jnp.float32), 'ff_w2': s * jax.random.normal(ks[5], (HID, FF), jnp.float32), 'ff_b2': jnp.zeros((HID,), jnp.float32)}
    _L1_attn_all = _L1_attn_setup()
    _L1_attn_in = {k: v for k, v in _L1_attn_all.items() if k in ('ip_w', 'ip_b', 'fw_ln_g', 'fw_ln_b', 'fw_slow_w', 'fw_out_w', 'ff_ln_g', 'ff_ln_b', 'ff_w1', 'ff_b1', 'ff_w2', 'ff_b2')}
    del _L1_attn_all

    def _L1_ffn_setup():
        import jax, jax.numpy as jnp
        import numpy as np
        B, S, H, E, K, DF, SH = (8, 1024, 128, 8, 2, 128, 128)
        key = jax.random.key(seed)
        ks = jax.random.split(key, 10)
        n = lambda i, shape, sc: jax.random.normal(ks[i], shape, jnp.float32) * sc
        return {'hidden_states': n(0, (B, S, H), 1.0), 'gate_w': n(1, (E, H), 0.05), 'w1': n(2, (E, H, DF), 0.05), 'b1': n(3, (E, DF), 0.01), 'w2': n(4, (E, DF, H), 0.05), 'b2': n(5, (E, H), 0.01), 'sw1': n(6, (H, SH), 0.05), 'sb1': n(7, (SH,), 0.01), 'sw2': n(8, (SH, H), 0.05), 'sb2': n(9, (H,), 0.01)}
    _L1_ffn_all = _L1_ffn_setup()
    _L1_ffn_in = {k: v for k, v in _L1_ffn_all.items() if k in ('gate_w', 'w1', 'b1', 'w2', 'b2', 'sw1', 'sb1', 'sw2', 'sb2')}
    del _L1_ffn_all
    return {'x': x, 'L0_tok_w_compress': _L0_tok_in['w_compress'], 'L0_tok_b_compress': _L0_tok_in['b_compress'], 'L0_tok_w_main': _L0_tok_in['w_main'], 'L0_tok_b_main': _L0_tok_in['b_main'], 'L0_tok_w_expand': _L0_tok_in['w_expand'], 'L0_tok_b_expand': _L0_tok_in['b_expand'], 'L0_tok_g_conv_norm': _L0_tok_in['g_conv_norm'], 'L0_tok_b_conv_norm': _L0_tok_in['b_conv_norm'], 'L0_tok_w_ff1': _L0_tok_in['w_ff1'], 'L0_tok_b_ff1': _L0_tok_in['b_ff1'], 'L0_tok_w_ff2': _L0_tok_in['w_ff2'], 'L0_tok_b_ff2': _L0_tok_in['b_ff2'], 'L0_tok_g_ff_norm': _L0_tok_in['g_ff_norm'], 'L0_tok_b_ff_norm': _L0_tok_in['b_ff_norm'], 'L0_attn_mk_w': _L0_attn_in['mk_w'], 'L0_attn_mv_w': _L0_attn_in['mv_w'], 'L0_attn_ln_g': _L0_attn_in['ln_g'], 'L0_attn_ln_b': _L0_attn_in['ln_b'], 'L0_attn_in_proj_w': _L0_attn_in['in_proj_w'], 'L0_attn_conv_w': _L0_attn_in['conv_w'], 'L0_attn_conv_b': _L0_attn_in['conv_b'], 'L0_attn_x_proj_w': _L0_attn_in['x_proj_w'], 'L0_attn_dt_proj_w': _L0_attn_in['dt_proj_w'], 'L0_attn_dt_proj_b': _L0_attn_in['dt_proj_b'], 'L0_attn_A_log': _L0_attn_in['A_log'], 'L0_attn_D': _L0_attn_in['D'], 'L0_attn_out_proj_w': _L0_attn_in['out_proj_w'], 'L0_ffn_router_w': _L0_ffn_in['router_w'], 'L0_ffn_router_b': _L0_ffn_in['router_b'], 'L0_ffn_gate_up_proj': _L0_ffn_in['gate_up_proj'], 'L0_ffn_gate_up_proj_bias': _L0_ffn_in['gate_up_proj_bias'], 'L0_ffn_down_proj': _L0_ffn_in['down_proj'], 'L0_ffn_down_proj_bias': _L0_ffn_in['down_proj_bias'], 'L1_attn_ip_w': _L1_attn_in['ip_w'], 'L1_attn_ip_b': _L1_attn_in['ip_b'], 'L1_attn_fw_ln_g': _L1_attn_in['fw_ln_g'], 'L1_attn_fw_ln_b': _L1_attn_in['fw_ln_b'], 'L1_attn_fw_slow_w': _L1_attn_in['fw_slow_w'], 'L1_attn_fw_out_w': _L1_attn_in['fw_out_w'], 'L1_attn_ff_ln_g': _L1_attn_in['ff_ln_g'], 'L1_attn_ff_ln_b': _L1_attn_in['ff_ln_b'], 'L1_attn_ff_w1': _L1_attn_in['ff_w1'], 'L1_attn_ff_b1': _L1_attn_in['ff_b1'], 'L1_attn_ff_w2': _L1_attn_in['ff_w2'], 'L1_attn_ff_b2': _L1_attn_in['ff_b2'], 'L1_ffn_gate_w': _L1_ffn_in['gate_w'], 'L1_ffn_w1': _L1_ffn_in['w1'], 'L1_ffn_b1': _L1_ffn_in['b1'], 'L1_ffn_w2': _L1_ffn_in['w2'], 'L1_ffn_b2': _L1_ffn_in['b2'], 'L1_ffn_sw1': _L1_ffn_in['sw1'], 'L1_ffn_sb1': _L1_ffn_in['sb1'], 'L1_ffn_sw2': _L1_ffn_in['sw2'], 'L1_ffn_sb2': _L1_ffn_in['sb2']}

def reference(x, L0_tok_w_compress, L0_tok_b_compress, L0_tok_w_main, L0_tok_b_main, L0_tok_w_expand, L0_tok_b_expand, L0_tok_g_conv_norm, L0_tok_b_conv_norm, L0_tok_w_ff1, L0_tok_b_ff1, L0_tok_w_ff2, L0_tok_b_ff2, L0_tok_g_ff_norm, L0_tok_b_ff_norm, L0_attn_mk_w, L0_attn_mv_w, L0_attn_ln_g, L0_attn_ln_b, L0_attn_in_proj_w, L0_attn_conv_w, L0_attn_conv_b, L0_attn_x_proj_w, L0_attn_dt_proj_w, L0_attn_dt_proj_b, L0_attn_A_log, L0_attn_D, L0_attn_out_proj_w, L0_ffn_router_w, L0_ffn_router_b, L0_ffn_gate_up_proj, L0_ffn_gate_up_proj_bias, L0_ffn_down_proj, L0_ffn_down_proj_bias, L1_attn_ip_w, L1_attn_ip_b, L1_attn_fw_ln_g, L1_attn_fw_ln_b, L1_attn_fw_slow_w, L1_attn_fw_out_w, L1_attn_ff_ln_g, L1_attn_ff_ln_b, L1_attn_ff_w1, L1_attn_ff_b1, L1_attn_ff_w2, L1_attn_ff_b2, L1_ffn_gate_w, L1_ffn_w1, L1_ffn_b1, L1_ffn_w2, L1_ffn_b2, L1_ffn_sw1, L1_ffn_sb1, L1_ffn_sw2, L1_ffn_sb2):
    import jax
    import jax.numpy as jnp

    def _L0_tok_ref(x, w_compress, b_compress, w_main, b_main, w_expand, b_expand, g_conv_norm, b_conv_norm, w_ff1, b_ff1, w_ff2, b_ff2, g_ff_norm, b_ff_norm):
        import jax, jax.numpy as jnp
        import numpy as np
        EPS = 1e-05

        def conv1d(x, w, b, stride=1, padding=0):
            out = jax.lax.conv_general_dilated(x, w, window_strides=(stride,), padding=[(padding, padding)], dimension_numbers=('NCH', 'OIH', 'NCH'))
            return out + b[None, :, None]

        def layer_norm(x, g, b):
            mu = jnp.mean(x, axis=-1, keepdims=True)
            var = jnp.mean(jnp.square(x - mu), axis=-1, keepdims=True)
            return (x - mu) * jax.lax.rsqrt(var + EPS) * g + b
        xt = jnp.transpose(x, (0, 2, 1))
        identity = xt
        h = jax.nn.silu(conv1d(xt, w_compress, b_compress))
        h = jax.nn.silu(conv1d(h, w_main, b_main, stride=1, padding=1))
        h = conv1d(h, w_expand, b_expand)
        h = jnp.transpose(h, (0, 2, 1))
        identity = jnp.transpose(identity, (0, 2, 1))
        y = layer_norm(h + identity, g_conv_norm, b_conv_norm)
        ff = jnp.einsum('bth,oh->bto', y, w_ff1) + b_ff1
        ff = jax.nn.gelu(ff, approximate=False)
        ff = jnp.einsum('bto,ho->bth', ff, w_ff2) + b_ff2
        y = layer_norm(ff + y, g_ff_norm, b_ff_norm)
        yt = jnp.transpose(y, (0, 2, 1))
        pooled = jax.lax.reduce_window(yt, -jnp.inf, jax.lax.max, (1, 1, 3), (1, 1, 1), 'VALID')
        return jnp.transpose(pooled, (0, 2, 1))

    def _L0_attn_ref(x, mk_w, mv_w, ln_g, ln_b, in_proj_w, conv_w, conv_b, x_proj_w, dt_proj_w, dt_proj_b, A_log, D, out_proj_w):
        import jax, jax.numpy as jnp
        import numpy as np
        B, L, D_MODEL = (8, 512, 128)
        S_EA = 128
        EXPAND = 2
        D_INNER = EXPAND * D_MODEL
        D_STATE = 16
        D_CONV = 4
        DT_RANK = (D_MODEL + 15) // 16

        def _layernorm(x, g, b, eps=1e-05):
            mu = jnp.mean(x, axis=-1, keepdims=True)
            var = jnp.var(x, axis=-1, keepdims=True)
            return (x - mu) * jax.lax.rsqrt(var + eps) * g + b

        def _mamba(x, in_proj_w, conv_w, conv_b, x_proj_w, dt_proj_w, dt_proj_b, A_log, Dp, out_proj_w):
            b, l, _ = x.shape
            xz = jnp.einsum('bld,ed->ble', x, in_proj_w)
            xin, z = jnp.split(xz, 2, axis=-1)
            xc = jnp.transpose(xin, (0, 2, 1))
            xc = jax.lax.conv_general_dilated(xc, conv_w[:, None, :], window_strides=(1,), padding=[(D_CONV - 1, 0)], dimension_numbers=('NCH', 'OIH', 'NCH'), feature_group_count=D_INNER)
            xc = xc + conv_b[None, :, None]
            xact = jax.nn.silu(jnp.transpose(xc, (0, 2, 1)))
            x_dbl = jnp.einsum('bld,ed->ble', xact, x_proj_w)
            dt = x_dbl[..., :DT_RANK]
            Bmat = x_dbl[..., DT_RANK:DT_RANK + D_STATE]
            Cmat = x_dbl[..., DT_RANK + D_STATE:]
            dt = jax.nn.softplus(jnp.einsum('blr,dr->bld', dt, dt_proj_w) + dt_proj_b)
            A = -jnp.exp(A_log)

            def step(h, t):
                dt_t, B_t, C_t, x_t = t
                dA = jnp.exp(dt_t[:, :, None] * A[None])
                dBx = (dt_t * x_t)[:, :, None] * B_t[:, None, :]
                h = h * dA + dBx
                y = jnp.einsum('bds,bs->bd', h, C_t)
                return (h, y)
            h0 = jnp.zeros((b, D_INNER, D_STATE), x.dtype)
            xs = (jnp.swapaxes(dt, 0, 1), jnp.swapaxes(Bmat, 0, 1), jnp.swapaxes(Cmat, 0, 1), jnp.swapaxes(xact, 0, 1))
            _, ys = jax.lax.scan(step, h0, xs)
            y = jnp.swapaxes(ys, 0, 1) + xact * Dp
            y = y * jax.nn.silu(z)
            return jnp.einsum('ble,de->bld', y, out_proj_w)
        attn = jax.nn.softmax(jnp.einsum('bld,sd->bls', x, mk_w), axis=-1)
        x_out = jnp.einsum('bls,ds->bld', attn, mv_w)
        x_out = _layernorm(x_out, ln_g, ln_b)
        x_out = jax.nn.gelu(x_out, approximate=False) + x
        return _mamba(x_out, in_proj_w, conv_w, conv_b, x_proj_w, dt_proj_w, dt_proj_b, A_log, D, out_proj_w)

    def _L0_ffn_ref(hidden_states, router_w, router_b, gate_up_proj, gate_up_proj_bias, down_proj, down_proj_bias):
        import jax, jax.numpy as jnp
        import numpy as np
        TOP_K = 2

        def quick_gelu(x):
            return x * jax.nn.sigmoid(1.702 * x)
        B, S, H = hidden_states.shape
        E = router_b.shape[0]
        x = hidden_states.reshape(-1, H)
        T = x.shape[0]
        logits = x @ router_w + router_b
        top_w, sel = jax.lax.top_k(logits, TOP_K)
        top_w = jax.nn.softmax(top_w, axis=-1)
        tok_w = jnp.zeros((T, E), x.dtype).at[jnp.arange(T)[:, None], sel].add(top_w)

        def body(acc, params):
            Wgu, bgu, Wd, bd, w_e = params
            gu = x @ Wgu + bgu
            gate, up = jnp.split(gu, 2, axis=-1)
            act = (up + 1.0) * quick_gelu(gate)
            out = act @ Wd + bd
            return (acc + out * w_e[:, None], None)
        acc0 = jnp.zeros((T, H), x.dtype)
        acc, _ = jax.lax.scan(body, acc0, (gate_up_proj, gate_up_proj_bias, down_proj, down_proj_bias, tok_w.T))
        return acc.reshape(B, S, H)

    def _L1_attn_ref(x, ip_w, ip_b, fw_ln_g, fw_ln_b, fw_slow_w, fw_out_w, ff_ln_g, ff_ln_b, ff_w1, ff_b1, ff_w2, ff_b2):
        import jax, jax.numpy as jnp
        import numpy as np
        B, S, IN, HID, H, D, FF = (8, 512, 128, 128, 8, 64, 512)
        EPS = 1e-05

        def layer_norm(x, g, b):
            m = jnp.mean(x, axis=-1, keepdims=True)
            v = jnp.mean(jnp.square(x - m), axis=-1, keepdims=True)
            return (x - m) * jax.lax.rsqrt(v + EPS) * g + b

        def delta_rule(q, k, v, beta):

            def step(W, inp):
                qt, kt, vt, bt = inp
                wk = jnp.einsum('bhde,bhe->bhd', W, kt)
                v_new = bt * (vt - wk)
                W = W + jnp.einsum('bhd,bhe->bhde', v_new, kt)
                out = jnp.einsum('bhde,bhe->bhd', W, qt)
                return (W, out)
            bsz = q.shape[1]
            W0 = jnp.zeros((bsz, H, D, D), dtype=q.dtype)
            _, outs = jax.lax.scan(step, W0, (q, k, v, beta))
            return outs

        def fast_ff(x, ln_g, ln_b, slow_w, out_w):
            slen, bsz, _ = x.shape
            h = layer_norm(x, ln_g, ln_b)
            qkvb = jnp.einsum('sbi,oi->sbo', h, slow_w).reshape(slen, bsz, H, 3 * D + 1)
            q, k, v, beta = jnp.split(qkvb, [D, 2 * D, 3 * D], axis=-1)
            q = jax.nn.softmax(q, axis=-1)
            k = jax.nn.softmax(k, axis=-1)
            beta = jax.nn.sigmoid(beta)
            attn = delta_rule(q, k, v, beta)
            o = jnp.einsum('sbd,od->sbo', attn.reshape(slen, bsz, H * D), out_w)
            return x + o

        def ffn(x, ln_g, ln_b, w1, b1, w2, b2):
            h = layer_norm(x, ln_g, ln_b)
            h = jax.nn.relu(jnp.einsum('sbi,fi->sbf', h, w1) + b1)
            return x + jnp.einsum('sbf,of->sbo', h, w2) + b2
        out = jnp.einsum('bsi,hi->bsh', x, ip_w) + ip_b
        out = out.transpose(1, 0, 2)
        out = fast_ff(out, fw_ln_g[0], fw_ln_b[0], fw_slow_w[0], fw_out_w[0])
        out = ffn(out, ff_ln_g, ff_ln_b, ff_w1, ff_b1, ff_w2, ff_b2)
        out = fast_ff(out, fw_ln_g[1], fw_ln_b[1], fw_slow_w[1], fw_out_w[1])
        return out.transpose(1, 0, 2)

    def _L1_ffn_ref(hidden_states, gate_w, w1, b1, w2, b2, sw1, sb1, sw2, sb2):
        import jax, jax.numpy as jnp
        import numpy as np
        B, S, H, E, K, DF, SH = (8, 1024, 128, 8, 2, 128, 128)
        x = hidden_states
        xf = x.reshape(-1, x.shape[-1])
        T = xf.shape[0]
        scores = jax.nn.softmax(xf @ gate_w.T, axis=-1)
        topk_w, topk_i = jax.lax.top_k(scores, K)
        topk_w = topk_w / (topk_w.sum(-1, keepdims=True) + 1e-20)
        combine = jnp.zeros((T, E), xf.dtype).at[jnp.arange(T)[:, None], topk_i].add(topk_w)
        h1 = jax.nn.relu(jnp.einsum('th,ehf->tef', xf, w1) + b1)
        eo = jnp.einsum('tef,efh->teh', h1, w2) + b2
        y = jnp.einsum('te,teh->th', combine, eo)
        shared = jax.nn.relu(xf @ sw1 + sb1) @ sw2 + sb2
        return (y + shared).reshape(x.shape)
    h = _L0_tok_ref(x, L0_tok_w_compress, L0_tok_b_compress, L0_tok_w_main, L0_tok_b_main, L0_tok_w_expand, L0_tok_b_expand, L0_tok_g_conv_norm, L0_tok_b_conv_norm, L0_tok_w_ff1, L0_tok_b_ff1, L0_tok_w_ff2, L0_tok_b_ff2, L0_tok_g_ff_norm, L0_tok_b_ff_norm)
    h = h + _L0_attn_ref(_layernorm(h, axis=-1), L0_attn_mk_w, L0_attn_mv_w, L0_attn_ln_g, L0_attn_ln_b, L0_attn_in_proj_w, L0_attn_conv_w, L0_attn_conv_b, L0_attn_x_proj_w, L0_attn_dt_proj_w, L0_attn_dt_proj_b, L0_attn_A_log, L0_attn_D, L0_attn_out_proj_w)
    h = h + _L0_ffn_ref(_layernorm(h, axis=-1), L0_ffn_router_w, L0_ffn_router_b, L0_ffn_gate_up_proj, L0_ffn_gate_up_proj_bias, L0_ffn_down_proj, L0_ffn_down_proj_bias)
    h = h + _L1_attn_ref(_layernorm(h, axis=-1), L1_attn_ip_w, L1_attn_ip_b, L1_attn_fw_ln_g, L1_attn_fw_ln_b, L1_attn_fw_slow_w, L1_attn_fw_out_w, L1_attn_ff_ln_g, L1_attn_ff_ln_b, L1_attn_ff_w1, L1_attn_ff_b1, L1_attn_ff_w2, L1_attn_ff_b2)
    h = h + _L1_ffn_ref(_layernorm(h, axis=-1), L1_ffn_gate_w, L1_ffn_w1, L1_ffn_b1, L1_ffn_w2, L1_ffn_b2, L1_ffn_sw1, L1_ffn_sb1, L1_ffn_sw2, L1_ffn_sb2)
    return h

_drawn_inputs = setup_inputs


def setup_inputs(seed=0):
    import zlib

    import numpy as np

    out = dict(_drawn_inputs(seed))
    spreads = {'L0_tok_b_compress': (0.0, 0.456),
     'L0_tok_b_main': (0.0, 0.1),
     'L0_tok_b_expand': (0.0, 0.1),
     'L0_tok_g_conv_norm': (1.0, 0.2),
     'L0_tok_b_conv_norm': (0.0, 0.1),
     'L0_tok_b_ff1': (0.0, 0.1),
     'L0_tok_b_ff2': (0.0, 0.1),
     'L0_tok_g_ff_norm': (1.0, 0.2),
     'L0_tok_b_ff_norm': (0.0, 0.1),
     'L0_attn_ln_g': (1.0, 0.6),
     'L0_attn_ln_b': (0.0, 0.8),
     'L0_attn_conv_b': (0.0, 0.39),
     'L0_attn_D': (1.0, 0.6),
     'L0_ffn_router_b': (0.0, 0.1),
     'L0_ffn_gate_up_proj_bias': (0.0, 0.1),
     'L0_ffn_down_proj_bias': (0.0, 0.1),
     'L1_attn_ip_b': (0.0, 0.1),
     'L1_attn_fw_ln_g': (1.0, 0.6),
     'L1_attn_fw_ln_b': (0.0, 0.75),
     'L1_attn_ff_ln_g': (1.0, 0.6),
     'L1_attn_ff_ln_b': (0.0, 0.712),
     'L1_attn_ff_b1': (0.0, 0.289),
     'L1_attn_ff_b2': (0.0, 0.1)}
    factors = {'L0_tok_w_compress': 3.869,
     'L0_attn_mk_w': 8.0,
     'L0_attn_mv_w': 6.442,
     'L0_attn_in_proj_w': 3.655,
     'L0_attn_conv_w': 8.0,
     'L0_attn_x_proj_w': 8.0,
     'L0_attn_dt_proj_w': 8.0,
     'L0_attn_dt_proj_b': 8.0,
     'L0_attn_A_log': 8.0,
     'L0_attn_out_proj_w': 3.484,
     'L1_ffn_b1': 34.472,
     'L1_ffn_b2': 8.0,
     'L1_ffn_sb1': 23.758,
     'L1_ffn_sb2': 7.106}
    for name, (base, spread) in spreads.items():
        noise = np.random.default_rng([zlib.crc32(name.encode()), seed]).standard_normal(out[name].shape)
        drawn = base * np.exp(spread * noise) if base else spread * noise
        out[name] = jnp.asarray(drawn.astype(out[name].dtype))
    for name, factor in factors.items():
        out[name] = (out[name] * factor).astype(out[name].dtype)
    return out
```

```python
from contextlib import ExitStack

import numpy as np

import concourse.bass as bass
from concourse import mybir

F32 = mybir.dt.float32
U32 = mybir.dt.uint32
BF16 = mybir.dt.bfloat16
ALU = mybir.AluOpType
ACT = mybir.ActivationFunctionType
AX = mybir.AxisListType.X

B, S, H = 16, 256, 128
L = S - 2
T = B * L
W2 = 2 * L
NT = B // 2
C = L // 2
BN = H // 2
E = 8
I0 = 256
DI = 2 * H
DS = 16
DR = 8
NH, D = 8, 64
FF = 512
EPS = 1e-5
LANES = 2
PARTS = (0, 64, 96)


class Kit:

    def __init__(self, nc, ins, out):
        self.nc, self.ins, self.out = nc, ins, out
        self.norms = 0

    def semaphore(self, phase, name):
        if self.phase is not phase:
            self.phase, mine = phase, []
            self.phase_semaphores = mine
            phase.callback(self.end_phase, mine)
        self.phase_semaphores.append(self.nc.alloc_semaphore(name))
        return self.phase_semaphores[-1]

    def end_phase(self, semaphores):
        self.nc.clear_and_free_semaphores(semaphores)
        self.nc.all_engine_barrier()

    phase = None


LN_STAGES = ("centred", "squares", "var", "log", "scale", "scaled")
EXP_AND_LN = 6


def load_exp_ln(act):
    act.add_instruction(mybir.InstLoadActFuncSet(
        name=act.bass.get_next_instruction_name(), engine=mybir.EngineType.Activation,
        act_func_set_id=EXP_AND_LN))


def work_out(engine, *counts):
    for count in counts:
        if not isinstance(count, int):
            engine.to_reg(count)


def cols(t, width):
    return bass.ds(t * width, width)



def token_mixer(k):
    nc = k.nc
    N = 2 * S
    with ExitStack() as ctx:
        def sb(name, shape):
            return ctx.enter_context(nc.sbuf_tensor(name, shape, F32))

        def sem(name):
            return k.semaphore(ctx, name)

        w_compress, w_expand = sb("w_compress", [H, BN]), sb("w_expand", [BN, H])
        w_main = sb("w_main", [BN, 3, H])
        w_up, w_down = sb("tok_up", [H, BN]), sb("tok_down", [BN, H])
        vec = sb("tok_vec", [H, 9])
        b_compress, b_main, b_up = vec[0:BN, 0:1], vec[0:BN, 1:2], vec[0:BN, 2:3]
        b_expand, b_down = vec[:, 3:4], vec[:, 4:5]
        g1, b1, g2, b2 = (vec[:, n:n + 1] for n in range(5, 9))
        x = sb("x_in", [H, B * S])
        lanes = range(LANES)
        squeezed = [sb(f"squeezed{u}", [BN, 2, S + 2]) for u in lanes]
        mixed = [sb(f"mixed{u}", [BN, N]) for u in lanes]
        summed = [sb(f"summed{u}", [H, N]) for u in lanes]
        squares = [sb(f"squares{u}", [H, N]) for u in lanes]
        scale = [sb(f"scale{u}", [H, N]) for u in lanes]
        normed = [sb(f"normed{u}", [H, N]) for u in lanes]
        second = [sb(f"second{u}", [H, N]) for u in lanes]
        pairmax = [sb(f"pairmax{u}", [H, 2, S - 1]) for u in lanes]
        acc = [[ctx.enter_context(nc.psum_tensor(f"tok_p{u}_{n}", [128, 512], F32)) for n in range(4)]
               for u in lanes]
        loaded, x_loaded, pad_zero = sem("tok_loaded"), sem("x_loaded"), sem("pad_zero")
        names = ["compressed", "squeezed", "convolved", "mixed", "expanded", "summed",
                 "norm1", "up", "gelu", "down", "summed2", "norm2", "affine2", "pairmax", "pooled",
                 "block"]
        s = {n: sem(f"tok_{n}") for n in names}
        ln = [{n: sem(f"tok_ln{j}_{n}") for n in LN_STAGES}
              for j in range(3)]

        block = ctx.enter_context(nc.Block())

        @block.sync
        def _(sp):
            w = k.ins
            for dst, src in ((w_compress[:, :], w["w_compress"]), (w_main[:, :, :], w["w_main"]),
                             (w_expand[:, :], w["w_expand"]), (w_up[:, :], w["tok_up"]),
                             (w_down[:, :], w["tok_down"]), (vec[:, :], w["tok_vec"])):
                sp.dma_start(dst, src).then_inc(loaded, 16)
            for n in range(4):
                sp.dma_start(x[:, n * B * S // 4:(n + 1) * B * S // 4],
                             w["x"][:, n * B * S // 4:(n + 1) * B * S // 4]).then_inc(x_loaded, 16)

        @block.tensor
        def _(pe):
            pe.wait_ge(loaded, 16 * 6)
            pe.wait_ge(x_loaded, 16 * 4)
            pe.wait_ge(pad_zero, 2 * LANES)
            with pe.Fori(0, NT // LANES) as step:
                i = step * LANES
                pe.wait_ge(ln[2]["scaled"], i)
                for u in lanes:
                    pe.matmul(acc[u][0][0:BN, :], w_compress[:, :], x[:, cols(i + u, N)],
                              start=True, stop=True).then_inc(s["compressed"], 1)
                for u in lanes:
                    pe.wait_ge(s["squeezed"], i + u + 1)
                    for tap in range(3):
                        mm = pe.matmul(acc[u][1][:, :], w_main[:, tap, :],
                                       squeezed[u][:, :, tap:tap + S], start=tap == 0, stop=tap == 2)
                    mm.then_inc(s["convolved"], 1)
                for u in lanes:
                    pe.wait_ge(s["mixed"], i + u + 1)
                    pe.matmul(acc[u][2][:, :], w_expand[:, :], mixed[u][:, :],
                              start=True, stop=True).then_inc(s["expanded"], 1)
                norm_pe(pe, k, ln[0], i, summed, s["summed"], squares, acc, 3, 0)
                for u in lanes:
                    pe.wait_ge(s["norm1"], i + u + 1)
                    pe.matmul(acc[u][1][0:BN, :], w_up[:, :], normed[u][:, :],
                              start=True, stop=True).then_inc(s["up"], 1)
                for u in lanes:
                    pe.wait_ge(s["gelu"], i + u + 1)
                    pe.matmul(acc[u][2][:, :], w_down[:, :], mixed[u][:, :],
                              start=True, stop=True).then_inc(s["down"], 1)
                norm_pe(pe, k, ln[1], i, second, s["summed2"], squares, acc, 3, 0)
                norm_pe(pe, k, ln[2], i, [k.h[:, cols(i + u, W2)] for u in lanes], s["pooled"],
                        squares, acc, 1, 2, W2)

        @block.scalar
        def _(act):
            act.wait_ge(loaded, 16 * 6)
            with act.Fori(0, NT // LANES) as step:
                i = step * LANES
                for u in lanes:
                    act.wait_ge(s["compressed"], i + u + 1)
                    act.activation(squeezed[u][:, :, 1:S + 1],
                                   acc[u][0][0:BN, :].rearrange("p (b s) -> p b s", b=2),
                                   ACT.Silu, bias=b_compress).then_inc(s["squeezed"], 1)
                for u in lanes:
                    act.wait_ge(s["convolved"], i + u + 1)
                    act.activation(mixed[u][:, :], acc[u][1][0:BN, :], ACT.Silu,
                                   bias=b_main).then_inc(s["mixed"], 1)
                norm_act(act, k, ln[0], i, squares, scale, acc, 3, 0)
                for u in lanes:
                    act.wait_ge(s["up"], i + u + 1)
                    act.activation(mixed[u][:, :], acc[u][1][0:BN, :], ACT.Gelu,
                                   bias=b_up).then_inc(s["gelu"], 1)
                norm_act(act, k, ln[1], i, squares, scale, acc, 3, 0)
                norm_act(act, k, ln[2], i, squares, scale, acc, 1, 2, W2)

        @block.vector
        def _(dve):
            for u in lanes:
                dve.memset(squeezed[u][:, :, 0:1], 0.0).then_inc(pad_zero, 1)
                dve.memset(squeezed[u][:, :, S + 1:S + 2], 0.0).then_inc(pad_zero, 1)
            dve.wait_ge(loaded, 16 * 6)
            dve.wait_ge(x_loaded, 16 * 4)
            with dve.Fori(0, NT // LANES) as step:
                i = step * LANES
                for u in lanes:
                    dve.wait_ge(s["expanded"], i + u + 1)
                    dve.scalar_tensor_tensor(summed[u][:, :], acc[u][2][:, :], b_expand,
                                             x[:, cols(i + u, N)], ALU.add, ALU.add)\
                        .then_inc(s["summed"], 1)
                norm_dve(dve, ln[0], i, scale, acc, 3, normed)
                for u in lanes:
                    dve.wait_ge(ln[0]["scaled"], i + u + 1)
                    dve.tensor_scalar(normed[u][:, :], normed[u][:, :], g1, b1, ALU.mult, ALU.add)\
                        .then_inc(s["norm1"], 1)
                for u in lanes:
                    dve.wait_ge(s["down"], i + u + 1)
                    dve.wait_ge(s["norm1"], i + u + 1)
                    dve.scalar_tensor_tensor(second[u][:, :], acc[u][2][:, :], b_down, normed[u][:, :],
                                             ALU.add, ALU.add).then_inc(s["summed2"], 1)
                norm_dve(dve, ln[1], i, scale, acc, 3, second)
                for u in lanes:
                    dve.wait_ge(ln[1]["scaled"], i + u + 1)
                    dve.tensor_scalar(second[u][:, :], second[u][:, :], g2, b2, ALU.mult, ALU.add)\
                        .then_inc(s["affine2"], 1)
                for u in lanes:
                    y = second[u][:, :].rearrange("p (b s) -> p b s", b=2)
                    dve.wait_ge(s["affine2"], i + u + 1)
                    dve.tensor_tensor(pairmax[u][:, :, :], y[:, :, 0:S - 1], y[:, :, 1:S], ALU.max)\
                        .then_inc(s["pairmax"], 1)
                for u in lanes:
                    dve.wait_ge(s["pairmax"], i + u + 1)
                    dve.tensor_tensor(k.h[:, cols(i + u, W2)].rearrange("p (b s) -> p b s", b=2),
                                      pairmax[u][:, :, 0:L], pairmax[u][:, :, 1:L + 1], ALU.max)\
                        .then_inc(s["pooled"], 1)
                norm_dve(dve, ln[2], i, scale, acc, 1, [k.xn[:, cols(i + u, W2)] for u in lanes], W2)



def norm_pe(pe, k, ln, i, source, ready, squares, acc, at, var, n=512):
    for u in range(LANES):
        if ready is not None:
            pe.wait_ge(ready, i + u + 1)
        src = source[u] if n != 512 else source[u][:, 0:n]
        pe.matmul(acc[u][at][:, 0:n], k.centre, src, start=True, stop=True).then_inc(ln["centred"], 1)
    for u in range(LANES):
        pe.wait_ge(ln["squares"], i + u + 1)
        pe.matmul(acc[u][var][:, 0:n], k.average, squares[u][:, 0:n],
                  start=True, stop=True).then_inc(ln["var"], 1)


def norm_act(act, k, ln, i, squares, scale, acc, at, var, n=512):
    load_exp_ln(act)
    for u in range(LANES):
        act.wait_ge(ln["centred"], i + u + 1)
        act.activation(squares[u][:, 0:n], acc[u][at][:, 0:n], ACT.Square).then_inc(ln["squares"], 1)
    for u in range(LANES):
        act.wait_ge(ln["var"], i + u + 1)
        act.activation(scale[u][:, 0:n], acc[u][var][:, 0:n], ACT.Ln, bias=k.eps)\
            .then_inc(ln["log"], 1)
    for u in range(LANES):
        act.wait_ge(ln["log"], i + u + 1)
        act.activation(scale[u][:, 0:n], scale[u][:, 0:n], ACT.Exp, scale=-0.5)\
            .then_inc(ln["scale"], 1)


def norm_dve(dve, ln, i, scale, acc, at, out, n=512):
    for u in range(LANES):
        dve.wait_ge(ln["scale"], i + u + 1)
        dst = out[u] if n != 512 else out[u][:, 0:n]
        dve.tensor_tensor(dst, acc[u][at][:, 0:n], scale[u][:, 0:n], ALU.mult).then_inc(ln["scaled"], 1)


def setup(k):
    nc = k.nc
    with ExitStack() as ctx:
        loaded = k.semaphore(ctx, "const_loaded")
        block = ctx.enter_context(nc.Block())

        @block.sync
        def _(sp):
            sp.dma_start(k.const[:, :], k.ins["const"]).then_inc(loaded, 16)

        @block.vector
        def _(dve):
            dve.wait_ge(loaded, 16)
            dve.tensor_copy(k.select[:, :], k.const[:, 385:417])



def block_norm(k):
    nc = k.nc
    name = f"norm{k.norms}"
    k.norms += 1
    with ExitStack() as ctx:
        lanes = range(LANES)
        squares = [ctx.enter_context(nc.sbuf_tensor(f"{name}_sq{u}", [H, W2], F32)) for u in lanes]
        scale = [ctx.enter_context(nc.sbuf_tensor(f"{name}_scale{u}", [H, W2], F32)) for u in lanes]
        acc = [[ctx.enter_context(nc.psum_tensor(f"{name}_p{u}_{n}", [128, 512], F32)) for n in range(2)]
               for u in lanes]
        ln = {n: k.semaphore(ctx, f"{name}_{n}") for n in LN_STAGES}
        block = ctx.enter_context(nc.Block())

        @block.tensor
        def _(pe):
            with pe.Fori(0, NT // LANES) as step:
                i = step * LANES
                pe.wait_ge(ln["scaled"], i)
                norm_pe(pe, k, ln, i, [k.h[:, cols(i + u, W2)] for u in lanes], None, squares, acc,
                        0, 1, W2)

        @block.scalar
        def _(act):
            with act.Fori(0, NT // LANES) as step:
                norm_act(act, k, ln, step * LANES, squares, scale, acc, 0, 1, W2)

        @block.vector
        def _(dve):
            with dve.Fori(0, NT // LANES) as step:
                i = step * LANES
                norm_dve(dve, ln, i, scale, acc, 0, [k.xn[:, cols(i + u, W2)] for u in lanes], W2)



def router(k, tag, w_name, bias, scores):
    nc = k.nc
    NC = T // C
    with ExitStack() as ctx:
        def sb(name, shape, dt=F32):
            return ctx.enter_context(nc.sbuf_tensor(f"{tag}_{name}", shape, dt))

        def sem(name):
            return k.semaphore(ctx, f"{tag}_{name}")

        w, b = sb("w", [H, E]), sb("b", [C, E])
        logits, ex = sb("logits", [C, NC, E]), sb("ex", [C, NC, E])
        best, where = sb("best", [C, NC, E]), sb("where", [C, NC, E], U32)
        index = sb("index", [C, NC, E])
        first, second = sb("first", [C, NC, 1]), sb("second", [C, NC, 1])
        total = sb("total", [C, NC, 1])
        hot = sb("hot", [C, NC, E])
        wide = sb("wide", [C, NC, 128])
        rest = sb("rest", [128, 2, W2])
        raw = ctx.enter_context(nc.psum_tensor(f"{tag}_raw", [128, 512], F32))
        turned = [ctx.enter_context(nc.psum_tensor(f"{tag}_turned{n}", [128, 512], F32)) for n in range(4)]
        loaded, projected, chain = sem("loaded"), sem("projected"), sem("chain")
        shifted, exped, spread, turned_done = sem("shifted"), sem("exped"), sem("spread"), sem("turned")
        kept, part = sem("kept"), sem("part")
        block = ctx.enter_context(nc.Block())
        n_loaded = 32 if bias else 16

        @block.sync
        def _(sp):
            sp.dma_start(w[:, :], k.ins[w_name]).then_inc(loaded, 16)
            if bias:
                sp.dma_start(b[:, :], k.ins[bias]).then_inc(loaded, 16)

        @block.tensor
        def _(pe):
            pe.wait_ge(loaded, n_loaded)
            for c in range(NC):
                mm = pe.matmul(raw[0:C, c * E:(c + 1) * E], k.xn[:, c * C:(c + 1) * C], w[:, :],
                               start=True, stop=True)
            mm.then_inc(projected, 1)
            pe.wait_ge(spread, 1)
            for t in range(NT):
                if t >= 4:
                    pe.wait_ge(part, 4 * (t - 3))
                for c in range(4):
                    mm = pe.transpose(turned[t % 4][:, c * C:(c + 1) * C], wide[:, 4 * t + c, :],
                                      k.ident[0:C, 0:C])
                mm.then_inc(turned_done, 1)

        @block.scalar
        def _(act):
            load_exp_ln(act)
            act.wait_ge(shifted, 1)
            act.activation(ex[:, :, :], ex[:, :, :], ACT.Exp).then_inc(exped, 1)
            for t in range(NT):
                act.wait_ge(turned_done, t + 1)
                act.activation(k.wt[:, t * W2:(t + 1) * W2], turned[t % 4][0:E, 0:W2], ACT.Copy)\
                    .then_inc(kept, 1)

        @block.vector
        def _(dve):
            count = 0

            def link(ins):
                nonlocal count
                count += 1
                ins.then_inc(chain, 1)
                dve.wait_ge(chain, count)

            def over(t, n=E):
                return t.to_broadcast([C, NC, n])

            dve.memset(wide[:, :, :], 0.0).then_inc(chain, 1)
            count += 1
            dve.wait_ge(projected, 1)
            dve.wait_ge(loaded, n_loaded)
            rows = raw[0:C, 0:NC * E].rearrange("p (c e) -> p c e", e=E)
            iota = k.const[0:C, 417:425].rearrange("p (a e) -> p a e", a=1)
            if bias:
                link(dve.tensor_tensor(logits[:, :, :], rows,
                                       over(b[:, :].rearrange("p (a e) -> p a e", a=1)), ALU.add))
            else:
                link(dve.tensor_copy(logits[:, :, :], rows))
            if scores:
                link(dve.tensor_reduce(total[:, :, :], logits[:, :, :], AX, ALU.max))
                dve.tensor_tensor(ex[:, :, :], logits[:, :, :], over(total[:, :, :]),
                                  ALU.subtract).then_inc(shifted, 1)
                dve.wait_ge(exped, 1)
                link(dve.tensor_reduce(total[:, :, :], ex[:, :, :], AX, ALU.add))
                link(dve.reciprocal(total[:, :, :], total[:, :, :]))
                link(dve.tensor_tensor(logits[:, :, :], ex[:, :, :], over(total[:, :, :]), ALU.mult))
            for c in range(NC):
                ins = dve.max(best[:, c, :], logits[:, c, :])
            link(ins)
            for c in range(NC):
                ins = dve.max_index(where[:, c, :], best[:, c, :], logits[:, c, :])
            link(ins)
            link(dve.tensor_copy(index[:, :, :], where[:, :, :]))
            if scores:
                link(dve.tensor_tensor(total[:, :, :], best[:, :, 0:1], best[:, :, 1:2], ALU.add))
                link(dve.tensor_scalar(total[:, :, :], total[:, :, :], 1e-20, None, ALU.add))
                link(dve.reciprocal(total[:, :, :], total[:, :, :]))
                link(dve.tensor_tensor(first[:, :, :], best[:, :, 0:1], total[:, :, :], ALU.mult))
                link(dve.tensor_tensor(second[:, :, :], best[:, :, 1:2], total[:, :, :], ALU.mult))
            else:
                dve.tensor_tensor(ex[:, :, 0:2], best[:, :, 0:2],
                                  best[:, :, 0:1].to_broadcast([C, NC, 2]), ALU.subtract)
                dve.tensor_tensor(ex[:, :, 2:E], best[:, :, 2:E],
                                  best[:, :, 0:1].to_broadcast([C, NC, E - 2]), ALU.subtract)\
                    .then_inc(shifted, 1)
                dve.wait_ge(exped, 1)
                link(dve.tensor_tensor(total[:, :, :], ex[:, :, 0:1], ex[:, :, 1:2], ALU.add))
                link(dve.reciprocal(total[:, :, :], total[:, :, :]))
                link(dve.tensor_tensor(first[:, :, :], ex[:, :, 0:1], total[:, :, :], ALU.mult))
                link(dve.tensor_tensor(second[:, :, :], ex[:, :, 1:2], total[:, :, :], ALU.mult))
            link(dve.tensor_tensor(hot[:, :, :], over(iota), over(index[:, :, 0:1]), ALU.is_equal))
            link(dve.tensor_tensor(hot[:, :, :], hot[:, :, :], over(first[:, :, :]), ALU.mult))
            link(dve.tensor_tensor(logits[:, :, :], over(iota), over(index[:, :, 1:2]), ALU.is_equal))
            link(dve.tensor_tensor(logits[:, :, :], logits[:, :, :], over(second[:, :, :]), ALU.mult))
            for at in PARTS:
                ins = dve.tensor_tensor(wide[:, :, at:at + E], hot[:, :, :], logits[:, :, :], ALU.add)
            ins.then_inc(spread, 1)
            for t in range(NT):
                at = slice(t * W2, (t + 1) * W2)
                dve.wait_ge(kept, t + 1)
                split_in_three(dve, k.wt_parts[:, at], turned[t % 4][:, 0:W2], rest[:, t % 2, :],
                               part, 4 * t)


def split_in_three(dve, parts, source, rest, done, before):
    dve.tensor_copy(parts, source).then_inc(done, 1)
    dve.wait_ge(done, before + 1)
    dve.tensor_tensor(rest[64:128], source[64:128], parts[64:128], ALU.subtract).then_inc(done, 1)
    dve.wait_ge(done, before + 2)
    dve.tensor_copy(parts[64:128], rest[64:128]).then_inc(done, 1)
    dve.wait_ge(done, before + 3)
    dve.tensor_tensor(parts[96:128], rest[96:128], parts[96:128], ALU.subtract).then_inc(done, 1)
    dve.wait_ge(done, before + 4)



def attention0(k):
    with ExitStack() as ctx:
        xm = ctx.enter_context(k.nc.sbuf_tensor("xm", [H, B, L + 3], F32))
        external_attention(k, xm)
        mamba(k, xm)


def external_attention(k, xm):
    nc = k.nc
    with ExitStack() as ctx:
        def sb(name, shape, dt=F32):
            return ctx.enter_context(nc.sbuf_tensor(f"ea_{name}", shape, dt))

        def sem(name):
            return k.semaphore(ctx, f"ea_{name}")

        lanes = range(LANES)
        mk, mv, vec = sb("mk", [H, 128]), sb("mv", [H, 128]), sb("vec", [H, 2])
        mv_centred = sb("mv_centred", [128, H])
        xs = [sb(f"xs{u}", [H, W2]) for u in lanes]
        probs = [sb(f"probs{u}", [C, 4, 128]) for u in lanes]
        top = [sb(f"top{u}", [C, 4, 1]) for u in lanes]
        total = [sb(f"total{u}", [C, 4, 1]) for u in lanes]
        turned = [sb(f"turned{u}", [128, W2]) for u in lanes]
        squares = [sb(f"squares{u}", [H, W2]) for u in lanes]
        scale = [sb(f"scale{u}", [H, W2]) for u in lanes]
        normed = [sb(f"normed{u}", [H, W2]) for u in lanes]
        acc = [[ctx.enter_context(nc.psum_tensor(f"ea_p{u}_{n}", [128, 512], F32)) for n in range(4)]
               for u in lanes]
        loaded, prepared = sem("loaded"), sem("prepared")
        s = {n: sem(n) for n in ("copied", "logits", "top", "shifted", "exps", "total", "recip",
                                 "probs", "turned", "kept", "affine", "gelu", "xm")}
        ln = {n: sem("ln_" + n) for n in LN_STAGES}
        block = ctx.enter_context(nc.Block())

        @block.sync
        def _(sp):
            for dst, src in ((mk, "mk"), (mv, "mv"), (vec, "ea_vec")):
                sp.dma_start(dst[:, :], k.ins[src]).then_inc(loaded, 16)

        @block.gpsimd
        def _(pool):
            with pool.Fori(0, NT // LANES) as step:
                i = step * LANES
                for u in lanes:
                    pool.wait_ge(s["logits"], i)
                    pool.tensor_copy(xs[u][:, :], k.xn[:, cols(i + u, W2)]).then_inc(s["copied"], 1)

        @block.tensor
        def _(pe):
            pe.wait_ge(loaded, 48)
            pe.matmul(acc[0][0][:, 0:H], mv[:, :], k.centre, start=True, stop=True).then_inc(prepared, 1)
            pe.wait_ge(prepared, 2)
            with pe.Fori(0, NT // LANES) as step:
                i = step * LANES
                pe.wait_ge(s["xm"], i)
                for u in lanes:
                    pe.wait_ge(s["copied"], i + u + 1)
                    for c in range(4):
                        mm = pe.matmul(acc[u][0][0:C, c * 128:(c + 1) * 128],
                                       xs[u][:, c * C:(c + 1) * C], mk[:, :], start=True, stop=True)
                    mm.then_inc(s["logits"], 1)
                for u in lanes:
                    pe.wait_ge(s["probs"], i + u + 1)
                    for c in range(4):
                        mm = pe.transpose(acc[u][1][:, c * C:(c + 1) * C], probs[u][:, c, :],
                                          k.ident[0:C, 0:C])
                    mm.then_inc(s["turned"], 1)
                for u in lanes:
                    pe.wait_ge(s["kept"], i + u + 1)
                    pe.matmul(acc[u][2][:, 0:W2], mv_centred[:, :], turned[u][:, :],
                              start=True, stop=True).then_inc(ln["centred"], 1)
                for u in lanes:
                    pe.wait_ge(ln["squares"], i + u + 1)
                    pe.matmul(acc[u][3][:, 0:W2], k.average, squares[u][:, :],
                              start=True, stop=True).then_inc(ln["var"], 1)

        @block.scalar
        def _(act):
            with act.Fori(0, NT // LANES) as step:
                i = step * LANES
                load_exp_ln(act)
                for u in lanes:
                    act.wait_ge(s["shifted"], i + u + 1)
                    act.activation(probs[u][:, :, :], probs[u][:, :, :], ACT.Exp).then_inc(s["exps"], 1)
                for u in lanes:
                    act.wait_ge(s["turned"], i + u + 1)
                    act.activation(turned[u][:, :], acc[u][1][:, 0:W2], ACT.Copy).then_inc(s["kept"], 1)
                norm_act(act, k, ln, i, squares, scale, acc, 2, 3, W2)
                for u in lanes:
                    act.wait_ge(s["affine"], i + u + 1)
                    act.activation(normed[u][:, :], normed[u][:, :], ACT.Gelu).then_inc(s["gelu"], 1)

        @block.vector
        def _(dve):
            dve.memset(xm[:, :, 0:3], 0.0)
            dve.wait_ge(prepared, 1)
            dve.tensor_copy(mv_centred[:, :], acc[0][0][:, 0:H]).then_inc(prepared, 1)
            dve.wait_ge(loaded, 48)
            with dve.Fori(0, NT // LANES) as step:
                i = step * LANES
                over = lambda t: t[:, :, 0:1].to_broadcast([C, 4, 128])
                rows = lambda u: acc[u][0][0:C, :].rearrange("p (c s) -> p c s", c=4)
                for u in lanes:
                    dve.wait_ge(s["logits"], i + u + 1)
                    dve.tensor_reduce(top[u][:, :, :], rows(u), AX, ALU.max).then_inc(s["top"], 1)
                for u in lanes:
                    dve.wait_ge(s["top"], i + u + 1)
                    dve.tensor_tensor(probs[u][:, :, :], rows(u), over(top[u]), ALU.subtract)\
                        .then_inc(s["shifted"], 1)
                for u in lanes:
                    dve.wait_ge(s["exps"], i + u + 1)
                    dve.tensor_reduce(total[u][:, :, :], probs[u][:, :, :], AX, ALU.add)\
                        .then_inc(s["total"], 1)
                for u in lanes:
                    dve.wait_ge(s["total"], i + u + 1)
                    dve.reciprocal(total[u][:, :, :], total[u][:, :, :]).then_inc(s["recip"], 1)
                for u in lanes:
                    dve.wait_ge(s["recip"], i + u + 1)
                    dve.tensor_tensor(probs[u][:, :, :], probs[u][:, :, :], over(total[u]), ALU.mult)\
                        .then_inc(s["probs"], 1)
                norm_dve(dve, ln, i, scale, acc, 2, [normed[u][:, :] for u in lanes], W2)
                for u in lanes:
                    dve.wait_ge(ln["scaled"], i + u + 1)
                    dve.tensor_scalar(normed[u][:, :], normed[u][:, :], vec[:, 0:1], vec[:, 1:2],
                                      ALU.mult, ALU.add).then_inc(s["affine"], 1)
                for u in lanes:
                    dve.wait_ge(s["gelu"], i + u + 1)
                    two = lambda ap: ap.rearrange("p (b s) -> p b s", b=2)
                    dve.tensor_tensor(xm[:, cols(i + u, 2), 3:L + 3], two(normed[u][:, :]),
                                      two(k.xn[:, cols(i + u, W2)]), ALU.add).then_inc(s["xm"], 1)


def mamba(k, xm):
    nc = k.nc
    HV = range(2)
    with ExitStack() as ctx:
        def sb(name, shape, dt=F32):
            return ctx.enter_context(nc.sbuf_tensor(f"ma_{name}", shape, dt))

        def sem(name):
            return k.semaphore(ctx, f"ma_{name}")

        w_in, w_z = sb("w_in", [H, 2, H]), sb("w_z", [H, 2, H])
        w_bc, w_dtr = sb("w_bc", [H, 2, 128]), sb("w_dtr", [H, 2, DR])
        w_dt, w_out = sb("w_dt", [DR, 2, H]), sb("w_out", [H, 2, H])
        vec = sb("vec", [H, 2, 3])
        conv, a = sb("conv", [H, 2, 4]), sb("a", [H, 2, DS])
        w_tap = sb("w_tap", [H, 4, 2, H])
        scaled_in = sb("scaled_in", [H, 2, 4, H])
        xact = [[sb(f"xact{q}{h}", [H, W2]) for h in HV] for q in HV]
        gate = [[sb(f"gate{q}{h}", [H, W2]) for h in HV] for q in HV]
        dt = [[sb(f"dt{q}{h}", [H, W2]) for h in HV] for q in HV]
        dtx = [[sb(f"dtx{q}{h}", [H, W2]) for h in HV] for q in HV]
        bc = [sb(f"bc{q}", [128, W2], BF16) for q in HV]
        rest, dtr = sb("rest", [128, W2]), sb("dtr", [DR, W2])
        soft = [sb(f"soft{h}", [H, W2]) for h in HV]
        da = [[sb(f"da{h}{n}", [H, W2]) for n in range(2)] for h in HV]
        dbx = [sb(f"dbx{n}", [H, W2]) for n in range(2)]
        state = [sb(f"state{n}", [H, W2]) for n in range(4)]
        c_kept = [sb(f"c{n}", [H, W2]) for n in range(2)]
        hc = [sb(f"hc{n}", [H, W2]) for n in range(4)]
        y = [sb(f"y{h}", [H, W2]) for h in HV]
        psum = lambda n: ctx.enter_context(nc.psum_tensor(f"ma_ps_{n}", [128, 512], F32))
        p = [psum("p0"), psum("p1")]
        b_all, c_all = [psum("b0"), psum("b1")], [psum("c0"), psum("c1")]
        y_sum = [psum("y0"), psum("y1")]
        loaded, scaled_w, turned_w, taps, a_exp, a_ready = (sem(n) for n in (
            "loaded", "scaled_w", "turned_w", "taps", "a_exp", "a_ready"))
        s = {n: sem(n) for n in (
            "conv", "xact", "z", "gate", "bc_sum", "split", "dtr_sum", "dtr", "dt_sum", "abs", "exp",
            "log", "relu", "dt", "dtx",
            "b", "c", "c_kept", "da", "dbx", "scan", "hc", "y_add",
            "y_skip", "y", "out", "added")}
        block = ctx.enter_context(nc.Block())
        N_LOADED = 16 * 9
        NS = 2 * DS

        @block.sync
        def _(sp):
            for dst, src in ((w_in[:, :, :], "in_proj_x"), (w_z[:, :, :], "in_proj_z"),
                             (w_bc[:, :, :], "x_proj_bc"), (w_dtr[:, :, :], "x_proj_dt"),
                             (w_dt[:, :, :], "dt_proj"), (w_out[:, :, :], "out_proj"),
                             (vec[:, :, :], "mamba_vec"), (conv[:, :, :], "conv_w"),
                             (a[:, :, :], "a_log")):
                sp.dma_start(dst, k.ins[src]).then_inc(loaded, 16)

        def run(eng, tile):
            with eng.Fori(0, NT // 2 - 1) as step:
                for u in range(2):
                    tile(step * 2 + u, u, True)
            for u in range(2):
                tile(NT - 2 + u, u, u == 0)

        @block.tensor
        def _(pe):
            pe.wait_ge(loaded, N_LOADED)
            for h in HV:
                pe.wait_ge(scaled_w, 4 * (h + 1))
                for tap in range(4):
                    mm = pe.transpose(p[h][:, tap * H:(tap + 1) * H], scaled_in[:, h, tap, :], k.ident)
                mm.then_inc(turned_w, 1)
            pe.wait_ge(taps, 2)

            def conv_half(t, h, first=False):
                if not first:
                    pe.wait_ge(s["added"], t - 1)
                for tap in range(4):
                    mm = pe.matmul(p[h][:, 0:W2], w_tap[:, tap, h, :],
                                   xm[:, cols(t, 2), tap:tap + L], start=tap == 0, stop=tap == 3)
                mm.then_inc(s["conv"], 1)

            def z_half(t, h):
                pe.wait_ge(s["xact"], 2 * t + h + 1)
                pe.matmul(p[h][:, 0:W2], w_z[:, h, :], xm[:, cols(t, 2), 3:3 + L],
                          start=True, stop=True).then_inc(s["z"], 1)

            def bc_rows(t, q):
                pe.wait_ge(s["gate"], 2 * t + 1)
                for h in HV:
                    mm = pe.matmul(p[0][:, 0:W2], w_bc[:, h, :], xact[q][h][:, :],
                                   start=h == 0, stop=h == 1)
                mm.then_inc(s["bc_sum"], 1)

            def dt_rank(t, q):
                pe.wait_ge(s["gate"], 2 * t + 2)
                for h in HV:
                    mm = pe.matmul(p[1][0:DR, 0:W2], w_dtr[:, h, :], xact[q][h][:, :],
                                   start=h == 0, stop=h == 1)
                mm.then_inc(s["dtr_sum"], 1)

            def dt_half(t, h):
                pe.wait_ge(s["dtr"], t + 1)
                pe.wait_ge(s["split"], 4 * (t + 1))
                pe.matmul(p[h][:, 0:W2], w_dt[:, h, :], dtr[:, :], start=True, stop=True)\
                    .then_inc(s["dt_sum"], 1)

            def ahead(t, q, first=False):
                return {1: lambda: conv_half(t, 0, first), 3: lambda: conv_half(t, 1, first),
                        6: lambda: z_half(t, 0), 7: lambda: z_half(t, 1), 9: lambda: bc_rows(t, q),
                        10: lambda: dt_rank(t, q), 12: lambda: (dt_half(t, 0), dt_half(t, 1))}

            for f in ahead(0, 0, True).values():
                f()

            def tile(t, u, more):
                steps = ahead(t + 1, 1 - u) if more else {}
                done, states = t * NS, t * DS

                def rows(n):
                    if n == 0:
                        pe.wait_ge(s["split"], 4 * (t + 1))
                    if n >= 2:
                        pe.wait_ge(s["dbx"], done + 2 * (n - 1))
                        pe.wait_ge(s["c_kept"], states + n - 1)
                    else:
                        pe.wait_ge(s["dbx"], done)
                        pe.wait_ge(s["c_kept"], states)
                    pe.matmul(b_all[n % 2][:, 0:W2], k.select[:, n:n + 1].to_broadcast([128, 128]),
                              bc[u][:, :], start=True, stop=True).then_inc(s["b"], 1)
                    pe.matmul(c_all[n % 2][:, 0:W2],
                              k.select[:, DS + n:DS + n + 1].to_broadcast([128, 128]),
                              bc[u][:, :], start=True, stop=True).then_inc(s["c"], 1)

                rows(0)
                for n in range(DS):
                    if n + 1 < DS:
                        rows(n + 1)
                    if n in steps:
                        steps[n]()
                    if n == 0:
                        pe.wait_ge(s["y_skip"], 2 * t)
                    for h in HV:
                        pe.wait_ge(s["hc"], done + 2 * n + h + 1)
                        pe.matmul(y_sum[h][:, 0:W2], k.ident, hc[(2 * n + h) % 4][:, :],
                                  start=n == 0, stop=n == DS - 1).then_inc(s["y_add"], 1)
                pe.wait_ge(s["y"], 2 * (t + 1))
                if more:
                    pe.wait_ge(s["relu"], 2 * (t + 2))
                for h in HV:
                    mm = pe.matmul(p[0][:, 0:W2], w_out[:, h, :], y[h][:, :], start=h == 0, stop=h == 1)
                mm.then_inc(s["out"], 1)

            run(pe, tile)

        @block.scalar
        def _(act):
            act.wait_ge(loaded, N_LOADED)
            load_exp_ln(act)
            act.activation(a[:, :, :], a[:, :, :], ACT.Exp).then_inc(a_exp, 1)
            for h in HV:
                act.wait_ge(turned_w, h + 1)
                act.activation(w_tap[:, :, h, :], p[h][:, :].rearrange("p (t d) -> p t d", t=4),
                               ACT.Copy).then_inc(taps, 1)
            act.wait_ge(a_ready, 1)

            def xacts(t, q):
                for h in HV:
                    act.wait_ge(s["conv"], 2 * t + h + 1)
                    act.activation(xact[q][h][:, :], p[h][:, 0:W2], ACT.Silu, bias=vec[:, h, 0:1])\
                        .then_inc(s["xact"], 1)

            def gates(t, q):
                for h in HV:
                    act.wait_ge(s["z"], 2 * t + h + 1)
                    act.activation(gate[q][h][:, :], p[h][:, 0:W2], ACT.Silu).then_inc(s["gate"], 1)

            def keep_rank(t):
                act.wait_ge(s["dtr_sum"], t + 1)
                act.activation(dtr[:, :], p[1][0:DR, 0:W2], ACT.Copy).then_inc(s["dtr"], 1)

            def softplus(t, q):
                load_exp_ln(act)
                for h in HV:
                    act.wait_ge(s["dt_sum"], 2 * t + h + 1)
                    act.wait_ge(s["dt"], 2 * t)
                    act.activation(soft[h][:, :], p[h][:, 0:W2], ACT.Abs, bias=vec[:, h, 1:2])\
                        .then_inc(s["abs"], 1)
                for h in HV:
                    act.wait_ge(s["abs"], 2 * t + h + 1)
                    act.activation(soft[h][:, :], soft[h][:, :], ACT.Exp, scale=-1.0)\
                        .then_inc(s["exp"], 1)
                for h in HV:
                    act.wait_ge(s["exp"], 2 * t + h + 1)
                    act.activation(soft[h][:, :], soft[h][:, :], ACT.Ln, bias=1.0).then_inc(s["log"], 1)

            def ahead(t, q):
                return {6: lambda: xacts(t, q), 8: lambda: gates(t, q), 11: lambda: keep_rank(t),
                        13: lambda: softplus(t, q)}

            for f in ahead(0, 0).values():
                f()

            def tile(t, u, more):
                steps = ahead(t + 1, 1 - u) if more else {}
                done, states = t * NS, t * DS
                act.wait_ge(s["dt"], 2 * (t + 1))
                for n in range(DS):
                    for h in HV:
                        act.wait_ge(s["scan"], done + 2 * n - 3 + h if n >= 2 else done)
                        act.activation(da[h][n % 2][:, :], dt[u][h][:, :], ACT.Exp,
                                       scale=a[:, h, n:n + 1]).then_inc(s["da"], 1)
                    act.wait_ge(s["c"], states + n + 1)
                    act.wait_ge(s["hc"], done + 2 * (n - 1) if n >= 2 else done)
                    act.activation(c_kept[n % 2][:, :], c_all[n % 2][:, 0:W2], ACT.Copy)\
                        .then_inc(s["c_kept"], 1)
                    if n in steps:
                        steps[n]()
                        load_exp_ln(act)

            run(act, tile)

        @block.gpsimd
        def _(pool):
            def tile(t, u, more):
                done, states = t * NS, t * DS
                for n in range(DS):
                    pool.wait_ge(s["c_kept"], states + n + 1)
                    for h in HV:
                        m = 2 * n + h
                        pool.wait_ge(s["scan"], done + m + 1)
                        pool.wait_ge(s["y_add"], done + m - 3 if m >= 4 else done)
                        pool.tensor_tensor(hc[m % 4][:, :], state[m % 4][:, :], c_kept[n % 2][:, :],
                                           ALU.mult).then_inc(s["hc"], 1)

            run(pool, tile)

        @block.vector
        def _(dve):
            dve.wait_ge(loaded, N_LOADED)
            for h in HV:
                for tap in range(4):
                    dve.tensor_scalar(scaled_in[:, h, tap, :], w_in[:, h, :], conv[:, h, tap:tap + 1],
                                      None, ALU.mult).then_inc(scaled_w, 1)
            dve.wait_ge(a_exp, 1)
            dve.tensor_scalar(a[:, :, :], a[:, :, :], -1.0, None, ALU.mult).then_inc(a_ready, 1)

            def split(t, q):
                dve.wait_ge(s["bc_sum"], t + 1)
                split_in_three(dve, bc[q][:, :], p[0][:, 0:W2], rest[:, :], s["split"], 4 * t)

            def steps_of_time(t, q):
                for h in HV:
                    dve.wait_ge(s["abs"], 2 * t + h + 1)
                    dve.tensor_scalar(dt[q][h][:, :], p[h][:, 0:W2], vec[:, h, 1:2], 0.0,
                                      ALU.add, ALU.max).then_inc(s["relu"], 1)
                for h in HV:
                    dve.wait_ge(s["relu"], 2 * t + h + 1)
                    dve.wait_ge(s["log"], 2 * t + h + 1)
                    dve.tensor_tensor(dt[q][h][:, :], dt[q][h][:, :], soft[h][:, :], ALU.add)\
                        .then_inc(s["dt"], 1)
                for h in HV:
                    dve.wait_ge(s["dt"], 2 * t + h + 1)
                    dve.tensor_tensor(dtx[q][h][:, :], dt[q][h][:, :], xact[q][h][:, :], ALU.mult)\
                        .then_inc(s["dtx"], 1)

            def ahead(t, q):
                return {11: lambda: split(t, q), 14: lambda: steps_of_time(t, q)}

            for f in ahead(0, 0).values():
                f()

            def tile(t, u, more):
                steps = ahead(t + 1, 1 - u) if more else {}
                done, states = t * NS, t * DS
                dve.wait_ge(s["dtx"], 2 * (t + 1))
                for n in range(DS):
                    for h in HV:
                        m = 2 * n + h
                        dve.wait_ge(s["b"], states + n + 1)
                        dve.wait_ge(s["scan"], done + m - 1 if m >= 2 else done)
                        dve.tensor_tensor(dbx[m % 2][:, :], b_all[n % 2][:, 0:W2], dtx[u][h][:, :],
                                          ALU.mult).then_inc(s["dbx"], 1)
                        dve.wait_ge(s["dbx"], done + m + 1)
                        dve.wait_ge(s["da"], done + m + 1)
                        dve.wait_ge(s["hc"], done + m - 3 if m >= 4 else done)
                        for b in range(2):
                            at = slice(b * L, (b + 1) * L)
                            ins = dve.tensor_tensor_scan(state[m % 4][:, at], da[h][n % 2][:, at],
                                                         dbx[m % 2][:, at], 0.0, ALU.mult, ALU.add)
                        ins.then_inc(s["scan"], 1)
                    if n in steps:
                        steps[n]()
                dve.wait_ge(s["y_add"], done + NS)
                dve.wait_ge(s["out"], t)
                for h in HV:
                    dve.scalar_tensor_tensor(y[h][:, :], xact[u][h][:, :], vec[:, h, 2:3],
                                             y_sum[h][:, 0:W2], ALU.mult, ALU.add)\
                        .then_inc(s["y_skip"], 1)
                for h in HV:
                    dve.wait_ge(s["y_skip"], 2 * t + h + 1)
                    dve.tensor_tensor(y[h][:, :], y[h][:, :], gate[u][h][:, :], ALU.mult)\
                        .then_inc(s["y"], 1)
                dve.wait_ge(s["out"], t + 1)
                dve.tensor_tensor(k.h[:, cols(t, W2)], p[0][:, 0:W2], k.h[:, cols(t, W2)], ALU.add)\
                    .then_inc(s["added"], 1)

            run(dve, tile)




def experts0(k):
    router(k, "route0", "router_w", "router_b", scores=False)
    nc = k.nc
    with ExitStack() as ctx:
        def sb(name, shape, dt=F32):
            return ctx.enter_context(nc.sbuf_tensor(f"ex0_{name}", shape, dt))

        def sem(name):
            return k.semaphore(ctx, f"ex0_{name}")

        gate_up, down = sb("gate_up", [H, E, 2 * I0]), sb("down", [H, E, 2, H])
        down_bias, bias = sb("down_bias", [E, H]), sb("bias", [H, E, 4])
        gate_scaled, up_one = sb("gate_scaled", [H, E, 2]), sb("up_one", [H, E, 2])
        sig = [sb(f"sig{n}", [H, W2]) for n in range(2)]
        gelu = [sb(f"gelu{n}", [H, W2]) for n in range(2)]
        inner = [sb(f"inner{n}", [H, W2]) for n in range(2)]
        weighted = [sb(f"weighted{n}", [H, W2]) for n in range(2)]
        psum = lambda n: ctx.enter_context(nc.psum_tensor(f"ex0_{n}", [128, 512], F32))
        gate, up = [psum("gate0"), psum("gate1")], [psum("up0"), psum("up1")]
        weight, total = [psum("weight0"), psum("weight1")], psum("total")
        loaded, ready = sem("loaded"), sem("ready")
        s = {n: sem(n) for n in ("gated", "upped", "spread", "sig", "gelu", "inner", "weighted",
                                 "downed", "added")}
        block = ctx.enter_context(nc.Block())
        halves = [(e, j) for e in range(E) for j in range(2)]
        NHF = len(halves)

        @block.sync
        def _(sp):
            for dst, src in ((gate_up[:, :, :], "gate_up"), (down[:, :, :, :], "down"),
                             (down_bias[:, :], "down_bias"), (bias[:, :, :], "gate_up_bias")):
                sp.dma_start(dst, k.ins[src]).then_inc(loaded, 16)

        @block.tensor
        def _(pe):
            pe.wait_ge(loaded, 64)
            with pe.Fori(0, NT) as t:
                done = t * NHF
                x = k.xn[:, cols(t, W2)]

                def down_half(n):
                    e, j = halves[n]
                    pe.wait_ge(s["weighted"], done + n + 1)
                    pe.matmul(total[:, 0:W2], down[:, e, j, :], weighted[n % 2][:, :], start=False,
                              stop=n == NHF - 1).then_inc(s["downed"], 1)

                for n, (e, j) in enumerate(halves):
                    if n >= 2:
                        pe.wait_ge(s["gelu"], done + n - 1)
                    elif n == 0:
                        pe.wait_ge(s["weighted"], done)
                    pe.matmul(gate[j][:, 0:W2], gate_up[:, e, j * H:(j + 1) * H], x,
                              start=True, stop=True).then_inc(s["gated"], 1)
                    if n >= 2:
                        pe.wait_ge(s["inner"], done + n - 1)
                    pe.matmul(up[j][:, 0:W2], gate_up[:, e, I0 + j * H:I0 + (j + 1) * H], x,
                              start=True, stop=True).then_inc(s["upped"], 1)
                    if j == 0:
                        if n >= 4:
                            pe.wait_ge(s["weighted"], done + n - 2)
                        pe.matmul(weight[e % 2][:, 0:W2], k.select[:, e:e + 1].to_broadcast([128, 128]),
                                  k.wt_parts[:, cols(t, W2)], start=True, stop=True)\
                            .then_inc(s["spread"], 1)
                    if n == 0:
                        pe.wait_ge(s["added"], t)
                        pe.matmul(total[:, 0:W2], down_bias[:, :], k.wt[:, cols(t, W2)],
                                  start=True, stop=False)
                    else:
                        down_half(n - 1)
                down_half(NHF - 1)

        @block.scalar
        def _(act):
            act.wait_ge(ready, 2)
            with act.Fori(0, NT) as t:
                done = t * NHF
                for n, (e, j) in enumerate(halves):
                    act.wait_ge(s["gated"], done + n + 1)
                    if n >= 2:
                        act.wait_ge(s["gelu"], done + n - 1)
                    act.activation(sig[j][:, :], gate[j][:, 0:W2], ACT.Sigmoid,
                                   bias=gate_scaled[:, e, j:j + 1], scale=1.702).then_inc(s["sig"], 1)

        @block.vector
        def _(dve):
            dve.wait_ge(loaded, 64)
            dve.tensor_scalar(gate_scaled[:, :, :], bias[:, :, 0:2], 1.702, None, ALU.mult)\
                .then_inc(ready, 1)
            dve.tensor_scalar(up_one[:, :, :], bias[:, :, 2:4], 1.0, None, ALU.add).then_inc(ready, 1)
            dve.wait_ge(ready, 2)
            with dve.Fori(0, NT) as t:
                done = t * NHF
                for n, (e, j) in enumerate(halves):
                    dve.wait_ge(s["sig"], done + n + 1)
                    dve.scalar_tensor_tensor(gelu[j][:, :], gate[j][:, 0:W2], bias[:, e, j:j + 1],
                                             sig[j][:, :], ALU.add, ALU.mult).then_inc(s["gelu"], 1)
                    dve.wait_ge(s["gelu"], done + n + 1)
                    dve.wait_ge(s["upped"], done + n + 1)
                    dve.scalar_tensor_tensor(inner[j][:, :], up[j][:, 0:W2], up_one[:, e, j:j + 1],
                                             gelu[j][:, :], ALU.add, ALU.mult).then_inc(s["inner"], 1)
                    dve.wait_ge(s["inner"], done + n + 1)
                    if j == 0:
                        dve.wait_ge(s["spread"], t * E + e + 1)
                    if n >= 2:
                        dve.wait_ge(s["downed"], done + n - 1)
                    dve.tensor_tensor(weighted[j][:, :], inner[j][:, :], weight[e % 2][:, 0:W2],
                                      ALU.mult).then_inc(s["weighted"], 1)
                dve.wait_ge(s["downed"], done + NHF)
                dve.tensor_tensor(k.h[:, cols(t, W2)], total[:, 0:W2], k.h[:, cols(t, W2)], ALU.add)\
                    .then_inc(s["added"], 1)



def attention1(k):
    with ExitStack() as ctx:
        k.r = ctx.enter_context(k.nc.sbuf_tensor("r", [H, T], F32))
        input_projection(k)
        fast_weights(k, 0)
        feed_forward(k)
        fast_weights(k, 1)


def input_projection(k):
    nc = k.nc
    with ExitStack() as ctx:
        def sb(name, shape, dt=F32):
            return ctx.enter_context(nc.sbuf_tensor(f"ip_{name}", shape, dt))

        def sem(name):
            return k.semaphore(ctx, f"ip_{name}")

        lanes = range(LANES)
        w, vec = sb("w", [H, H]), sb("vec", [H, 3])
        squares = [sb(f"squares{u}", [H, W2]) for u in lanes]
        scale = [sb(f"scale{u}", [H, W2]) for u in lanes]
        acc = [[ctx.enter_context(nc.psum_tensor(f"ip_p{u}_{n}", [128, 512], F32)) for n in range(3)]
               for u in lanes]
        loaded, projected, added, affine = sem("loaded"), sem("projected"), sem("added"), sem("affine")
        ln = {n: sem("ln_" + n) for n in LN_STAGES}
        block = ctx.enter_context(nc.Block())

        @block.sync
        def _(sp):
            sp.dma_start(w[:, :], k.ins["ip_w"]).then_inc(loaded, 16)
            sp.dma_start(vec[:, :], k.ins["ip_vec"]).then_inc(loaded, 16)

        @block.tensor
        def _(pe):
            pe.wait_ge(loaded, 32)
            with pe.Fori(0, NT // LANES) as step:
                i = step * LANES
                pe.wait_ge(affine, i)
                for u in lanes:
                    pe.matmul(acc[u][0][:, 0:W2], w[:, :], k.xn[:, cols(i + u, W2)],
                              start=True, stop=True).then_inc(projected, 1)
                norm_pe(pe, k, ln, i, [k.r[:, cols(i + u, W2)] for u in lanes], added, squares, acc,
                        1, 2, W2)

        @block.scalar
        def _(act):
            with act.Fori(0, NT // LANES) as step:
                norm_act(act, k, ln, step * LANES, squares, scale, acc, 1, 2, W2)

        @block.vector
        def _(dve):
            dve.wait_ge(loaded, 32)
            with dve.Fori(0, NT // LANES) as step:
                i = step * LANES
                xn = [k.xn[:, cols(i + u, W2)] for u in lanes]
                for u in lanes:
                    dve.wait_ge(projected, i + u + 1)
                    dve.tensor_scalar(k.r[:, cols(i + u, W2)], acc[u][0][:, 0:W2], vec[:, 0:1], None,
                                      ALU.add).then_inc(added, 1)
                norm_dve(dve, ln, i, scale, acc, 1, xn, W2)
                for u in lanes:
                    dve.wait_ge(ln["scaled"], i + u + 1)
                    dve.tensor_scalar(xn[u], xn[u], vec[:, 1:2], vec[:, 2:3], ALU.mult, ALU.add)\
                        .then_inc(affine, 1)


def feed_forward(k):
    nc = k.nc
    NB = FF // H
    with ExitStack() as ctx:
        def sb(name, shape, dt=F32):
            return ctx.enter_context(nc.sbuf_tensor(f"ff_{name}", shape, dt))

        def sem(name):
            return k.semaphore(ctx, f"ff_{name}")

        lanes = range(LANES)
        w1, w2 = sb("w1", [H, NB, H]), sb("w2", [H, NB, H])
        vec = sb("vec", [H, 5 + NB])
        squares = [sb(f"squares{u}", [H, W2]) for u in lanes]
        scale = [sb(f"scale{u}", [H, W2]) for u in lanes]
        normed = [sb(f"normed{u}", [H, W2]) for u in lanes]
        hidden = [[sb(f"hidden{u}{n}", [H, W2]) for n in range(NB)] for u in lanes]
        acc = [[ctx.enter_context(nc.psum_tensor(f"ff_p{u}_{n}", [128, 512], F32)) for n in range(4)]
               for u in lanes]
        loaded = sem("loaded")
        s = {n: sem(n) for n in ("affine1", "up", "relu", "down", "added", "affine2")}
        ln = [{n: sem(f"ln{j}_{n}") for n in LN_STAGES} for j in range(2)]
        block = ctx.enter_context(nc.Block())

        @block.sync
        def _(sp):
            for dst, src in ((w1[:, :, :], "ff_w1"), (w2[:, :, :], "ff_w2"), (vec[:, :], "ff_vec")):
                sp.dma_start(dst, k.ins[src]).then_inc(loaded, 16)

        @block.tensor
        def _(pe):
            pe.wait_ge(loaded, 48)
            with pe.Fori(0, NT // LANES) as step:
                i = step * LANES
                pe.wait_ge(s["affine2"], i)
                norm_pe(pe, k, ln[0], i, [k.r[:, cols(i + u, W2)] for u in lanes], None, squares,
                        acc, 0, 1, W2)
                for n in range(NB):
                    for u in lanes:
                        if n == 0:
                            pe.wait_ge(s["affine1"], i + u + 1)
                        else:
                            pe.wait_ge(s["relu"], i * NB + (n - 1) * LANES + u + 1)
                        pe.matmul(acc[u][1 + n % 2][:, 0:W2], w1[:, n, :], normed[u][:, :],
                                  start=True, stop=True).then_inc(s["up"], 1)
                for u in lanes:
                    pe.wait_ge(s["relu"], (i + LANES) * NB)
                    for n in range(NB):
                        mm = pe.matmul(acc[u][3][:, 0:W2], w2[:, n, :], hidden[u][n][:, :],
                                       start=n == 0, stop=n == NB - 1)
                    mm.then_inc(s["down"], 1)
                norm_pe(pe, k, ln[1], i, [k.r[:, cols(i + u, W2)] for u in lanes], s["added"],
                        squares, acc, 0, 1, W2)

        @block.scalar
        def _(act):
            act.wait_ge(loaded, 48)
            with act.Fori(0, NT // LANES) as step:
                i = step * LANES
                norm_act(act, k, ln[0], i, squares, scale, acc, 0, 1, W2)
                for n in range(NB):
                    for u in lanes:
                        act.wait_ge(s["up"], i * NB + n * LANES + u + 1)
                        act.activation(hidden[u][n][:, :], acc[u][1 + n % 2][:, 0:W2], ACT.Relu,
                                       bias=vec[:, 5 + n:6 + n]).then_inc(s["relu"], 1)
                norm_act(act, k, ln[1], i, squares, scale, acc, 0, 1, W2)

        @block.vector
        def _(dve):
            dve.wait_ge(loaded, 48)
            with dve.Fori(0, NT // LANES) as step:
                i = step * LANES
                xn = [k.xn[:, cols(i + u, W2)] for u in lanes]
                norm_dve(dve, ln[0], i, scale, acc, 0, [normed[u][:, :] for u in lanes], W2)
                for u in lanes:
                    dve.wait_ge(ln[0]["scaled"], i + u + 1)
                    dve.tensor_scalar(normed[u][:, :], normed[u][:, :], vec[:, 0:1], vec[:, 1:2],
                                      ALU.mult, ALU.add).then_inc(s["affine1"], 1)
                for u in lanes:
                    r = k.r[:, cols(i + u, W2)]
                    dve.wait_ge(s["down"], i + u + 1)
                    dve.scalar_tensor_tensor(r, acc[u][3][:, 0:W2], vec[:, 4:5], r, ALU.add, ALU.add)\
                        .then_inc(s["added"], 1)
                norm_dve(dve, ln[1], i, scale, acc, 0, xn, W2)
                for u in lanes:
                    dve.wait_ge(ln[1]["scaled"], i + u + 1)
                    dve.tensor_scalar(xn[u], xn[u], vec[:, 2:3], vec[:, 3:4], ALU.mult, ALU.add)\
                        .then_inc(s["affine2"], 1)


def fast_weights(k, layer):
    nc = k.nc
    tag = f"fw{layer}"
    NP = NH // 2
    BLOCK = 32
    NB = 128 // BLOCK
    LANES_OF = NB * LANES * NH
    with ExitStack() as ctx:
        def sb(name, shape, dt=F32):
            return ctx.enter_context(nc.sbuf_tensor(f"{tag}_{name}", shape, dt))

        def sem(name):
            return k.semaphore(ctx, f"{tag}_{name}")

        chunks = range(LANES)
        w = sb("w", [H, 3 * NH * D + NH])
        w_out = sb("w_out", [H, NP, H])
        masks = sb("masks", [128, MASK_COLS])
        lower = masks[:, 0:128].rearrange("p (a c) -> p a c", a=1)
        unit = masks[:, 128:MASK_COLS]
        xs = sb("xs", [H, L])
        per = lambda name, shape: [sb(f"{name}{u}", shape) for u in chunks]
        both = lambda name, shape: [per(f"{name}{parity}_", shape) for parity in range(2)]
        top = {n: per("top_" + n, [C, NH, 1]) for n in "kq"}
        total = {n: per("total_" + n, [C, NH, 1]) for n in "kq"}
        q_rows = per("q_rows", [128, NH, D])
        beta = sb("beta", [C, LANES, NH, 1])
        kb = per("kb", [128, NH, D])
        k_t = per("k_t", [128, NP, 128])
        lane_a = sb("lane_a", [2 * LANES_OF, BLOCK, BLOCK])
        lane_x = sb("lane_x", [2 * LANES_OF, BLOCK // 2, BLOCK])
        lane_p = sb("lane_p", [2 * LANES_OF, BLOCK // 2, BLOCK])
        k_rows = both("k_rows", [128, NH, D])
        rhs = both("rhs", [128, NH, D])
        kb_t = both("kb_t", [128, NP, 128])
        q_t = both("q_t", [128, NP, 128])
        qk = both("qk", [128, 2, NP, 128])
        a_t = [sb(f"a_t{parity}", [128, LANES, 2, NP, 128]) for parity in range(2)]
        x_t = sb("x_t", [128, LANES, 2, NP, BLOCK])
        u_new = per("u_new", [128, NH, D])
        state = sb("state", [128, NP, D])
        out_t = sb("out_t", [128, NP, L])
        bank = ctx.enter_context(nc.psum_tensor(f"{tag}_p", [128, 8, 512], F32))
        a_dram = nc.dram_tensor(f"{tag}_a_dram", (NB, LANES * NH, BLOCK, BLOCK), F32).ap()
        x_dram = nc.dram_tensor(f"{tag}_x_dram", (NB, LANES * NH, BLOCK, BLOCK), F32).ap()
        heads = lambda ap: ap.rearrange("p (h d) -> p h d", h=NH)
        pairs = lambda ap: ap.rearrange("p (n c) -> p n c", n=NP)
        half = lambda r: slice(64 * r, 64 * r + 64)
        rows_of = lambda g: slice(BLOCK * g, BLOCK * g + BLOCK)

        SOLVE, JOIN, OUT, PROJECT = 0, 1, 2, 1
        PROJ_K, PROJ_V, PROJ_Q, BETA = (4, 5), (7, 3), (3, 4), 6
        TURN_K, TURN_KB, TURN_Q = (4, 5), (6, 7), (3, 4)
        SUM_A, SUM_QK = (4, 6), ((6, 7), (5, 3))

        loaded, cleared = sem("loaded"), sem("cleared")
        s = {n: sem(n) for n in (
            "copied", "proj_k", "proj_q", "proj_v", "proj_beta", "top_k", "top_q", "shift_k", "shift_q",
            "exp_k", "exp_q", "total_k", "total_q", "recip_k", "recip_q", "rows_k", "rows_q",
            "beta_exp", "beta_one", "beta", "kb", "rhs", "turn_k", "turn_q", "turn_kb", "k_t", "q_t",
            "kb_t", "a_sum", "a_t", "qk_sum", "qk_even", "qk_copied", "qk_odd",
            "a_out", "a_in", "unit", "inverted_row", "x_out", "x_in",
            *(f"solve_sum{g}" for g in range(NB)), *(f"solved{g}" for g in range(NB)),
            *(f"join_sum{g}" for g in range(1, NB)), *(f"joined{g}" for g in range(1, NB)),
            "state_sum", "state", "carried_sum", "carried", "out_sum", "out_t", "projected", "added")}
        product = [sem(f"product{j}") for j in range(BLOCK - 1)]
        block = ctx.enter_context(nc.Block())
        N_LOADED = 48

        def stages(eng, stage):
            stage(0, 0, True, False)
            with eng.Fori(0, (B - 2) // 2) as step:
                first = step * 2
                stage(first + 1, 1, True, True)
                stage(first + 2, 0, True, True)
            stage(B - 1, (B - 1) % 2, True, True)
            stage(B, B % 2, False, True)

        @block.sync
        def _(sp):
            for dst, src in ((w[:, :], f"slow_w{layer}"), (w_out[:, :, :], f"fw_out{layer}"),
                             (masks[:, :], "masks")):
                sp.dma_start(dst, k.ins[src]).then_inc(loaded, 16)
            lanes_of = lambda f: slice(f * LANES_OF, (f + 1) * LANES_OF)

            def stage(b, par, prepares, finishes):
                if not prepares:
                    return
                chunks_ready, steps_before = b * 2 + 2, b * (BLOCK - 1)
                steps_done, a_written, x_written = steps_before + (BLOCK - 1), b * (16 * NB) + 16 * NB, b * 32 + 32
                solved_before = b * 2
                work_out(sp, chunks_ready, steps_before, steps_done, a_written, x_written, solved_before)
                sp.wait_ge(s["a_t"], chunks_ready)
                for g in range(NB):
                    sp.dma_start(a_dram[g].rearrange("n j i -> j n i"),
                                 a_t[par][rows_of(g), :, :, :, rows_of(g)].rearrange("j u r p i -> j (u r p) i"))\
                        .then_inc(s["a_out"], 16)
                sp.wait_ge(s["a_out"], a_written)
                sp.wait_ge(s["inverted_row"], steps_before)
                for f in range(2):
                    sp.dma_start(lane_a[lanes_of(f)], a_dram.rearrange("g n j i -> (g n) j i"))\
                        .then_inc(s["a_in"], 16)
                sp.wait_ge(s["inverted_row"], steps_done)
                for f in range(2):
                    sp.dma_start(x_dram.rearrange("g n (c f) i -> f (g n) c i", f=2)[f],
                                 lane_x[lanes_of(f)]).then_inc(s["x_out"], 16)
                sp.wait_ge(s["x_out"], x_written)
                sp.wait_ge(s[f"solve_sum{NB - 1}"], solved_before)
                for g in range(NB):
                    sp.dma_start(x_t[rows_of(g)].rearrange("c u r p i -> c (u r p) i"),
                                 x_dram[g].rearrange("n c i -> c n i")).then_inc(s["x_in"], 16)

            stages(sp, stage)
            sp.wait_ge(s["x_in"], B * 16 * NB)

        @block.gpsimd
        def _(pool):
            for u in chunks:
                for t in (k_rows[0][u], k_rows[1][u], q_rows[u], kb[u], rhs[0][u], rhs[1][u]):
                    ins = pool.memset(t[:, :, :], 0.0)
            ins.then_inc(cleared, 1)
            pool.wait_ge(cleared, 1)
            pool.wait_ge(loaded, N_LOADED)
            pool.tensor_copy(xs[:, :], k.xn[:, cols(0, L)]).then_inc(s["copied"], 1)
            wide = lambda ap: ap.to_broadcast([C, NH, D])

            def stage(b, par, prepares, finishes):
                if not prepares:
                    return
                c = b * 2
                x_left = b * 32
                work_out(pool, x_left)
                pool.wait_ge(cleared, 1)
                pool.wait_ge(s["x_out"], x_left)
                pool.tensor_copy(lane_x[:, :, :].rearrange("p c i -> p (c i)"), unit).then_inc(s["unit"], 1)
                for u in chunks:
                    pool.wait_ge(s["recip_k"], c + u + 1)
                    pool.tensor_tensor(k_rows[par][u][0:C], k_rows[par][u][0:C], wide(total["k"][u][:, :, :]),
                                       ALU.mult).then_inc(s["rows_k"], 1)
                    pool.wait_ge(s["rows_k"], c + u + 1)
                    pool.wait_ge(s["beta"], b + 1)
                    pool.tensor_tensor(kb[u][0:C], k_rows[par][u][0:C], wide(beta[:, u]), ALU.mult)\
                        .then_inc(s["kb"], 1)
                for u in chunks:
                    pool.wait_ge(s["recip_q"], c + u + 1)
                    pool.tensor_tensor(q_rows[u][0:C], q_rows[u][0:C], wide(total["q"][u][:, :, :]), ALU.mult)\
                        .then_inc(s["rows_q"], 1)
                if not (isinstance(b, int) and b == B - 1):
                    pool.wait_ge(s["proj_q"], c + 2)
                    pool.tensor_copy(xs[:, :], k.xn[:, cols(b + 1, L)]).then_inc(s["copied"], 1)
                for u in chunks:
                    pool.wait_ge(s["qk_copied"], c + u + 1)
                    pool.tensor_tensor(qk[par][u][:, 1], qk[par][u][:, 1],
                                       lower.to_broadcast([128, NP, 128]), ALU.mult).then_inc(s["qk_odd"], 1)

            stages(pool, stage)

        @block.tensor
        def _(pe):
            pe.wait_ge(loaded, N_LOADED)
            pe.wait_ge(cleared, 1)

            def settle():
                pe.wait_ge(loaded, N_LOADED)

            def stage(b, par, prepares, finishes):
                c = b * 2
                done = par ^ 1
                if finishes:
                    upto = (c - 1, c)
                    x_ready, batches_before = b * (16 * NB), b - 1
                    work_out(pe, *upto, x_ready, batches_before)

                def project(name, u, bk, free, count):
                    if not prepares:
                        return
                    at, n = {"k": (NH * D, NH * D), "q": (0, NH * D), "v": (2 * NH * D, NH * D),
                             "beta": (3 * NH * D, NH)}[name]
                    if name == "k":
                        pe.wait_ge(s["copied"], b + 1)
                    pe.wait_ge(s[free], count)
                    pe.matmul(bank[0:C, bk, u * NH:u * NH + n] if name == "beta" else bank[0:C, bk, 0:n],
                              xs[:, u * C:(u + 1) * C], w[:, at:at + n],
                              start=True, stop=True).then_inc(s["proj_" + name], 1)

                def turn(name, u, src, bk, ready, free, count):
                    if not prepares:
                        return
                    pe.wait_ge(s[free], count)
                    pe.wait_ge(s[ready], c + u + 1)
                    for p in range(NP):
                        mm = pe.transpose(bank[:, bk, p * 128:(p + 1) * 128], src[:, 2 * p:2 * p + 2, :], k.ident)
                    mm.then_inc(s["turn_" + name], 1)

                def sum_a(u):
                    if not prepares:
                        return
                    settle()
                    if u == 0:
                        pe.wait_ge(s["k_t"], c + 2)
                    pe.wait_ge(s["kb_t"], c + (1 if u == 0 else 2))
                    for p in range(NP):
                        for r in range(2):
                            mm = pe.matmul(bank[:, SUM_A[u] + r, p * 128:(p + 1) * 128], k_t[u][half(r), p, :],
                                           kb_t[par][u][half(r), p, :], start=True, stop=True)
                    mm.then_inc(s["a_sum"], 1)

                def sum_qk(u):
                    if not prepares:
                        return
                    settle()
                    pe.wait_ge(s["a_t"], c + 2)
                    pe.wait_ge(s["q_t"], c + u + 1)
                    for p in range(NP):
                        for r in range(2):
                            mm = pe.matmul(bank[:, SUM_QK[u][r], p * 128:(p + 1) * 128], k_t[u][half(r), p, :],
                                           q_t[par][u][half(r), p, :], start=True, stop=True)
                    mm.then_inc(s["qk_sum"], 1)

                def solve(u, g):
                    if not finishes:
                        return
                    settle()
                    if u == 0 and g == 0:
                        pe.wait_ge(s["x_in"], x_ready)
                        pe.wait_ge(s["rhs"], c)
                        pe.wait_ge(s["added"], batches_before)
                    elif g == 0:
                        pe.wait_ge(s["carried"], b)
                    else:
                        pe.wait_ge(s[f"joined{g}"], upto[u])
                    for h in range(NH):
                        mm = pe.matmul(bank[rows_of(g), SOLVE, h * D:(h + 1) * D],
                                       x_t[rows_of(g), u, h % 2, h // 2, :], rhs[done][u][rows_of(g), h, :],
                                       start=True, stop=True, tile_position=(BLOCK * g, BLOCK * g))
                    mm.then_inc(s[f"solve_sum{g}"], 1)

                def join(u, g):
                    if not finishes:
                        return
                    settle()
                    pe.wait_ge(s[f"solved{g - 1}"], upto[u])
                    above = slice(0, BLOCK * g)
                    for h in range(NH):
                        mm = pe.matmul(bank[rows_of(g), JOIN, h * D:(h + 1) * D],
                                       a_t[done][above, u, h % 2, h // 2, rows_of(g)], u_new[u][above, h, :],
                                       start=True, stop=True, tile_position=(0, BLOCK * g))
                    mm.then_inc(s[f"join_sum{g}"], 1)

                def next_state():
                    if not finishes:
                        return
                    settle()
                    pe.wait_ge(s[f"solved{NB - 1}"], upto[0])
                    for h in range(NH):
                        p, r = divmod(h, 2)
                        mm = pe.matmul(bank[half(r), SOLVE, p * D:(p + 1) * D], k_rows[done][0][:, h, :],
                                       u_new[0][:, h, :], start=True, stop=True)
                    mm.then_inc(s["state_sum"], 1)

                def carry():
                    if not finishes:
                        return
                    settle()
                    pe.wait_ge(s["state"], b)
                    for p in range(NP):
                        for r in range(2):
                            mm = pe.matmul(bank[:, (SOLVE, JOIN)[r], p * D:(p + 1) * D], kb_t[done][1][half(r), p, :],
                                           state[half(r), p, :], start=True, stop=True)
                    mm.then_inc(s["carried_sum"], 1)

                def outputs(u):
                    if not finishes:
                        return
                    settle()
                    pe.wait_ge(s["qk_even"], upto[u])
                    pe.wait_ge(s["qk_odd"], upto[u])
                    if u == 1:
                        pe.wait_ge(s[f"solved{NB - 1}"], c)
                        pe.wait_ge(s["out_t"], upto[0])
                    for h in range(NH):
                        p, r = divmod(h, 2)
                        dst = bank[half(r), OUT, p * 128:(p + 1) * 128]
                        mm = pe.matmul(dst, u_new[u][:, h, :], qk[done][u][:, r, p, :], start=True, stop=u == 0)
                        if u == 1:
                            mm = pe.matmul(dst, state[half(r), p, :], q_t[done][1][half(r), p, :],
                                           start=False, stop=True)
                    mm.then_inc(s["out_sum"], 1)

                def project_out():
                    if not finishes:
                        return
                    pe.wait_ge(s["out_t"], c)
                    for p in range(NP):
                        mm = pe.matmul(bank[:, PROJECT, 0:L], w_out[:, p, :], out_t[:, p, :],
                                       start=p == 0, stop=p == NP - 1)
                    mm.then_inc(s["projected"], 1)

                project("k", 0, PROJ_K[0], "qk_even", c)
                project("k", 1, PROJ_K[1], "qk_copied", c)
                project("beta", 0, BETA, "qk_even", c)
                project("beta", 1, BETA, "qk_even", c)
                solve(0, 0)
                project("v", 0, PROJ_V[0], "qk_copied", c)
                join(0, 1)
                project("v", 1, PROJ_V[1], "qk_copied", c)
                solve(0, 1)
                join(0, 2)
                solve(0, 2)
                turn("k", 0, k_rows[par][0], TURN_K[0], "rows_k", "shift_k", c + 1)
                join(0, 3)
                turn("k", 1, k_rows[par][1], TURN_K[1], "rows_k", "shift_k", c + 2)
                solve(0, 3)
                turn("kb", 0, kb[0], TURN_KB[0], "kb", "beta_exp", b + 1)
                next_state()
                outputs(0)
                turn("kb", 1, kb[1], TURN_KB[1], "kb", "rhs", c + 1)
                carry()
                project("q", 0, PROJ_Q[0], "rhs", c + 2)
                sum_a(0)
                solve(1, 0)
                sum_a(1)
                join(1, 1)
                project("q", 1, PROJ_Q[1], "a_t", c + 1)
                solve(1, 1)
                turn("q", 0, q_rows[0], TURN_Q[0], "rows_q", "shift_q", c + 1)
                join(1, 2)
                solve(1, 2)
                sum_qk(0)
                join(1, 3)
                turn("q", 1, q_rows[1], TURN_Q[1], "rows_q", "shift_q", c + 2)
                solve(1, 3)
                sum_qk(1)
                outputs(1)
                project_out()

            stages(pe, stage)

        @block.scalar
        def _(act):
            load_exp_ln(act)

            def stage(b, par, prepares, finishes):
                c = b * 2

                def exp(name, u, rows):
                    if prepares:
                        act.wait_ge(s["shift_" + name], c + u + 1)
                        act.activation(rows[0:C], rows[0:C], ACT.Exp).then_inc(s["exp_" + name], 1)

                def turned(name, u, bk, dst):
                    if prepares:
                        act.wait_ge(s["turn_" + name], c + u + 1)
                        act.activation(dst[:, :, :], pairs(bank[:, bk, :]), ACT.Copy).then_inc(s[name + "_t"], 1)

                def copy_a(u):
                    if prepares:
                        act.wait_ge(s["a_sum"], c + u + 1)
                        act.activation(a_t[par][:, u].rearrange("j r p i -> j r (p i)"),
                                       bank[:, SUM_A[u]:SUM_A[u] + 2, :], ACT.Copy).then_inc(s["a_t"], 1)

                def copy_qk(u):
                    if prepares:
                        act.wait_ge(s["qk_sum"], c + u + 1)
                        act.activation(qk[par][u][:, 1], pairs(bank[:, SUM_QK[u][1], :]), ACT.Copy)\
                            .then_inc(s["qk_copied"], 1)

                def solved(u, g):
                    if finishes:
                        act.wait_ge(s[f"solve_sum{g}"], c - 1 + u)
                        act.activation(u_new[u][rows_of(g)], heads(bank[rows_of(g), SOLVE, :]), ACT.Copy)\
                            .then_inc(s[f"solved{g}"], 1)

                def outputs(u):
                    if finishes:
                        act.wait_ge(s["out_sum"], c - 1 + u)
                        act.wait_ge(s["projected"], b - 1)
                        act.activation(out_t[:, :, u * C:(u + 1) * C], pairs(bank[:, OUT, :])[:, :, 0:C],
                                       ACT.Copy).then_inc(s["out_t"], 1)

                if prepares:
                    act.wait_ge(s["proj_beta"], c + 2)
                    act.activation(beta[:, :, :, 0], bank[0:C, BETA, 0:LANES * NH].rearrange("p (u h) -> p u h", u=LANES),
                                   ACT.Exp, scale=-1.0).then_inc(s["beta_exp"], 1)
                solved(0, 0)
                exp("k", 0, k_rows[par][0])
                exp("k", 1, k_rows[par][1])
                solved(0, 1)
                solved(0, 2)
                turned("k", 0, TURN_K[0], k_t[0])
                solved(0, 3)
                turned("k", 1, TURN_K[1], k_t[1])
                turned("kb", 0, TURN_KB[0], kb_t[par][0])
                if finishes:
                    act.wait_ge(s["state_sum"], b)
                    act.activation(state[:, :, :], bank[:, SOLVE, 0:NP * D].rearrange("p (n d) -> p n d", n=NP),
                                   ACT.Copy).then_inc(s["state"], 1)
                turned("kb", 1, TURN_KB[1], kb_t[par][1])
                outputs(0)
                copy_a(0)
                solved(1, 0)
                copy_a(1)
                exp("q", 0, q_rows[0])
                solved(1, 1)
                turned("q", 0, TURN_Q[0], q_t[par][0])
                exp("q", 1, q_rows[1])
                solved(1, 2)
                copy_qk(0)
                turned("q", 1, TURN_Q[1], q_t[par][1])
                solved(1, 3)
                copy_qk(1)
                outputs(1)

            stages(act, stage)

        @block.vector
        def _(dve):
            dve.wait_ge(loaded, N_LOADED)
            dve.wait_ge(cleared, 1)
            wide = lambda ap: ap.to_broadcast([C, NH, D])

            def stage(b, par, prepares, finishes):
                c = b * 2
                done = par ^ 1
                bank_of = {"k": PROJ_K, "q": PROJ_Q}
                rows = {"k": k_rows[par], "q": q_rows}

                def maximum(n, u):
                    if prepares:
                        dve.wait_ge(s["proj_" + n], c + u + 1)
                        dve.tensor_reduce(top[n][u][:, :, :], heads(bank[0:C, bank_of[n][u], :]), AX, ALU.max)\
                            .then_inc(s["top_" + n], 1)

                def shift(n, u):
                    if prepares:
                        dve.wait_ge(s["top_" + n], c + u + 1)
                        dve.tensor_tensor(rows[n][u][0:C], heads(bank[0:C, bank_of[n][u], :]),
                                          wide(top[n][u][:, :, :]), ALU.subtract).then_inc(s["shift_" + n], 1)

                def sums(n, u):
                    if prepares:
                        dve.wait_ge(s["exp_" + n], c + u + 1)
                        dve.tensor_reduce(total[n][u][:, :, :], rows[n][u][0:C], AX, ALU.add)\
                            .then_inc(s["total_" + n], 1)

                def inverse_sums(n, u):
                    if prepares:
                        dve.wait_ge(s["total_" + n], c + u + 1)
                        dve.reciprocal(total[n][u][:, :, :], total[n][u][:, :, :]).then_inc(s["recip_" + n], 1)

                def right_hand_side(u):
                    if prepares:
                        dve.wait_ge(s["proj_v"], c + u + 1)
                        dve.tensor_tensor(rhs[par][u][0:C], heads(bank[0:C, PROJ_V[u], :]), wide(beta[:, u]), ALU.mult)\
                            .then_inc(s["rhs"], 1)

                def joined(u, g):
                    if finishes:
                        at = rhs[done][u][rows_of(g)]
                        dve.wait_ge(s[f"join_sum{g}"], c - 1 + u)
                        dve.tensor_tensor(at, at, heads(bank[rows_of(g), JOIN, :]), ALU.subtract)\
                            .then_inc(s[f"joined{g}"], 1)

                def mask_qk(u):
                    if prepares:
                        dve.wait_ge(s["qk_sum"], c + u + 1)
                        dve.tensor_tensor(qk[par][u][:, 0], pairs(bank[:, SUM_QK[u][0], :]),
                                          lower.to_broadcast([128, NP, 128]), ALU.mult).then_inc(s["qk_even"], 1)

                def invert(start, stop):
                    if not prepares:
                        return
                    for j in range(start, stop):
                        shape = [2 * LANES_OF, j // 2 + 1, BLOCK - 1 - j]
                        if j == 0:
                            dve.wait_ge(s["a_in"], b * 32 + 32)
                            dve.wait_ge(s["unit"], b + 1)
                        else:
                            dve.wait_ge(s["inverted_row"], b * (BLOCK - 1) + j)
                        below = lane_x[:, 0:shape[1], j + 1:BLOCK]
                        p = lane_p[:, 0:shape[1], 0:shape[2]]
                        dve.tensor_tensor(p, lane_a[:, j:j + 1, j + 1:BLOCK].to_broadcast(shape),
                                          lane_x[:, 0:shape[1], j:j + 1].to_broadcast(shape), ALU.mult)\
                            .then_inc(product[j], 1)
                        dve.wait_ge(product[j], b + 1)
                        dve.tensor_tensor(below, below, p, ALU.subtract).then_inc(s["inverted_row"], 1)

                maximum("k", 0)
                maximum("k", 1)
                shift("k", 0)
                shift("k", 1)
                joined(0, 1)
                if prepares:
                    dve.wait_ge(s["beta_exp"], b + 1)
                    dve.tensor_scalar(beta[:, :, :, :], beta[:, :, :, :], 1.0, None, ALU.add)\
                        .then_inc(s["beta_one"], 1)
                sums("k", 0)
                if prepares:
                    dve.wait_ge(s["beta_one"], b + 1)
                    dve.reciprocal(beta[:, :, :, :], beta[:, :, :, :]).then_inc(s["beta"], 1)
                inverse_sums("k", 0)
                joined(0, 2)
                sums("k", 1)
                if prepares:
                    dve.wait_ge(s["beta"], b + 1)
                right_hand_side(0)
                inverse_sums("k", 1)
                joined(0, 3)
                right_hand_side(1)
                if finishes:
                    v = rhs[done][1][:, :, :].rearrange("p (n r) d -> p r n d", r=2)
                    dve.wait_ge(s["carried_sum"], b)
                    dve.tensor_tensor(v, v, bank[:, 0:2, 0:NP * D].rearrange("p r (n d) -> p r n d", n=NP),
                                      ALU.subtract).then_inc(s["carried"], 1)
                maximum("q", 0)
                shift("q", 0)
                joined(1, 1)
                sums("q", 0)
                maximum("q", 1)
                inverse_sums("q", 0)
                shift("q", 1)
                joined(1, 2)
                invert(0, 4)
                sums("q", 1)
                inverse_sums("q", 1)
                mask_qk(0)
                invert(4, 8)
                joined(1, 3)
                invert(8, 16)
                mask_qk(1)
                invert(16, BLOCK - 1)
                if finishes:
                    f = b - 1
                    dve.wait_ge(s["projected"], b)
                    r_at = k.r[:, cols(f, L)]
                    dve.tensor_tensor(r_at, bank[:, PROJECT, 0:L], r_at, ALU.add).then_inc(s["added"], 1)

            stages(dve, stage)
            if layer == 1:
                dve.wait_ge(s["added"], B)
                dve.tensor_tensor(k.h[:, :], k.h[:, :], k.r[:, :], ALU.add)


MASK_COLS = 128 + 16 * 32


def delta_masks():
    m = np.zeros((128, MASK_COLS), np.float32)
    m[:, 0:128] = np.arange(128)[:, None] <= np.arange(128)[None, :]
    for odd in range(2):
        m[64 * odd:64 * odd + 64, 128:] = np.eye(32, dtype=np.float32)[odd::2].reshape(-1)
    return m



def experts1(k):
    router(k, "route1", "gate_w", None, scores=True)
    nc = k.nc
    with ExitStack() as ctx:
        def sb(name, shape, dt=F32):
            return ctx.enter_context(nc.sbuf_tensor(f"ex1_{name}", shape, dt))

        def sem(name):
            return k.semaphore(ctx, f"ex1_{name}")

        w1, w2, sw1, sw2 = sb("w1", [H, E, H]), sb("w2", [H, E, H]), sb("sw1", [H, H]), sb("sw2", [H, H])
        b2, vec = sb("b2", [E, H]), sb("vec", [H, E + 2])
        relu = [sb(f"relu{n}", [H, W2]) for n in range(2)]
        weighted = [sb(f"weighted{n}", [H, W2]) for n in range(2)]
        shared = sb("shared", [H, W2])
        psum = lambda n: ctx.enter_context(nc.psum_tensor(f"ex1_{n}", [128, 512], F32))
        hidden, weight = [psum("hidden0"), psum("hidden1")], [psum("weight0"), psum("weight1")]
        hidden_shared, total = psum("hidden_shared"), psum("total")
        loaded = sem("loaded")
        s = {n: sem(n) for n in ("hidden", "spread", "relu", "weighted", "summed", "shared_in",
                                 "shared", "total", "added")}
        block = ctx.enter_context(nc.Block())

        @block.sync
        def _(sp):
            for dst, src in ((w1[:, :, :], "w1"), (w2[:, :, :], "w2"), (sw1[:, :], "sw1"),
                             (sw2[:, :], "sw2"), (b2[:, :], "b2"), (vec[:, :], "ffn1_vec")):
                sp.dma_start(dst, k.ins[src]).then_inc(loaded, 16)

        @block.tensor
        def _(pe):
            pe.wait_ge(loaded, 16 * 6)
            with pe.Fori(0, NT) as t:
                done = t * E
                x = k.xn[:, cols(t, W2)]

                def second(e):
                    pe.wait_ge(s["weighted"], done + e + 1)
                    pe.matmul(total[:, 0:W2], w2[:, e, :], weighted[e % 2][:, :], start=False,
                              stop=False).then_inc(s["summed"], 1)

                pe.wait_ge(s["shared"], t)
                pe.matmul(hidden_shared[:, 0:W2], sw1[:, :], x, start=True, stop=True)\
                    .then_inc(s["shared_in"], 1)
                for e in range(E):
                    if e >= 2:
                        pe.wait_ge(s["relu"], done + e - 1)
                        pe.wait_ge(s["weighted"], done + e - 1)
                    elif e == 0:
                        pe.wait_ge(s["weighted"], done)
                    pe.matmul(hidden[e % 2][:, 0:W2], w1[:, e, :], x, start=True, stop=True)\
                        .then_inc(s["hidden"], 1)
                    pe.matmul(weight[e % 2][:, 0:W2], k.select[:, e:e + 1].to_broadcast([128, 128]),
                              k.wt_parts[:, cols(t, W2)], start=True, stop=True).then_inc(s["spread"], 1)
                    if e == 0:
                        pe.wait_ge(s["added"], t)
                        pe.matmul(total[:, 0:W2], b2[:, :], k.wt[:, cols(t, W2)], start=True, stop=False)
                    else:
                        second(e - 1)
                second(E - 1)
                pe.wait_ge(s["shared"], t + 1)
                pe.matmul(total[:, 0:W2], sw2[:, :], shared[:, :], start=False, stop=True)\
                    .then_inc(s["total"], 1)

        @block.scalar
        def _(act):
            act.wait_ge(loaded, 16 * 6)
            with act.Fori(0, NT) as t:
                done = t * E
                act.wait_ge(s["shared_in"], t + 1)
                act.wait_ge(s["total"], t)
                act.activation(shared[:, :], hidden_shared[:, 0:W2], ACT.Relu, bias=vec[:, E:E + 1])\
                    .then_inc(s["shared"], 1)
                for e in range(E):
                    act.wait_ge(s["hidden"], done + e + 1)
                    if e >= 2:
                        act.wait_ge(s["weighted"], done + e - 1)
                    act.activation(relu[e % 2][:, :], hidden[e % 2][:, 0:W2], ACT.Relu,
                                   bias=vec[:, e:e + 1]).then_inc(s["relu"], 1)

        @block.vector
        def _(dve):
            dve.wait_ge(loaded, 16 * 6)
            with dve.Fori(0, NT) as t:
                done = t * E
                for e in range(E):
                    dve.wait_ge(s["relu"], done + e + 1)
                    dve.wait_ge(s["spread"], done + e + 1)
                    if e >= 2:
                        dve.wait_ge(s["summed"], done + e - 1)
                    dve.tensor_tensor(weighted[e % 2][:, :], relu[e % 2][:, :], weight[e % 2][:, 0:W2],
                                      ALU.mult).then_inc(s["weighted"], 1)
                dve.wait_ge(s["total"], t + 1)
                dve.scalar_tensor_tensor(k.h[:, cols(t, W2)], total[:, 0:W2], vec[:, E + 1:E + 2],
                                         k.h[:, cols(t, W2)], ALU.add, ALU.add).then_inc(s["added"], 1)



def store(k):
    nc = k.nc
    with ExitStack() as ctx:
        stored = k.semaphore(ctx, "stored")
        block = ctx.enter_context(nc.Block())

        @block.sync
        def _(sp):
            sp.dma_start(k.out, k.h[:, :]).then_inc(stored, 16)
            sp.wait_ge(stored, 16)


PHASES = [setup, token_mixer, attention0, block_norm, experts0, block_norm, attention1,
          block_norm, experts1, store]


def build(nc, ins, out, phases=None):
    k = Kit(nc, ins, out)
    with ExitStack() as ctx:
        k.h = ctx.enter_context(nc.sbuf_tensor("h", [H, T], F32))
        k.xn = ctx.enter_context(nc.sbuf_tensor("xn", [H, T], F32))
        k.wt = ctx.enter_context(nc.sbuf_tensor("wt", [E, T], F32))
        k.wt_parts = ctx.enter_context(nc.sbuf_tensor("wt_parts", [128, T], BF16))
        k.select = ctx.enter_context(nc.sbuf_tensor("select", [128, 32], BF16))
        k.const = ctx.enter_context(nc.sbuf_tensor("const", [128, CONST_COLS], F32))
        k.ident = k.const[:, 0:128]
        k.centre = k.const[:, 128:256]
        k.average = k.const[:, 256:384]
        k.eps = k.const[:, 384:385]
        for phase in phases or PHASES:
            phase(k)


CONST_COLS = 385 + 32 + 8


def constants():
    c = np.zeros((128, CONST_COLS), np.float32)
    c[:, 0:128] = np.eye(128)
    c[:, 128:256] = np.eye(128) - 1.0 / H
    c[:, 256:384] = 1.0 / H
    c[:, 384] = EPS
    for r in range(32):
        for part in PARTS:
            c[part + r, 385 + r] = 1.0
    c[:, 417:425] = np.arange(E)
    return c


def columns(*vectors):
    out = np.zeros((128, len(vectors)), np.float32)
    for n, v in enumerate(vectors):
        out[:len(v), n] = v
    return out


def layout(p):
    t = lambda a: np.ascontiguousarray(a)
    a = {"const": constants()}
    a["x"] = t(p["x"].transpose(2, 0, 1).reshape(H, B * S))
    a["w_compress"] = t(p["L0_tok_w_compress"][:, :, 0].T)
    a["w_main"] = np.zeros((BN, 3, H), np.float32)
    a["w_main"][:, :, :BN] = p["L0_tok_w_main"].transpose(1, 2, 0)
    a["w_expand"] = t(p["L0_tok_w_expand"][:, :, 0].T)
    a["tok_up"] = t(p["L0_tok_w_ff1"].T)
    a["tok_down"] = t(p["L0_tok_w_ff2"].T)
    a["tok_vec"] = columns(*(p["L0_tok_" + n] for n in (
        "b_compress", "b_main", "b_ff1", "b_expand", "b_ff2", "g_conv_norm", "b_conv_norm",
        "g_ff_norm", "b_ff_norm")))
    a["mk"] = t(p["L0_attn_mk_w"].T)
    a["mv"] = t(p["L0_attn_mv_w"])
    a["ea_vec"] = columns(p["L0_attn_ln_g"], p["L0_attn_ln_b"])
    halves = lambda m: t(m.reshape((2, H) + m.shape[1:]).swapaxes(0, 1))
    a["in_proj_x"] = halves(p["L0_attn_in_proj_w"][:DI])
    a["in_proj_z"] = t(p["L0_attn_in_proj_w"][DI:].T.reshape(H, 2, H))
    a["conv_w"] = halves(p["L0_attn_conv_w"])
    x_proj = halves(p["L0_attn_x_proj_w"].T)
    a["x_proj_dt"] = t(x_proj[:, :, :DR])
    a["x_proj_bc"] = np.zeros((H, 2, 128), np.float32)
    for at in PARTS:
        a["x_proj_bc"][:, :, at:at + 2 * DS] = x_proj[:, :, DR:]
    a["dt_proj"] = t(p["L0_attn_dt_proj_w"].T.reshape(DR, 2, H))
    a["out_proj"] = halves(p["L0_attn_out_proj_w"].T)
    a["mamba_vec"] = halves(np.stack([p["L0_attn_" + n] for n in ("conv_b", "dt_proj_b", "D")], 1))
    a["a_log"] = halves(p["L0_attn_A_log"])
    a["router_w"] = t(p["L0_ffn_router_w"])
    a["router_b"] = t(np.broadcast_to(p["L0_ffn_router_b"], (C, E)))
    a["gate_up"] = t(p["L0_ffn_gate_up_proj"].transpose(1, 0, 2))
    a["gate_up_bias"] = t(p["L0_ffn_gate_up_proj_bias"].reshape(E, 4, H).transpose(2, 0, 1))
    a["down"] = t(p["L0_ffn_down_proj"].reshape(E, 2, H, H).transpose(2, 0, 1, 3))
    a["down_bias"] = t(p["L0_ffn_down_proj_bias"])
    a["masks"] = delta_masks()
    a["ip_w"] = t(p["L1_attn_ip_w"].T)
    a["ip_vec"] = columns(p["L1_attn_ip_b"], p["L1_attn_fw_ln_g"][0], p["L1_attn_fw_ln_b"][0])
    a["ff_w1"] = t(p["L1_attn_ff_w1"].T.reshape(H, FF // H, H))
    a["ff_w2"] = t(p["L1_attn_ff_w2"].T.reshape(FF // H, H, H).transpose(1, 0, 2))
    a["ff_vec"] = columns(p["L1_attn_ff_ln_g"], p["L1_attn_ff_ln_b"], p["L1_attn_fw_ln_g"][1],
                          p["L1_attn_fw_ln_b"][1], p["L1_attn_ff_b2"],
                          *p["L1_attn_ff_b1"].reshape(FF // H, H))
    for n in range(2):
        slow = p["L1_attn_fw_slow_w"][n].reshape(NH, 3 * D + 1, H)
        parts = [slow[:, at:at + m].reshape(NH * m, H) for at, m in ((0, D), (D, D), (2 * D, D), (3 * D, 1))]
        a[f"slow_w{n}"] = t(np.concatenate(parts).T)
        a[f"fw_out{n}"] = t(p["L1_attn_fw_out_w"][n].T.reshape(NH // 2, 2 * D, H).transpose(1, 0, 2))
    a["gate_w"] = t(p["L1_ffn_gate_w"].T)
    a["w1"] = t(p["L1_ffn_w1"].transpose(1, 0, 2))
    a["w2"] = t(p["L1_ffn_w2"].transpose(1, 0, 2))
    a["sw1"] = t(p["L1_ffn_sw1"])
    a["sw2"] = t(p["L1_ffn_sw2"])
    a["b2"] = t(p["L1_ffn_b2"])
    a["ffn1_vec"] = t(np.concatenate([p["L1_ffn_b1"].T, columns(p["L1_ffn_sb1"], p["L1_ffn_sb2"])], 1))
    return a


def kernel(**inputs):
    import concourse.bacc as bacc
    from concourse.bass_utils import run_bass_kernel_spmd

    arrays = layout({n: np.asarray(a) for n, a in inputs.items()})
    nc = bacc.Bacc("TRN2", target_bir_lowering=False, num_devices=1)
    ins = {n: nc.dram_tensor(f"in_{n}", a.shape, mybir.dt.from_np(a.dtype), kind="ExternalInput").ap()
           for n, a in arrays.items()}
    out = nc.dram_tensor("out", (H, T), F32, kind="ExternalOutput").ap()
    build(nc, ins, out)
    r = run_bass_kernel_spmd(nc, [{f"in_{n}": a for n, a in arrays.items()}], core_ids=[0])
    return np.ascontiguousarray(r.results[0]["out"].reshape(H, B, L).transpose(1, 2, 0))
```

```python
from contextlib import ExitStack

import numpy as np

import concourse.bass as bass
from concourse import mybir

F32 = mybir.dt.float32
U32 = mybir.dt.uint32
BF16 = mybir.dt.bfloat16
ALU = mybir.AluOpType
ACT = mybir.ActivationFunctionType
AX = mybir.AxisListType.X

B, S, H = 16, 256, 128
L = S - 2
T = B * L
W2 = 2 * L
NT = B // 2
C = L // 2
BN = H // 2
E = 8
I0 = 256
DI = 2 * H
DS = 16
DR = 8
NH, D = 8, 64
FF = 512
EPS = 1e-5
LANES = 2
WIDE = 4
WHOLE = 32
PARTS = (0, 64, 96)


class Kit:

    def __init__(self, nc, ins, out):
        self.nc, self.ins, self.out = nc, ins, out
        self.norms = 0
        self.to_load, self.lasting = [], []

    def semaphore(self, phase, name):
        if self.phase is not phase:
            self.phase, mine = phase, []
            self.phase_semaphores = mine
            phase.callback(self.end_phase, mine)
        self.phase_semaphores.append(self.nc.alloc_semaphore(name))
        return self.phase_semaphores[-1]

    def ahead(self, ctx, tag, tiles):
        semaphore = self.nc.alloc_semaphore(f"{tag}_loaded")
        self.lasting.append(semaphore)
        made = [ctx.enter_context(self.nc.sbuf_tensor(f"{tag}_{name}", shape, F32))
                for name, (shape, _) in tiles.items()]
        self.to_load += [(t, source, semaphore) for t, (_, source) in zip(made, tiles.values())]
        return made, semaphore

    def load_ahead(self, sp):
        for tile, source, semaphore in self.to_load:
            sp.dma_start(tile[tuple(slice(None) for _ in tile.shape)], self.ins[source]).then_inc(semaphore, 16)
        self.to_load = []

    def end_phase(self, semaphores):
        self.nc.clear_and_free_semaphores(semaphores)
        self.nc.all_engine_barrier()

    phase = None


LN_STAGES = ("centred", "squares", "var", "log", "scale", "scaled")
EXP_AND_LN = 6


def load_exp_ln(act):
    act.add_instruction(mybir.InstLoadActFuncSet(
        name=act.bass.get_next_instruction_name(), engine=mybir.EngineType.Activation,
        act_func_set_id=EXP_AND_LN))


def work_out(engine, *counts):
    for count in counts:
        if not isinstance(count, int):
            engine.to_reg(count)


def cols(t, width):
    return bass.ds(t * width, width)



def token_mixer(k):
    nc = k.nc
    N = 2 * S
    with ExitStack() as ctx:
        def sb(name, shape):
            return ctx.enter_context(nc.sbuf_tensor(name, shape, F32))

        def sem(name):
            return k.semaphore(ctx, name)

        w_compress, w_expand = sb("w_compress", [H, BN]), sb("w_expand", [BN, H])
        w_main = sb("w_main", [BN, 3, H])
        w_up, w_down = sb("tok_up", [H, BN]), sb("tok_down", [BN, H])
        vec = sb("tok_vec", [H, 9])
        b_compress, b_main, b_up = vec[0:BN, 0:1], vec[0:BN, 1:2], vec[0:BN, 2:3]
        b_expand, b_down = vec[:, 3:4], vec[:, 4:5]
        g1, b1, g2, b2 = (vec[:, n:n + 1] for n in range(5, 9))
        x = sb("x_in", [H, B * S])
        lanes = range(WIDE)
        squeezed = [sb(f"squeezed{u}", [BN, 2, S + 2]) for u in lanes]
        mixed = [sb(f"mixed{u}", [BN, N]) for u in lanes]
        summed = [sb(f"summed{u}", [H, N]) for u in lanes]
        squares = [sb(f"squares{u}", [H, N]) for u in lanes]
        scale = [sb(f"scale{u}", [H, N]) for u in lanes]
        normed = [sb(f"normed{u}", [H, N]) for u in lanes]
        second = [sb(f"second{u}", [H, N]) for u in lanes]
        pairmax = [sb(f"pairmax{u}", [H, 2, S - 1]) for u in lanes]
        acc = [[ctx.enter_context(nc.psum_tensor(f"tok_p{u}_{n}", [128, 512], F32)) for n in range(2)]
               for u in lanes]
        loaded, x_loaded, pad_zero = sem("tok_loaded"), sem("x_loaded"), sem("pad_zero")
        names = ["compressed", "squeezed", "convolved", "mixed", "expanded", "summed",
                 "norm1", "up", "gelu", "down", "summed2", "norm2", "affine2", "pairmax", "pooled",
                 "block"]
        s = {n: sem(f"tok_{n}") for n in names}
        ln = [{n: sem(f"tok_ln{j}_{n}") for n in LN_STAGES}
              for j in range(3)]

        block = ctx.enter_context(nc.Block())

        @block.sync
        def _(sp):
            w = k.ins
            for dst, src in ((w_compress[:, :], w["w_compress"]), (w_main[:, :, :], w["w_main"]),
                             (w_expand[:, :], w["w_expand"]), (w_up[:, :], w["tok_up"]),
                             (w_down[:, :], w["tok_down"]), (vec[:, :], w["tok_vec"])):
                sp.dma_start(dst, src).then_inc(loaded, 16)
            for n in range(4):
                sp.dma_start(x[:, n * B * S // 4:(n + 1) * B * S // 4],
                             w["x"][:, n * B * S // 4:(n + 1) * B * S // 4]).then_inc(x_loaded, 16)

        @block.tensor
        def _(pe):
            pe.wait_ge(loaded, 16 * 6)
            pe.wait_ge(x_loaded, 16 * 4)
            pe.wait_ge(pad_zero, 2 * WIDE)
            with pe.Fori(0, NT // WIDE) as step:
                i = step * WIDE
                pe.wait_ge(ln[2]["scaled"], i)
                for u in lanes:
                    pe.matmul(acc[u][0][0:BN, :], w_compress[:, :], x[:, cols(i + u, N)],
                              start=True, stop=True).then_inc(s["compressed"], 1)
                for u in lanes:
                    pe.wait_ge(s["squeezed"], i + u + 1)
                    for tap in range(3):
                        mm = pe.matmul(acc[u][1][:, :], w_main[:, tap, :],
                                       squeezed[u][:, :, tap:tap + S], start=tap == 0, stop=tap == 2)
                    mm.then_inc(s["convolved"], 1)
                for u in lanes:
                    pe.wait_ge(s["mixed"], i + u + 1)
                    pe.matmul(acc[u][0][:, :], w_expand[:, :], mixed[u][:, :],
                              start=True, stop=True).then_inc(s["expanded"], 1)
                norm_pe(pe, k, ln[0], i, summed, s["summed"], squares, acc, 1, 0)
                for u in lanes:
                    pe.wait_ge(s["norm1"], i + u + 1)
                    pe.matmul(acc[u][1][0:BN, :], w_up[:, :], normed[u][:, :],
                              start=True, stop=True).then_inc(s["up"], 1)
                for u in lanes:
                    pe.wait_ge(s["gelu"], i + u + 1)
                    pe.matmul(acc[u][0][:, :], w_down[:, :], mixed[u][:, :],
                              start=True, stop=True).then_inc(s["down"], 1)
                norm_pe(pe, k, ln[1], i, second, s["summed2"], squares, acc, 1, 0)
                norm_pe(pe, k, ln[2], i, [k.h[:, cols(i + u, W2)] for u in lanes], s["pooled"],
                        squares, acc, 1, 0, W2)

        @block.scalar
        def _(act):
            act.wait_ge(loaded, 16 * 6)
            with act.Fori(0, NT // WIDE) as step:
                i = step * WIDE
                for u in lanes:
                    act.wait_ge(s["compressed"], i + u + 1)
                    act.activation(squeezed[u][:, :, 1:S + 1],
                                   acc[u][0][0:BN, :].rearrange("p (b s) -> p b s", b=2),
                                   ACT.Silu, bias=b_compress).then_inc(s["squeezed"], 1)
                for u in lanes:
                    act.wait_ge(s["convolved"], i + u + 1)
                    act.activation(mixed[u][:, :], acc[u][1][0:BN, :], ACT.Silu,
                                   bias=b_main).then_inc(s["mixed"], 1)
                norm_act(act, k, ln[0], i, squares, scale, acc, 1, 0)
                for u in lanes:
                    act.wait_ge(s["up"], i + u + 1)
                    act.activation(mixed[u][:, :], acc[u][1][0:BN, :], ACT.Gelu,
                                   bias=b_up).then_inc(s["gelu"], 1)
                norm_act(act, k, ln[1], i, squares, scale, acc, 1, 0)
                norm_act(act, k, ln[2], i, squares, scale, acc, 1, 0, W2)

        @block.vector
        def _(dve):
            for u in lanes:
                dve.memset(squeezed[u][:, :, 0:1], 0.0).then_inc(pad_zero, 1)
                dve.memset(squeezed[u][:, :, S + 1:S + 2], 0.0).then_inc(pad_zero, 1)
            dve.wait_ge(loaded, 16 * 6)
            dve.wait_ge(x_loaded, 16 * 4)
            with dve.Fori(0, NT // WIDE) as step:
                i = step * WIDE
                for u in lanes:
                    dve.wait_ge(s["expanded"], i + u + 1)
                    dve.scalar_tensor_tensor(summed[u][:, :], acc[u][0][:, :], b_expand,
                                             x[:, cols(i + u, N)], ALU.add, ALU.add)\
                        .then_inc(s["summed"], 1)
                norm_dve(dve, ln[0], i, scale, acc, 1, normed)
                for u in lanes:
                    dve.wait_ge(ln[0]["scaled"], i + u + 1)
                    dve.tensor_scalar(normed[u][:, :], normed[u][:, :], g1, b1, ALU.mult, ALU.add)\
                        .then_inc(s["norm1"], 1)
                for u in lanes:
                    dve.wait_ge(s["down"], i + u + 1)
                    dve.wait_ge(s["norm1"], i + u + 1)
                    dve.scalar_tensor_tensor(second[u][:, :], acc[u][0][:, :], b_down, normed[u][:, :],
                                             ALU.add, ALU.add).then_inc(s["summed2"], 1)
                norm_dve(dve, ln[1], i, scale, acc, 1, second)
                for u in lanes:
                    dve.wait_ge(ln[1]["scaled"], i + u + 1)
                    dve.tensor_scalar(second[u][:, :], second[u][:, :], g2, b2, ALU.mult, ALU.add)\
                        .then_inc(s["affine2"], 1)
                for u in lanes:
                    y = second[u][:, :].rearrange("p (b s) -> p b s", b=2)
                    dve.wait_ge(s["affine2"], i + u + 1)
                    dve.tensor_tensor(pairmax[u][:, :, :], y[:, :, 0:S - 1], y[:, :, 1:S], ALU.max)\
                        .then_inc(s["pairmax"], 1)
                for u in lanes:
                    dve.wait_ge(s["pairmax"], i + u + 1)
                    dve.tensor_tensor(k.h[:, cols(i + u, W2)].rearrange("p (b s) -> p b s", b=2),
                                      pairmax[u][:, :, 0:L], pairmax[u][:, :, 1:L + 1], ALU.max)\
                        .then_inc(s["pooled"], 1)
                norm_dve(dve, ln[2], i, scale, acc, 1, [k.xn[:, cols(i + u, W2)] for u in lanes], W2)



def norm_pe(pe, k, ln, i, source, ready, squares, acc, at, var, n=512):
    for u in range(len(squares)):
        if ready is not None:
            pe.wait_ge(ready, i + u + 1)
        src = source[u] if n != 512 else source[u][:, 0:n]
        pe.matmul(acc[u][at][:, 0:n], k.centre, src, start=True, stop=True).then_inc(ln["centred"], 1)
    for u in range(len(squares)):
        pe.wait_ge(ln["squares"], i + u + 1)
        pe.matmul(acc[u][var][:, 0:n], k.average, squares[u][:, 0:n],
                  start=True, stop=True).then_inc(ln["var"], 1)


def norm_act(act, k, ln, i, squares, scale, acc, at, var, n=512):
    load_exp_ln(act)
    for u in range(len(squares)):
        act.wait_ge(ln["centred"], i + u + 1)
        act.activation(squares[u][:, 0:n], acc[u][at][:, 0:n], ACT.Square).then_inc(ln["squares"], 1)
    for u in range(len(squares)):
        act.wait_ge(ln["var"], i + u + 1)
        act.activation(scale[u][:, 0:n], acc[u][var][:, 0:n], ACT.Ln, bias=k.eps)\
            .then_inc(ln["log"], 1)
    for u in range(len(squares)):
        act.wait_ge(ln["log"], i + u + 1)
        act.activation(scale[u][:, 0:n], scale[u][:, 0:n], ACT.Exp, scale=-0.5)\
            .then_inc(ln["scale"], 1)


def norm_dve(dve, ln, i, scale, acc, at, out, n=512):
    for u in range(len(out)):
        dve.wait_ge(ln["scale"], i + u + 1)
        dst = out[u] if n != 512 else out[u][:, 0:n]
        dve.tensor_tensor(dst, acc[u][at][:, 0:n], scale[u][:, 0:n], ALU.mult).then_inc(ln["scaled"], 1)


def setup(k):
    nc = k.nc
    with ExitStack() as ctx:
        loaded = k.semaphore(ctx, "const_loaded")
        block = ctx.enter_context(nc.Block())

        @block.sync
        def _(sp):
            sp.dma_start(k.const[:, :], k.ins["const"]).then_inc(loaded, 16)

        @block.vector
        def _(dve):
            dve.wait_ge(loaded, 16)
            dve.tensor_copy(k.select[:, :], k.const[:, 385:417])



def block_norm(k):
    nc = k.nc
    name = f"norm{k.norms}"
    k.norms += 1
    with ExitStack() as ctx:
        lanes = range(WIDE)
        squares = [ctx.enter_context(nc.sbuf_tensor(f"{name}_sq{u}", [H, W2], F32)) for u in lanes]
        scale = [ctx.enter_context(nc.sbuf_tensor(f"{name}_scale{u}", [H, W2], F32)) for u in lanes]
        acc = [[ctx.enter_context(nc.psum_tensor(f"{name}_p{u}_{n}", [128, 512], F32)) for n in range(2)]
               for u in lanes]
        ln = {n: k.semaphore(ctx, f"{name}_{n}") for n in LN_STAGES}
        block = ctx.enter_context(nc.Block())

        @block.sync
        def _(sp):
            k.load_ahead(sp)

        @block.tensor
        def _(pe):
            with pe.Fori(0, NT // WIDE) as step:
                i = step * WIDE
                pe.wait_ge(ln["scaled"], i)
                norm_pe(pe, k, ln, i, [k.h[:, cols(i + u, W2)] for u in lanes], None, squares, acc,
                        0, 1, W2)

        @block.scalar
        def _(act):
            with act.Fori(0, NT // WIDE) as step:
                norm_act(act, k, ln, step * WIDE, squares, scale, acc, 0, 1, W2)

        @block.vector
        def _(dve):
            with dve.Fori(0, NT // WIDE) as step:
                i = step * WIDE
                norm_dve(dve, ln, i, scale, acc, 0, [k.xn[:, cols(i + u, W2)] for u in lanes], W2)



def router(k, tag, w, b, loaded, scores):
    nc = k.nc
    NC = T // C
    with ExitStack() as ctx:
        def sb(name, shape, dt=F32):
            return ctx.enter_context(nc.sbuf_tensor(f"{tag}_{name}", shape, dt))

        def sem(name):
            return k.semaphore(ctx, f"{tag}_{name}")

        logits, ex = sb("logits", [C, NC, E]), sb("ex", [C, NC, E])
        best, where = sb("best", [C, NC, E]), sb("where", [C, NC, E], U32)
        index = sb("index", [C, NC, E])
        first, second = sb("first", [C, NC, 1]), sb("second", [C, NC, 1])
        total = sb("total", [C, NC, 1])
        hot = sb("hot", [C, NC, E])
        wide = sb("wide", [C, NC, 128])
        whole, parted = sb("whole", [C, NC, E]), sb("parted", [C, NC, E], BF16)
        raw = ctx.enter_context(nc.psum_tensor(f"{tag}_raw", [128, 512], F32))
        turned = [ctx.enter_context(nc.psum_tensor(f"{tag}_turned{n}", [128, 512], F32)) for n in range(4)]
        projected, chain = sem("projected"), sem("chain")
        shifted, exped, spread, turned_done = sem("shifted"), sem("exped"), sem("spread"), sem("turned")
        kept = sem("kept")
        block = ctx.enter_context(nc.Block())
        n_loaded = 32 if b is not None else 16

        @block.tensor
        def _(pe):
            pe.wait_ge(loaded, n_loaded)
            for c in range(NC):
                mm = pe.matmul(raw[0:C, c * E:(c + 1) * E], k.xn[:, c * C:(c + 1) * C], w[:, :],
                               start=True, stop=True)
            mm.then_inc(projected, 1)
            pe.wait_ge(spread, 1)
            for t in range(NT):
                if t >= 4:
                    pe.wait_ge(kept, 2 * (t - 3))
                for c in range(4):
                    mm = pe.transpose(turned[t % 4][:, c * C:(c + 1) * C], wide[:, 4 * t + c, :],
                                      k.ident[0:C, 0:C])
                mm.then_inc(turned_done, 1)

        @block.scalar
        def _(act):
            load_exp_ln(act)
            act.wait_ge(shifted, 1)
            act.activation(ex[:, :, :], ex[:, :, :], ACT.Exp).then_inc(exped, 1)
            for t in range(NT):
                act.wait_ge(turned_done, t + 1)
                at = slice(t * W2, (t + 1) * W2)
                act.activation(k.wt[:, at], turned[t % 4][WHOLE:WHOLE + E, 0:W2], ACT.Copy)\
                    .then_inc(kept, 1)
                act.activation(k.wt_parts[:, at], turned[t % 4][:, 0:W2], ACT.Copy).then_inc(kept, 1)

        @block.vector
        def _(dve):
            count = 0

            def link(ins):
                nonlocal count
                count += 1
                ins.then_inc(chain, 1)
                dve.wait_ge(chain, count)

            def over(t, n=E):
                return t.to_broadcast([C, NC, n])

            dve.memset(wide[:, :, :], 0.0).then_inc(chain, 1)
            count += 1
            dve.wait_ge(loaded, n_loaded)
            dve.wait_ge(projected, 1)
            rows = raw[0:C, 0:NC * E].rearrange("p (c e) -> p c e", e=E)
            iota = k.const[0:C, 417:425].rearrange("p (a e) -> p a e", a=1)
            if b is not None:
                link(dve.tensor_tensor(logits[:, :, :], rows,
                                       over(b[:, :].rearrange("p (a e) -> p a e", a=1)), ALU.add))
            else:
                link(dve.tensor_copy(logits[:, :, :], rows))
            if scores:
                link(dve.tensor_reduce(total[:, :, :], logits[:, :, :], AX, ALU.max))
                dve.tensor_tensor(ex[:, :, :], logits[:, :, :], over(total[:, :, :]),
                                  ALU.subtract).then_inc(shifted, 1)
                dve.wait_ge(exped, 1)
                link(dve.tensor_reduce(total[:, :, :], ex[:, :, :], AX, ALU.add))
                link(dve.reciprocal(total[:, :, :], total[:, :, :]))
                link(dve.tensor_tensor(logits[:, :, :], ex[:, :, :], over(total[:, :, :]), ALU.mult))
            for c in range(NC):
                ins = dve.max(best[:, c, :], logits[:, c, :])
            link(ins)
            for c in range(NC):
                ins = dve.max_index(where[:, c, :], best[:, c, :], logits[:, c, :])
            link(ins)
            link(dve.tensor_copy(index[:, :, :], where[:, :, :]))
            if scores:
                link(dve.tensor_tensor(total[:, :, :], best[:, :, 0:1], best[:, :, 1:2], ALU.add))
                link(dve.tensor_scalar(total[:, :, :], total[:, :, :], 1e-20, None, ALU.add))
                link(dve.reciprocal(total[:, :, :], total[:, :, :]))
                link(dve.tensor_tensor(first[:, :, :], best[:, :, 0:1], total[:, :, :], ALU.mult))
                link(dve.tensor_tensor(second[:, :, :], best[:, :, 1:2], total[:, :, :], ALU.mult))
            else:
                dve.tensor_tensor(ex[:, :, 0:2], best[:, :, 0:2],
                                  best[:, :, 0:1].to_broadcast([C, NC, 2]), ALU.subtract)
                dve.tensor_tensor(ex[:, :, 2:E], best[:, :, 2:E],
                                  best[:, :, 0:1].to_broadcast([C, NC, E - 2]), ALU.subtract)\
                    .then_inc(shifted, 1)
                dve.wait_ge(exped, 1)
                link(dve.tensor_tensor(total[:, :, :], ex[:, :, 0:1], ex[:, :, 1:2], ALU.add))
                link(dve.reciprocal(total[:, :, :], total[:, :, :]))
                link(dve.tensor_tensor(first[:, :, :], ex[:, :, 0:1], total[:, :, :], ALU.mult))
                link(dve.tensor_tensor(second[:, :, :], ex[:, :, 1:2], total[:, :, :], ALU.mult))
            link(dve.tensor_tensor(hot[:, :, :], over(iota), over(index[:, :, 0:1]), ALU.is_equal))
            link(dve.tensor_tensor(hot[:, :, :], hot[:, :, :], over(first[:, :, :]), ALU.mult))
            link(dve.tensor_tensor(logits[:, :, :], over(iota), over(index[:, :, 1:2]), ALU.is_equal))
            link(dve.tensor_tensor(logits[:, :, :], logits[:, :, :], over(second[:, :, :]), ALU.mult))
            link(dve.tensor_tensor(whole[:, :, :], hot[:, :, :], logits[:, :, :], ALU.add))
            link(dve.tensor_copy(wide[:, :, WHOLE:WHOLE + E], whole[:, :, :]))
            for at in PARTS:
                link(dve.tensor_copy(parted[:, :, :], whole[:, :, :]))
                ins = dve.tensor_copy(wide[:, :, at:at + E], parted[:, :, :])
                if at != PARTS[-1]:
                    link(ins)
                    link(dve.tensor_tensor(whole[:, :, :], whole[:, :, :], parted[:, :, :], ALU.subtract))
            ins.then_inc(spread, 1)


def split_in_three(dve, parts, source, rest, done, before):
    dve.tensor_copy(parts, source).then_inc(done, 1)
    dve.wait_ge(done, before + 1)
    dve.tensor_tensor(rest[64:128], source[64:128], parts[64:128], ALU.subtract).then_inc(done, 1)
    dve.wait_ge(done, before + 2)
    dve.tensor_copy(parts[64:128], rest[64:128]).then_inc(done, 1)
    dve.wait_ge(done, before + 3)
    dve.tensor_tensor(parts[96:128], rest[96:128], parts[96:128], ALU.subtract).then_inc(done, 1)
    dve.wait_ge(done, before + 4)



def attention0(k):
    with ExitStack() as ctx:
        xm = ctx.enter_context(k.nc.sbuf_tensor("xm", [H, B, L + 3], F32))
        tiles = k.ahead(ctx, "ma", {
            "w_in": ([H, 2, H], "in_proj_x"), "w_z": ([H, 2, H], "in_proj_z"),
            "w_bc": ([H, 2, 128], "x_proj_bc"), "w_dtr": ([H, 2, DR], "x_proj_dt"),
            "w_dt": ([DR, 2, H], "dt_proj"), "w_out": ([H, 2, H], "out_proj"),
            "vec": ([H, 2, 3], "mamba_vec"),
            "conv": ([H, 2, 4], "conv_w"), "a": ([H, 2, DS], "a_log")})
        external_attention(k, xm)
        mamba(k, xm, *tiles)


def external_attention(k, xm):
    nc = k.nc
    with ExitStack() as ctx:
        def sb(name, shape, dt=F32):
            return ctx.enter_context(nc.sbuf_tensor(f"ea_{name}", shape, dt))

        def sem(name):
            return k.semaphore(ctx, f"ea_{name}")

        lanes = range(WIDE)
        mk, mv, vec = sb("mk", [H, 128]), sb("mv", [H, 128]), sb("vec", [H, 2])
        mv_centred = sb("mv_centred", [128, H])
        xs = [sb(f"xs{u}", [H, W2]) for u in lanes]
        probs = [sb(f"probs{u}", [C, 4, 128]) for u in lanes]
        top = [sb(f"top{u}", [C, 4, 1]) for u in lanes]
        total = [sb(f"total{u}", [C, 4, 1]) for u in lanes]
        turned = [sb(f"turned{u}", [128, W2]) for u in lanes]
        squares = [sb(f"squares{u}", [H, W2]) for u in lanes]
        scale = [sb(f"scale{u}", [H, W2]) for u in lanes]
        normed = [sb(f"normed{u}", [H, W2]) for u in lanes]
        acc = [[ctx.enter_context(nc.psum_tensor(f"ea_p{u}_{n}", [128, 512], F32)) for n in range(2)]
               for u in lanes]
        loaded, prepared = sem("loaded"), sem("prepared")
        s = {n: sem(n) for n in ("copied", "logits", "top", "shifted", "exps", "total", "recip",
                                 "probs", "turned", "kept", "affine", "gelu", "xm")}
        ln = {n: sem("ln_" + n) for n in LN_STAGES}
        block = ctx.enter_context(nc.Block())

        @block.sync
        def _(sp):
            for dst, src in ((mk, "mk"), (mv, "mv"), (vec, "ea_vec")):
                sp.dma_start(dst[:, :], k.ins[src]).then_inc(loaded, 16)
            k.load_ahead(sp)

        @block.gpsimd
        def _(pool):
            with pool.Fori(0, NT // WIDE) as step:
                i = step * WIDE
                for u in lanes:
                    pool.wait_ge(s["logits"], i)
                    pool.tensor_copy(xs[u][:, :], k.xn[:, cols(i + u, W2)]).then_inc(s["copied"], 1)

        @block.tensor
        def _(pe):
            pe.wait_ge(loaded, 48)
            pe.matmul(acc[0][0][:, 0:H], mv[:, :], k.centre, start=True, stop=True).then_inc(prepared, 1)
            pe.wait_ge(prepared, 2)
            with pe.Fori(0, NT // WIDE) as step:
                i = step * WIDE
                pe.wait_ge(s["xm"], i)
                for u in lanes:
                    pe.wait_ge(s["copied"], i + u + 1)
                    for c in range(4):
                        mm = pe.matmul(acc[u][0][0:C, c * 128:(c + 1) * 128],
                                       xs[u][:, c * C:(c + 1) * C], mk[:, :], start=True, stop=True)
                    mm.then_inc(s["logits"], 1)
                for u in lanes:
                    pe.wait_ge(s["probs"], i + u + 1)
                    for c in range(4):
                        mm = pe.transpose(acc[u][1][:, c * C:(c + 1) * C], probs[u][:, c, :],
                                          k.ident[0:C, 0:C])
                    mm.then_inc(s["turned"], 1)
                for u in lanes:
                    pe.wait_ge(s["kept"], i + u + 1)
                    pe.matmul(acc[u][0][:, 0:W2], mv_centred[:, :], turned[u][:, :],
                              start=True, stop=True).then_inc(ln["centred"], 1)
                for u in lanes:
                    pe.wait_ge(ln["squares"], i + u + 1)
                    pe.matmul(acc[u][1][:, 0:W2], k.average, squares[u][:, :],
                              start=True, stop=True).then_inc(ln["var"], 1)

        @block.scalar
        def _(act):
            with act.Fori(0, NT // WIDE) as step:
                i = step * WIDE
                load_exp_ln(act)
                for u in lanes:
                    act.wait_ge(s["shifted"], i + u + 1)
                    act.activation(probs[u][:, :, :], probs[u][:, :, :], ACT.Exp).then_inc(s["exps"], 1)
                for u in lanes:
                    act.wait_ge(s["turned"], i + u + 1)
                    act.activation(turned[u][:, :], acc[u][1][:, 0:W2], ACT.Copy).then_inc(s["kept"], 1)
                norm_act(act, k, ln, i, squares, scale, acc, 0, 1, W2)
                for u in lanes:
                    act.wait_ge(s["affine"], i + u + 1)
                    act.activation(normed[u][:, :], normed[u][:, :], ACT.Gelu).then_inc(s["gelu"], 1)

        @block.vector
        def _(dve):
            dve.memset(xm[:, :, 0:3], 0.0)
            dve.wait_ge(prepared, 1)
            dve.tensor_copy(mv_centred[:, :], acc[0][0][:, 0:H]).then_inc(prepared, 1)
            dve.wait_ge(loaded, 48)
            with dve.Fori(0, NT // WIDE) as step:
                i = step * WIDE
                over = lambda t: t[:, :, 0:1].to_broadcast([C, 4, 128])
                rows = lambda u: acc[u][0][0:C, :].rearrange("p (c s) -> p c s", c=4)
                for u in lanes:
                    dve.wait_ge(s["logits"], i + u + 1)
                    dve.tensor_reduce(top[u][:, :, :], rows(u), AX, ALU.max).then_inc(s["top"], 1)
                for u in lanes:
                    dve.wait_ge(s["top"], i + u + 1)
                    dve.tensor_tensor(probs[u][:, :, :], rows(u), over(top[u]), ALU.subtract)\
                        .then_inc(s["shifted"], 1)
                for u in lanes:
                    dve.wait_ge(s["exps"], i + u + 1)
                    dve.tensor_reduce(total[u][:, :, :], probs[u][:, :, :], AX, ALU.add)\
                        .then_inc(s["total"], 1)
                for u in lanes:
                    dve.wait_ge(s["total"], i + u + 1)
                    dve.reciprocal(total[u][:, :, :], total[u][:, :, :]).then_inc(s["recip"], 1)
                for u in lanes:
                    dve.wait_ge(s["recip"], i + u + 1)
                    dve.tensor_tensor(probs[u][:, :, :], probs[u][:, :, :], over(total[u]), ALU.mult)\
                        .then_inc(s["probs"], 1)
                norm_dve(dve, ln, i, scale, acc, 0, [normed[u][:, :] for u in lanes], W2)
                for u in lanes:
                    dve.wait_ge(ln["scaled"], i + u + 1)
                    dve.tensor_scalar(normed[u][:, :], normed[u][:, :], vec[:, 0:1], vec[:, 1:2],
                                      ALU.mult, ALU.add).then_inc(s["affine"], 1)
                for u in lanes:
                    dve.wait_ge(s["gelu"], i + u + 1)
                    two = lambda ap: ap.rearrange("p (b s) -> p b s", b=2)
                    dve.tensor_tensor(xm[:, cols(i + u, 2), 3:L + 3], two(normed[u][:, :]),
                                      two(k.xn[:, cols(i + u, W2)]), ALU.add).then_inc(s["xm"], 1)


def mamba(k, xm, weights, loaded):
    nc = k.nc
    HV = range(2)
    with ExitStack() as ctx:
        def sb(name, shape, dt=F32):
            return ctx.enter_context(nc.sbuf_tensor(f"ma_{name}", shape, dt))

        def sem(name):
            return k.semaphore(ctx, f"ma_{name}")

        w_in, w_z, w_bc, w_dtr, w_dt, w_out, vec, conv, a = weights
        w_tap = sb("w_tap", [H, 4, 2, H])
        scaled_in = sb("scaled_in", [H, 2, 4, H])
        xact = [[sb(f"xact{q}{h}", [H, W2]) for h in HV] for q in HV]
        gate = [[sb(f"gate{q}{h}", [H, W2]) for h in HV] for q in HV]
        dt = [[sb(f"dt{q}{h}", [H, W2]) for h in HV] for q in HV]
        dtx = [[sb(f"dtx{q}{h}", [H, W2]) for h in HV] for q in HV]
        bc = [sb(f"bc{q}", [128, W2], BF16) for q in HV]
        rest, dtr = sb("rest", [128, W2]), sb("dtr", [DR, W2])
        soft = [sb(f"soft{h}", [H, W2]) for h in HV]
        da = [[sb(f"da{h}{n}", [H, W2]) for n in range(4)] for h in HV]
        dbx = [sb(f"dbx{n}", [H, W2]) for n in range(2)]
        state = [sb(f"state{n}", [H, W2]) for n in range(4)]
        c_kept = [sb(f"c{n}", [H, W2]) for n in range(2)]
        hc = [sb(f"hc{n}", [H, W2]) for n in range(8)]
        y = [sb(f"y{h}", [H, W2]) for h in HV]
        psum = lambda n: ctx.enter_context(nc.psum_tensor(f"ma_ps_{n}", [128, 512], F32))
        p = [psum("p0"), psum("p1")]
        b_all, c_all = [psum("b0"), psum("b1")], [psum("c0"), psum("c1")]
        y_sum = [psum("y0"), psum("y1")]
        scaled_w, turned_w, taps, a_exp, a_ready = (sem(n) for n in (
            "scaled_w", "turned_w", "taps", "a_exp", "a_ready"))
        s = {n: sem(n) for n in (
            "conv", "xact", "z", "gate", "bc_sum", "split", "dtr_sum", "dtr", "dt_sum", "abs", "exp",
            "log", "relu", "dt", "dtx",
            "b", "c", "c_kept", "da", "dbx", "scan", "hc", "y_add", "paired",
            "y_skip", "y", "out", "added")}
        block = ctx.enter_context(nc.Block())
        N_LOADED = 16 * 9
        NS = 2 * DS
        PAIRED = (5,)
        NPAIR = 2 * len(PAIRED)

        def run(eng, tile):
            for u in range(2):
                tile(u, u, u == 1, True)
            with eng.Fori(0, NT // 2 - 2) as step:
                for u in range(2):
                    tile(step * 2 + (2 + u), u, True, True)
            for u in range(2):
                tile(NT - 2 + u, u, True, u == 0)

        @block.tensor
        def _(pe):
            pe.wait_ge(loaded, N_LOADED)
            for h in HV:
                pe.wait_ge(scaled_w, 4 * (h + 1))
                for tap in range(4):
                    mm = pe.transpose(p[h][:, tap * H:(tap + 1) * H], scaled_in[:, h, tap, :], k.ident)
                mm.then_inc(turned_w, 1)
            pe.wait_ge(taps, 2)

            def conv_part(t, h, taps, first=False):
                if taps[0] == 0 and not first:
                    pe.wait_ge(s["added"], t - 1)
                for tap in taps:
                    mm = pe.matmul(p[h][:, 0:W2], w_tap[:, tap, h, :],
                                   xm[:, cols(t, 2), tap:tap + L], start=tap == 0, stop=tap == 3)
                if taps[-1] == 3:
                    mm.then_inc(s["conv"], 1)

            def z_half(t, h):
                pe.wait_ge(s["xact"], 2 * t + h + 1)
                pe.matmul(p[h][:, 0:W2], w_z[:, h, :], xm[:, cols(t, 2), 3:3 + L],
                          start=True, stop=True).then_inc(s["z"], 1)

            def bc_rows(t, q):
                pe.wait_ge(s["gate"], 2 * t + 1)
                for h in HV:
                    mm = pe.matmul(p[0][:, 0:W2], w_bc[:, h, :], xact[q][h][:, :],
                                   start=h == 0, stop=h == 1)
                mm.then_inc(s["bc_sum"], 1)

            def dt_rank(t, q):
                pe.wait_ge(s["gate"], 2 * t + 2)
                for h in HV:
                    mm = pe.matmul(p[1][0:DR, 0:W2], w_dtr[:, h, :], xact[q][h][:, :],
                                   start=h == 0, stop=h == 1)
                mm.then_inc(s["dtr_sum"], 1)

            def dt_half(t, h):
                pe.wait_ge(s["dtr"], t + 1)
                pe.wait_ge(s["split"], 4 * (t + 1))
                pe.matmul(p[h][:, 0:W2], w_dt[:, h, :], dtr[:, :], start=True, stop=True)\
                    .then_inc(s["dt_sum"], 1)

            def ahead(t, q, first=False):
                return {4: lambda: conv_part(t, 0, (0, 1), first), 5: lambda: conv_part(t, 0, (2, 3), first),
                        6: lambda: conv_part(t, 1, (0, 1), first), 7: lambda: conv_part(t, 1, (2, 3), first),
                        8: lambda: (z_half(t, 0), z_half(t, 1)), 9: lambda: bc_rows(t, q),
                        10: lambda: dt_rank(t, q), 12: lambda: (dt_half(t, 0), dt_half(t, 1))}

            def output(t):
                pe.wait_ge(s["y"], 2 * (t + 1))
                pe.wait_ge(s["relu"], 2 * (t + 2) if not (isinstance(t, int) and t == NT - 1) else 2 * NT)
                for h in HV:
                    mm = pe.matmul(p[0][:, 0:W2], w_out[:, h, :], y[h][:, :], start=h == 0, stop=h == 1)
                mm.then_inc(s["out"], 1)

            for f in ahead(0, 0, True).values():
                f()

            def tile(t, u, before, more):
                steps = ahead(t + 1, 1 - u) if more else {}
                done, states = t * NS, t * DS

                def rows(n):
                    if n == 0:
                        pe.wait_ge(s["split"], 4 * (t + 1))
                    if n >= 2:
                        pe.wait_ge(s["dbx"], done + 2 * (n - 1))
                        pe.wait_ge(s["c_kept"], states + n - 1)
                    else:
                        pe.wait_ge(s["dbx"], done)
                        pe.wait_ge(s["c_kept"], states)
                    pe.matmul(b_all[n % 2][:, 0:W2], k.select[:, n:n + 1].to_broadcast([128, 128]),
                              bc[u][:, :], start=True, stop=True).then_inc(s["b"], 1)
                    pe.matmul(c_all[n % 2][:, 0:W2],
                              k.select[:, DS + n:DS + n + 1].to_broadcast([128, 128]),
                              bc[u][:, :], start=True, stop=True).then_inc(s["c"], 1)

                def y_adds(n):
                    if n == 0:
                        pe.wait_ge(s["y_skip"], 2 * t)
                    if n in PAIRED:
                        return
                    for h in HV:
                        if n - 1 in PAIRED:
                            pe.wait_ge(s["paired"], t * NPAIR + 2 * PAIRED.index(n - 1) + h + 1)
                        pe.wait_ge(s["hc"], done + 2 * n + h + 1)
                        pe.matmul(y_sum[h][:, 0:W2], k.ident, hc[(2 * n + h) % 8][:, :],
                                  start=n <= 1 and n - 1 in (-1, *PAIRED), stop=n == DS - 1)\
                            .then_inc(s["y_add"], 2 if n - 1 in PAIRED else 1)

                rows(0)
                rows(1)
                for n in range(DS):
                    if n in steps:
                        steps[n]()
                    if n == 2 and before:
                        output(t - 1)
                    if n:
                        y_adds(n - 1)
                    if n + 2 < DS:
                        rows(n + 2)
                y_adds(DS - 1)

            run(pe, tile)
            output(NT - 1)

        @block.scalar
        def _(act):
            act.wait_ge(loaded, N_LOADED)
            load_exp_ln(act)
            act.activation(a[:, :, :], a[:, :, :], ACT.Exp).then_inc(a_exp, 1)
            for h in HV:
                act.wait_ge(turned_w, h + 1)
                act.activation(w_tap[:, :, h, :], p[h][:, :].rearrange("p (t d) -> p t d", t=4),
                               ACT.Copy).then_inc(taps, 1)
            act.wait_ge(a_ready, 1)

            def xacts(t, q):
                for h in HV:
                    act.wait_ge(s["conv"], 2 * t + h + 1)
                    act.activation(xact[q][h][:, :], p[h][:, 0:W2], ACT.Silu, bias=vec[:, h, 0:1])\
                        .then_inc(s["xact"], 1)

            def gates(t, q):
                for h in HV:
                    act.wait_ge(s["z"], 2 * t + h + 1)
                    act.activation(gate[q][h][:, :], p[h][:, 0:W2], ACT.Silu).then_inc(s["gate"], 1)

            def keep_rank(t):
                act.wait_ge(s["dtr_sum"], t + 1)
                act.activation(dtr[:, :], p[1][0:DR, 0:W2], ACT.Copy).then_inc(s["dtr"], 1)

            def softplus(t, q):
                for h in HV:
                    act.wait_ge(s["dt_sum"], 2 * t + h + 1)
                    act.wait_ge(s["dt"], 2 * t)
                    act.activation(soft[h][:, :], p[h][:, 0:W2], ACT.Abs, bias=vec[:, h, 1:2])\
                        .then_inc(s["abs"], 1)
                for h in HV:
                    act.wait_ge(s["abs"], 2 * t + h + 1)
                    act.activation(soft[h][:, :], soft[h][:, :], ACT.Exp, scale=-1.0)\
                        .then_inc(s["exp"], 1)
                for h in HV:
                    act.wait_ge(s["exp"], 2 * t + h + 1)
                    act.activation(soft[h][:, :], soft[h][:, :], ACT.Ln, bias=1.0).then_inc(s["log"], 1)

            def ahead(t, q):
                return {8: lambda: (xacts(t, q), gates(t, q), load_exp_ln(act)),
                        11: lambda: keep_rank(t), 13: lambda: softplus(t, q)}

            for f in ahead(0, 0).values():
                f()

            def tile(t, u, before, more):
                steps = ahead(t + 1, 1 - u) if more else {}
                done, states = t * NS, t * DS
                if u == 0:
                    load_exp_ln(act)
                act.wait_ge(s["dt"], 2 * (t + 1))
                for n in range(DS):
                    for h in HV:
                        act.wait_ge(s["scan"], done + 2 * n - 7 + h if n >= 4 else done)
                        act.activation(da[h][n % 4][:, :], dt[u][h][:, :], ACT.Exp,
                                       scale=a[:, h, n:n + 1]).then_inc(s["da"], 1)
                    act.wait_ge(s["c"], states + n + 1)
                    act.wait_ge(s["hc"], done + 2 * (n - 1) if n >= 2 else done)
                    act.activation(c_kept[n % 2][:, :], c_all[n % 2][:, 0:W2], ACT.Copy)\
                        .then_inc(s["c_kept"], 1)
                    if n in steps:
                        steps[n]()

            run(act, tile)

        @block.gpsimd
        def _(pool):
            def tile(t, u, before, more):
                done, states = t * NS, t * DS
                for n in range(DS):
                    pool.wait_ge(s["c_kept"], states + n + 1)
                    for h in HV:
                        m = 2 * n + h
                        pool.wait_ge(s["scan"], done + m + 1)
                        pool.wait_ge(s["y_add"], done + m - 7 if m >= 8 else done)
                        pool.tensor_tensor(hc[m % 8][:, :], state[m % 4][:, :], c_kept[n % 2][:, :],
                                           ALU.mult).then_inc(s["hc"], 1)
                    if n - 1 in PAIRED:
                        for h in HV:
                            m = 2 * n + h
                            pool.wait_ge(s["hc"], done + m + 1)
                            pool.tensor_tensor(hc[m % 8][:, :], hc[m % 8][:, :], hc[(m - 2) % 8][:, :],
                                               ALU.add).then_inc(s["paired"], 1)

            run(pool, tile)

        @block.vector
        def _(dve):
            dve.wait_ge(loaded, N_LOADED)
            for h in HV:
                for tap in range(4):
                    dve.tensor_scalar(scaled_in[:, h, tap, :], w_in[:, h, :], conv[:, h, tap:tap + 1],
                                      None, ALU.mult).then_inc(scaled_w, 1)
            dve.wait_ge(a_exp, 1)
            dve.tensor_scalar(a[:, :, :], a[:, :, :], -1.0, None, ALU.mult).then_inc(a_ready, 1)

            def split(t, q):
                dve.wait_ge(s["bc_sum"], t + 1)
                split_in_three(dve, bc[q][:, :], p[0][:, 0:W2], rest[:, :], s["split"], 4 * t)

            def steps_of_time(t, q):
                for h in HV:
                    dve.wait_ge(s["abs"], 2 * t + h + 1)
                    dve.tensor_scalar(dt[q][h][:, :], p[h][:, 0:W2], vec[:, h, 1:2], 0.0,
                                      ALU.add, ALU.max).then_inc(s["relu"], 1)
                for h in HV:
                    dve.wait_ge(s["relu"], 2 * t + h + 1)
                    dve.wait_ge(s["log"], 2 * t + h + 1)
                    dve.tensor_tensor(dt[q][h][:, :], dt[q][h][:, :], soft[h][:, :], ALU.add)\
                        .then_inc(s["dt"], 1)
                for h in HV:
                    dve.wait_ge(s["dt"], 2 * t + h + 1)
                    dve.tensor_tensor(dtx[q][h][:, :], dt[q][h][:, :], xact[q][h][:, :], ALU.mult)\
                        .then_inc(s["dtx"], 1)

            def ahead(t, q):
                return {11: lambda: split(t, q), 15: lambda: steps_of_time(t, q)}

            for f in ahead(0, 0).values():
                f()

            def skip(t, q):
                dve.wait_ge(s["y_add"], (t + 1) * NS)
                for h in HV:
                    dve.scalar_tensor_tensor(y[h][:, :], xact[q][h][:, :], vec[:, h, 2:3],
                                             y_sum[h][:, 0:W2], ALU.mult, ALU.add)\
                        .then_inc(s["y_skip"], 1)

            def gated(t, q):
                for h in HV:
                    dve.wait_ge(s["y_skip"], 2 * t + h + 1)
                    dve.tensor_tensor(y[h][:, :], y[h][:, :], gate[q][h][:, :], ALU.mult)\
                        .then_inc(s["y"], 1)

            def add(t):
                dve.wait_ge(s["out"], t + 1)
                dve.tensor_tensor(k.h[:, cols(t, W2)], p[0][:, 0:W2], k.h[:, cols(t, W2)], ALU.add)\
                    .then_inc(s["added"], 1)

            def tile(t, u, before, more):
                steps = ahead(t + 1, 1 - u) if more else {}
                if before:
                    steps |= {0: lambda: skip(t - 1, 1 - u), 1: lambda: gated(t - 1, 1 - u),
                              3: lambda: add(t - 1)}
                done, states = t * NS, t * DS
                dve.wait_ge(s["dtx"], 2 * (t + 1))
                for n in range(DS):
                    for h in HV:
                        m = 2 * n + h
                        dve.wait_ge(s["b"], states + n + 1)
                        dve.wait_ge(s["scan"], done + m - 1 if m >= 2 else done)
                        dve.tensor_tensor(dbx[m % 2][:, :], b_all[n % 2][:, 0:W2], dtx[u][h][:, :],
                                          ALU.mult).then_inc(s["dbx"], 1)
                        dve.wait_ge(s["dbx"], done + m + 1)
                        dve.wait_ge(s["da"], done + m + 1)
                        dve.wait_ge(s["hc"], done + m - 3 if m >= 4 else done)
                        for b in range(2):
                            at = slice(b * L, (b + 1) * L)
                            ins = dve.tensor_tensor_scan(state[m % 4][:, at], da[h][n % 4][:, at],
                                                         dbx[m % 2][:, at], 0.0, ALU.mult, ALU.add)
                        ins.then_inc(s["scan"], 1)
                    if n in steps:
                        steps[n]()

            run(dve, tile)
            skip(NT - 1, (NT - 1) % 2)
            gated(NT - 1, (NT - 1) % 2)
            add(NT - 1)




def experts0(k):
    with ExitStack() as weights:
        routing = k.ahead(weights, "route0", {"w": ([H, E], "router_w"), "b": ([C, E], "router_b")})
        tiles = k.ahead(weights, "ex0", {
            "gate_up": ([H, E, 2 * I0], "gate_up"), "down": ([H, E, 2, H], "down"),
            "down_bias": ([E, H], "down_bias"), "bias": ([H, E, 4], "gate_up_bias")})
        block_norm(k)
        router(k, "route0", *routing[0], routing[1], scores=False)
        run_experts0(k, *tiles)


def run_experts0(k, weights, loaded):
    nc = k.nc
    with ExitStack() as ctx:
        def sb(name, shape, dt=F32):
            return ctx.enter_context(nc.sbuf_tensor(f"ex0_{name}", shape, dt))

        def sem(name):
            return k.semaphore(ctx, f"ex0_{name}")

        gate_up, down, down_bias, bias = weights
        gate_scaled, up_one = sb("gate_scaled", [H, E, 2]), sb("up_one", [H, E, 2])
        sig = [sb(f"sig{n}", [H, W2]) for n in range(2)]
        gelu = [sb(f"gelu{n}", [H, W2]) for n in range(2)]
        inner = [sb(f"inner{n}", [H, W2]) for n in range(2)]
        weighted = [sb(f"weighted{n}", [H, W2]) for n in range(2)]
        psum = lambda n: ctx.enter_context(nc.psum_tensor(f"ex0_{n}", [128, 512], F32))
        gate, up = [psum("gate0"), psum("gate1")], [psum("up0"), psum("up1")]
        weight, total = [psum("weight0"), psum("weight1")], psum("total")
        ready = sem("ready")
        s = {n: sem(n) for n in ("gated", "upped", "spread", "sig", "gelu", "inner", "weighted",
                                 "downed", "added")}
        block = ctx.enter_context(nc.Block())
        halves = [(e, j) for e in range(E) for j in range(2)]
        NHF = len(halves)

        @block.tensor
        def _(pe):
            pe.wait_ge(loaded, 64)
            with pe.Fori(0, NT) as t:
                done = t * NHF
                x = k.xn[:, cols(t, W2)]

                def down_half(n):
                    e, j = halves[n]
                    pe.wait_ge(s["weighted"], done + n + 1)
                    pe.matmul(total[:, 0:W2], down[:, e, j, :], weighted[n % 2][:, :], start=False,
                              stop=n == NHF - 1).then_inc(s["downed"], 1)

                for n, (e, j) in enumerate(halves):
                    if n >= 2:
                        pe.wait_ge(s["gelu"], done + n - 1)
                    elif n == 0:
                        pe.wait_ge(s["weighted"], done)
                    pe.matmul(gate[j][:, 0:W2], gate_up[:, e, j * H:(j + 1) * H], x,
                              start=True, stop=True).then_inc(s["gated"], 1)
                    if n >= 2:
                        pe.wait_ge(s["inner"], done + n - 1)
                    pe.matmul(up[j][:, 0:W2], gate_up[:, e, I0 + j * H:I0 + (j + 1) * H], x,
                              start=True, stop=True).then_inc(s["upped"], 1)
                    if j == 0:
                        if n >= 4:
                            pe.wait_ge(s["weighted"], done + n - 2)
                        pe.matmul(weight[e % 2][:, 0:W2], k.select[:, e:e + 1].to_broadcast([128, 128]),
                                  k.wt_parts[:, cols(t, W2)], start=True, stop=True)\
                            .then_inc(s["spread"], 1)
                    if n == 0:
                        pe.wait_ge(s["added"], t)
                        pe.matmul(total[:, 0:W2], down_bias[:, :], k.wt[:, cols(t, W2)],
                                  start=True, stop=False)
                    else:
                        down_half(n - 1)
                down_half(NHF - 1)

        @block.scalar
        def _(act):
            act.wait_ge(ready, 2)
            with act.Fori(0, NT) as t:
                done = t * NHF
                for n, (e, j) in enumerate(halves):
                    act.wait_ge(s["gated"], done + n + 1)
                    if n >= 2:
                        act.wait_ge(s["gelu"], done + n - 1)
                    act.activation(sig[j][:, :], gate[j][:, 0:W2], ACT.Sigmoid,
                                   bias=gate_scaled[:, e, j:j + 1], scale=1.702).then_inc(s["sig"], 1)

        @block.vector
        def _(dve):
            dve.wait_ge(loaded, 64)
            dve.tensor_scalar(gate_scaled[:, :, :], bias[:, :, 0:2], 1.702, None, ALU.mult)\
                .then_inc(ready, 1)
            dve.tensor_scalar(up_one[:, :, :], bias[:, :, 2:4], 1.0, None, ALU.add).then_inc(ready, 1)
            dve.wait_ge(ready, 2)
            with dve.Fori(0, NT) as t:
                done = t * NHF
                for n, (e, j) in enumerate(halves):
                    dve.wait_ge(s["sig"], done + n + 1)
                    dve.scalar_tensor_tensor(gelu[j][:, :], gate[j][:, 0:W2], bias[:, e, j:j + 1],
                                             sig[j][:, :], ALU.add, ALU.mult).then_inc(s["gelu"], 1)
                    dve.wait_ge(s["gelu"], done + n + 1)
                    dve.wait_ge(s["upped"], done + n + 1)
                    dve.scalar_tensor_tensor(inner[j][:, :], up[j][:, 0:W2], up_one[:, e, j:j + 1],
                                             gelu[j][:, :], ALU.add, ALU.mult).then_inc(s["inner"], 1)
                    dve.wait_ge(s["inner"], done + n + 1)
                    if j == 0:
                        dve.wait_ge(s["spread"], t * E + e + 1)
                    if n >= 2:
                        dve.wait_ge(s["downed"], done + n - 1)
                    dve.tensor_tensor(weighted[j][:, :], inner[j][:, :], weight[e % 2][:, 0:W2],
                                      ALU.mult).then_inc(s["weighted"], 1)
                dve.wait_ge(s["downed"], done + NHF)
                dve.tensor_tensor(k.h[:, cols(t, W2)], total[:, 0:W2], k.h[:, cols(t, W2)], ALU.add)\
                    .then_inc(s["added"], 1)



def attention1(k):
    with ExitStack() as ctx:
        k.r = ctx.enter_context(k.nc.sbuf_tensor("r", [H, T], F32))
        tables = {"w": ([H, 3 * NH * D + NH], "slow_w0"),
                  "w_out": ([H, NH // 2, H], "fw_out0"), "masks": ([128, MASK_COLS], "masks")}
        ip = k.ahead(ctx, "ip", {"w": ([H, H], "ip_w"), "vec": ([H, 3], "ip_vec")})
        fw = k.ahead(ctx, "fw", tables)
        ff = k.ahead(ctx, "ff", {"w1": ([H, FF // H, H], "ff_w1"), "w2": ([H, FF // H, H], "ff_w2"),
                                 "vec": ([H, 5 + FF // H], "ff_vec")})
        block_norm(k)
        input_projection(k, *ip)
        fast_weights(k, 0, *fw, 48)
        k.to_load = [(fw[0][0], "slow_w1", fw[1]), (fw[0][1], "fw_out1", fw[1])]
        feed_forward(k, *ff)
        fast_weights(k, 1, *fw, 80)


def input_projection(k, weights, loaded):
    nc = k.nc
    with ExitStack() as ctx:
        def sb(name, shape, dt=F32):
            return ctx.enter_context(nc.sbuf_tensor(f"ip_{name}", shape, dt))

        def sem(name):
            return k.semaphore(ctx, f"ip_{name}")

        lanes = range(WIDE)
        w, vec = weights
        squares = [sb(f"squares{u}", [H, W2]) for u in lanes]
        scale = [sb(f"scale{u}", [H, W2]) for u in lanes]
        acc = [[ctx.enter_context(nc.psum_tensor(f"ip_p{u}_{n}", [128, 512], F32)) for n in range(2)]
               for u in lanes]
        projected, added, affine = sem("projected"), sem("added"), sem("affine")
        ln = {n: sem("ln_" + n) for n in LN_STAGES}
        block = ctx.enter_context(nc.Block())

        @block.tensor
        def _(pe):
            pe.wait_ge(loaded, 32)
            with pe.Fori(0, NT // WIDE) as step:
                i = step * WIDE
                pe.wait_ge(affine, i)
                for u in lanes:
                    pe.matmul(acc[u][0][:, 0:W2], w[:, :], k.xn[:, cols(i + u, W2)],
                              start=True, stop=True).then_inc(projected, 1)
                norm_pe(pe, k, ln, i, [k.r[:, cols(i + u, W2)] for u in lanes], added, squares, acc,
                        1, 0, W2)

        @block.scalar
        def _(act):
            with act.Fori(0, NT // WIDE) as step:
                norm_act(act, k, ln, step * WIDE, squares, scale, acc, 1, 0, W2)

        @block.vector
        def _(dve):
            dve.wait_ge(loaded, 32)
            with dve.Fori(0, NT // WIDE) as step:
                i = step * WIDE
                xn = [k.xn[:, cols(i + u, W2)] for u in lanes]
                for u in lanes:
                    dve.wait_ge(projected, i + u + 1)
                    dve.tensor_scalar(k.r[:, cols(i + u, W2)], acc[u][0][:, 0:W2], vec[:, 0:1], None,
                                      ALU.add).then_inc(added, 1)
                norm_dve(dve, ln, i, scale, acc, 1, xn, W2)
                for u in lanes:
                    dve.wait_ge(ln["scaled"], i + u + 1)
                    dve.tensor_scalar(xn[u], xn[u], vec[:, 1:2], vec[:, 2:3], ALU.mult, ALU.add)\
                        .then_inc(affine, 1)


def feed_forward(k, weights, loaded):
    nc = k.nc
    NB = FF // H
    with ExitStack() as ctx:
        def sb(name, shape, dt=F32):
            return ctx.enter_context(nc.sbuf_tensor(f"ff_{name}", shape, dt))

        def sem(name):
            return k.semaphore(ctx, f"ff_{name}")

        lanes = range(WIDE)
        w1, w2, vec = weights
        squares = [sb(f"squares{u}", [H, W2]) for u in lanes]
        scale = [sb(f"scale{u}", [H, W2]) for u in lanes]
        normed = [sb(f"normed{u}", [H, W2]) for u in lanes]
        hidden = [[sb(f"hidden{u}{n}", [H, W2]) for n in range(NB)] for u in lanes]
        acc = [[ctx.enter_context(nc.psum_tensor(f"ff_p{u}_{n}", [128, 512], F32)) for n in range(2)]
               for u in lanes]
        s = {n: sem(n) for n in ("affine1", "up", "relu", "down", "added", "affine2")}
        ln = [{n: sem(f"ln{j}_{n}") for n in LN_STAGES} for j in range(2)]
        block = ctx.enter_context(nc.Block())

        @block.sync
        def _(sp):
            k.load_ahead(sp)

        @block.tensor
        def _(pe):
            pe.wait_ge(loaded, 48)
            with pe.Fori(0, NT // WIDE) as step:
                i = step * WIDE
                pe.wait_ge(s["affine2"], i)
                norm_pe(pe, k, ln[0], i, [k.r[:, cols(i + u, W2)] for u in lanes], None, squares,
                        acc, 0, 1, W2)
                for n in range(NB):
                    for u in lanes:
                        if n == 0:
                            pe.wait_ge(s["affine1"], i + u + 1)
                        else:
                            pe.wait_ge(s["relu"], i * NB + (n - 1) * WIDE + u + 1)
                        pe.matmul(acc[u][n % 2][:, 0:W2], w1[:, n, :], normed[u][:, :],
                                  start=True, stop=True).then_inc(s["up"], 1)
                for u in lanes:
                    pe.wait_ge(s["relu"], (i + WIDE) * NB)
                    for n in range(NB):
                        mm = pe.matmul(acc[u][0][:, 0:W2], w2[:, n, :], hidden[u][n][:, :],
                                       start=n == 0, stop=n == NB - 1)
                    mm.then_inc(s["down"], 1)
                norm_pe(pe, k, ln[1], i, [k.r[:, cols(i + u, W2)] for u in lanes], s["added"],
                        squares, acc, 1, 0, W2)

        @block.scalar
        def _(act):
            act.wait_ge(loaded, 48)
            with act.Fori(0, NT // WIDE) as step:
                i = step * WIDE
                norm_act(act, k, ln[0], i, squares, scale, acc, 0, 1, W2)
                for n in range(NB):
                    for u in lanes:
                        act.wait_ge(s["up"], i * NB + n * WIDE + u + 1)
                        act.activation(hidden[u][n][:, :], acc[u][n % 2][:, 0:W2], ACT.Relu,
                                       bias=vec[:, 5 + n:6 + n]).then_inc(s["relu"], 1)
                norm_act(act, k, ln[1], i, squares, scale, acc, 1, 0, W2)

        @block.vector
        def _(dve):
            dve.wait_ge(loaded, 48)
            with dve.Fori(0, NT // WIDE) as step:
                i = step * WIDE
                xn = [k.xn[:, cols(i + u, W2)] for u in lanes]
                norm_dve(dve, ln[0], i, scale, acc, 0, [normed[u][:, :] for u in lanes], W2)
                for u in lanes:
                    dve.wait_ge(ln[0]["scaled"], i + u + 1)
                    dve.tensor_scalar(normed[u][:, :], normed[u][:, :], vec[:, 0:1], vec[:, 1:2],
                                      ALU.mult, ALU.add).then_inc(s["affine1"], 1)
                for u in lanes:
                    r = k.r[:, cols(i + u, W2)]
                    dve.wait_ge(s["down"], i + u + 1)
                    dve.scalar_tensor_tensor(r, acc[u][0][:, 0:W2], vec[:, 4:5], r, ALU.add, ALU.add)\
                        .then_inc(s["added"], 1)
                norm_dve(dve, ln[1], i, scale, acc, 1, xn, W2)
                for u in lanes:
                    dve.wait_ge(ln[1]["scaled"], i + u + 1)
                    dve.tensor_scalar(xn[u], xn[u], vec[:, 2:3], vec[:, 3:4], ALU.mult, ALU.add)\
                        .then_inc(s["affine2"], 1)


def fast_weights(k, layer, weights, loaded, n_loaded):
    nc = k.nc
    tag = f"fw{layer}"
    NP = NH // 2
    BLOCK = 32
    NB = 128 // BLOCK
    LANES_OF = NB * LANES * NH
    with ExitStack() as ctx:
        def sb(name, shape, dt=F32):
            return ctx.enter_context(nc.sbuf_tensor(f"{tag}_{name}", shape, dt))

        def sem(name):
            return k.semaphore(ctx, f"{tag}_{name}")

        chunks = range(LANES)
        w, w_out, masks = weights
        lower = masks[:, 0:128].rearrange("p (a c) -> p a c", a=1)
        unit = masks[:, 128:MASK_COLS]
        xs = sb("xs", [H, L])
        per = lambda name, shape: [sb(f"{name}{u}", shape) for u in chunks]
        both = lambda name, shape: [per(f"{name}{parity}_", shape) for parity in range(2)]
        top = {n: per("top_" + n, [C, NH, 1]) for n in "kq"}
        total = {n: per("total_" + n, [C, NH, 1]) for n in "kq"}
        q_rows = per("q_rows", [128, NH, D])
        beta = sb("beta", [C, LANES, NH, 1])
        kb_scale = per("kb_scale", [C, NH, 1])
        kb = per("kb", [128, NH, D])
        k_t = per("k_t", [128, NP, 128])
        lane_a = sb("lane_a", [2 * LANES_OF, BLOCK, BLOCK])
        lane_x = sb("lane_x", [2 * LANES_OF, BLOCK // 2, BLOCK])
        lane_p = sb("lane_p", [2 * LANES_OF, BLOCK // 2, BLOCK])
        k_rows = both("k_rows", [128, NH, D])
        rhs = both("rhs", [128, NH, D])
        kb_t = both("kb_t", [128, NP, 128])
        q_t = both("q_t", [128, NP, 128])
        qk = both("qk", [128, 2, NP, 128])
        a_t = [sb(f"a_t{parity}", [128, LANES, 2, NP, 128]) for parity in range(2)]
        x_t = sb("x_t", [128, LANES, 2, NP, BLOCK])
        u_new = per("u_new", [128, NH, D])
        state = sb("state", [128, NP, D])
        out_t = sb("out_t", [128, NP, L])
        bank = ctx.enter_context(nc.psum_tensor(f"{tag}_p", [128, 8, 512], F32))
        a_dram = nc.dram_tensor(f"{tag}_a_dram", (NB, LANES * NH, BLOCK, BLOCK), F32).ap()
        x_dram = nc.dram_tensor(f"{tag}_x_dram", (NB, LANES * NH, BLOCK, BLOCK), F32).ap()
        heads = lambda ap: ap.rearrange("p (h d) -> p h d", h=NH)
        pairs = lambda ap: ap.rearrange("p (n c) -> p n c", n=NP)
        half = lambda r: slice(64 * r, 64 * r + 64)
        rows_of = lambda g: slice(BLOCK * g, BLOCK * g + BLOCK)

        SOLVE, JOIN, OUT, PROJECT = 0, 1, 2, 1
        PROJ_K, PROJ_Q, PROJ_V, BETA = (4, 5), (7, 3), (4, 5), 6
        TURN_K, TURN_KB, TURN_Q = (4, 5), (6, 7), (3, 6)
        SUM_A, SUM_QK = (4, 6), ((7, 3), (4, 5))

        cleared = sem("cleared")
        s = {n: sem(n) for n in (
            "copied", "proj_k", "proj_q", "proj_v", "proj_beta", "top_k", "top_q", "shift_k", "shift_q",
            "exp_k", "exp_q", "total_k", "total_q", "recip_k", "recip_q", "rows_k", "rows_q",
            "beta_exp", "beta_one", "beta", "kb", "rhs", "turn_k", "turn_q", "turn_kb", "k_t", "q_t",
            "kb_t", "a_sum", "a_t", "qk_sum", "qk_even", "qk_copied", "qk_odd",
            "a_out", "a_in", "unit", "kb_scale", "x_out", "x_in",
            *(f"solve_sum{g}" for g in range(NB)), *(f"solved{g}" for g in range(NB)),
            *(f"join_sum{g}" for g in range(1, NB)), *(f"joined{g}" for g in range(1, NB)),
            "state_sum", "state", "carried_sum", "carried", "out_sum", "out_t", "projected", "added")}
        product = [sem(f"product{j}") for j in range(BLOCK - 1)]
        inverted = [sem(f"inverted{j}") for j in range(BLOCK - 1)]
        block = ctx.enter_context(nc.Block())

        def stages(eng, stage):
            stage(0, 0, True, False, False)
            stage(1, 1, True, True, False)
            with eng.Fori(0, (B - 2) // 2) as step:
                first = step * 2
                stage(first + 2, 0, True, True, True)
                stage(first + 3, 1, True, True, True)
            stage(B, B % 2, False, True, True)
            stage(B + 1, (B + 1) % 2, False, False, True)

        @block.sync
        def _(sp):
            lanes_of = lambda f: slice(f * LANES_OF, (f + 1) * LANES_OF)

            def stage(b, par, prepares, substitutes, finishes):
                if substitutes:
                    x_written, solved_before = b * 32, b * 2 - 2
                    work_out(sp, b, x_written, solved_before)
                    sp.wait_ge(inverted[-1], b)
                    for f in range(2):
                        sp.dma_start(x_dram.rearrange("g n (c f) i -> f (g n) c i", f=2)[f],
                                     lane_x[lanes_of(f)]).then_inc(s["x_out"], 16)
                    sp.wait_ge(s["x_out"], x_written)
                    sp.wait_ge(s[f"solve_sum{NB - 1}"], solved_before)
                    for g in range(NB):
                        sp.dma_start(x_t[rows_of(g)].rearrange("c u r p i -> c (u r p) i"),
                                     x_dram[g].rearrange("n c i -> c n i")).then_inc(s["x_in"], 16)
                if prepares:
                    chunks_ready, a_written = b * 2 + 2, b * (16 * NB) + 16 * NB
                    work_out(sp, chunks_ready, a_written)
                    sp.wait_ge(s["a_t"], chunks_ready)
                    for g in range(NB):
                        sp.dma_start(a_dram[g].rearrange("n j i -> j n i"),
                                     a_t[par][rows_of(g), :, :, :, rows_of(g)].rearrange("j u r p i -> j (u r p) i"))\
                            .then_inc(s["a_out"], 16)
                    sp.wait_ge(s["a_out"], a_written)
                    for f in range(2):
                        sp.dma_start(lane_a[lanes_of(f)], a_dram.rearrange("g n j i -> (g n) j i"))\
                            .then_inc(s["a_in"], 16)

            stages(sp, stage)
            sp.wait_ge(s["x_in"], B * 16 * NB)

        @block.gpsimd
        def _(pool):
            for u in chunks:
                for t in (k_rows[0][u], k_rows[1][u], q_rows[u], kb[u], rhs[0][u], rhs[1][u]):
                    ins = pool.memset(t[:, :, :], 0.0)
            ins.then_inc(cleared, 1)
            pool.wait_ge(cleared, 1)
            pool.wait_ge(loaded, n_loaded)
            pool.tensor_copy(xs[:, :], k.xn[:, cols(0, L)]).then_inc(s["copied"], 1)
            wide = lambda ap: ap.to_broadcast([C, NH, D])

            def stage(b, par, prepares, substitutes, finishes):
                if not prepares:
                    return
                c = b * 2
                for u in chunks:
                    pool.wait_ge(s["kb_scale"], c + u + 1)
                    pool.tensor_tensor(kb[u][0:C], k_rows[par][u][0:C], wide(kb_scale[u][:, :, :]), ALU.mult)\
                        .then_inc(s["kb"], 1)
                    pool.tensor_tensor(k_rows[par][u][0:C], k_rows[par][u][0:C], wide(total["k"][u][:, :, :]),
                                       ALU.mult).then_inc(s["rows_k"], 1)
                for u in chunks:
                    pool.wait_ge(s["recip_q"], c + u + 1)
                    pool.tensor_tensor(q_rows[u][0:C], q_rows[u][0:C], wide(total["q"][u][:, :, :]), ALU.mult)\
                        .then_inc(s["rows_q"], 1)
                x_left = b * 32
                work_out(pool, x_left)
                pool.wait_ge(cleared, 1)
                pool.wait_ge(s["x_out"], x_left)
                pool.tensor_copy(lane_x[:, :, :].rearrange("p c i -> p (c i)"), unit).then_inc(s["unit"], 1)
                pool.wait_ge(s["proj_v"], c + 2)
                pool.tensor_copy(xs[:, :], k.xn[:, cols((b + 1) % B, L)]).then_inc(s["copied"], 1)
                for u in chunks:
                    pool.wait_ge(s["qk_copied"], c + u + 1)
                    pool.tensor_tensor(qk[par][u][:, 1], qk[par][u][:, 1],
                                       lower.to_broadcast([128, NP, 128]), ALU.mult).then_inc(s["qk_odd"], 1)

            stages(pool, stage)

        @block.tensor
        def _(pe):
            pe.wait_ge(loaded, n_loaded)
            pe.wait_ge(cleared, 1)

            def settle():
                pe.wait_ge(loaded, n_loaded)

            def stage(b, par, prepares, substitutes, finishes):
                c = b * 2
                done = par ^ 1
                middle = (substitutes, done, (c - 1, c))
                final = (finishes, par, (c - 3, c - 2))
                if substitutes:
                    x_ready, batches_before = b * (16 * NB), b - 1
                    work_out(pe, b, *middle[2], x_ready, batches_before)
                if finishes:
                    work_out(pe, *final[2])

                def project(name, u, bk, free, count):
                    if not prepares:
                        return
                    at, n = {"k": (NH * D, NH * D), "q": (0, NH * D), "v": (2 * NH * D, NH * D),
                             "beta": (3 * NH * D, NH)}[name]
                    if name == "k":
                        pe.wait_ge(s["copied"], b + 1)
                    pe.wait_ge(s[free], count)
                    pe.matmul(bank[0:C, bk, u * NH:u * NH + n] if name == "beta" else bank[0:C, bk, 0:n],
                              xs[:, u * C:(u + 1) * C], w[:, at:at + n],
                              start=True, stop=True).then_inc(s["proj_" + name], 1)

                def turn(name, u, src, bk, ready, free, count):
                    if not prepares:
                        return
                    pe.wait_ge(s[free], count)
                    pe.wait_ge(s[ready], c + u + 1)
                    for p in range(NP):
                        mm = pe.transpose(bank[:, bk, p * 128:(p + 1) * 128], src[:, 2 * p:2 * p + 2, :], k.ident)
                    mm.then_inc(s["turn_" + name], 1)

                def sum_a(u):
                    if not prepares:
                        return
                    settle()
                    if u == 0:
                        pe.wait_ge(s["k_t"], c + 2)
                    pe.wait_ge(s["kb_t"], c + (1 if u == 0 else 2))
                    for p in range(NP):
                        for r in range(2):
                            mm = pe.matmul(bank[:, SUM_A[u] + r, p * 128:(p + 1) * 128], k_t[u][half(r), p, :],
                                           kb_t[par][u][half(r), p, :], start=True, stop=True)
                    mm.then_inc(s["a_sum"], 1)

                def sum_qk(u, part):
                    if not prepares:
                        return
                    if part == 0:
                        settle()
                        if u == 0:
                            pe.wait_ge(s["a_t"], c + 2)
                        else:
                            pe.wait_ge(s["rhs"], c + 2)
                        pe.wait_ge(s["q_t"], c + u + 1)
                    for p in (2 * part, 2 * part + 1):
                        for r in range(2):
                            mm = pe.matmul(bank[:, SUM_QK[u][r], p * 128:(p + 1) * 128], k_t[u][half(r), p, :],
                                           q_t[par][u][half(r), p, :], start=True, stop=True)
                    if part == 1:
                        mm.then_inc(s["qk_sum"], 1)

                def solve(batch, u, g):
                    wanted, parity, upto = batch
                    if not wanted:
                        return
                    settle()
                    if u == 0 and g == 0:
                        pe.wait_ge(s["x_in"], x_ready)
                        pe.wait_ge(s["rhs"], c)
                        pe.wait_ge(s["added"], batches_before)
                    elif g == 0:
                        pe.wait_ge(s["carried"], b)
                    else:
                        pe.wait_ge(s[f"joined{g}"], upto[u])
                    for h in range(NH):
                        mm = pe.matmul(bank[rows_of(g), SOLVE, h * D:(h + 1) * D],
                                       x_t[rows_of(g), u, h % 2, h // 2, :], rhs[parity][u][rows_of(g), h, :],
                                       start=True, stop=True, tile_position=(BLOCK * g, BLOCK * g))
                    mm.then_inc(s[f"solve_sum{g}"], 1)

                def join(batch, u, g):
                    wanted, parity, upto = batch
                    if not wanted:
                        return
                    settle()
                    pe.wait_ge(s[f"solved{g - 1}"], upto[u])
                    above = slice(0, BLOCK * g)
                    for h in range(NH):
                        mm = pe.matmul(bank[rows_of(g), JOIN, h * D:(h + 1) * D],
                                       a_t[parity][above, u, h % 2, h // 2, rows_of(g)], u_new[u][above, h, :],
                                       start=True, stop=True, tile_position=(0, BLOCK * g))
                    mm.then_inc(s[f"join_sum{g}"], 1)

                def next_state():
                    if not substitutes:
                        return
                    settle()
                    pe.wait_ge(s[f"solved{NB - 1}"], middle[2][0])
                    for h in range(NH):
                        p, r = divmod(h, 2)
                        mm = pe.matmul(bank[half(r), SOLVE, p * D:(p + 1) * D], k_rows[done][0][:, h, :],
                                       u_new[0][:, h, :], start=True, stop=True)
                    mm.then_inc(s["state_sum"], 1)

                def carry():
                    if not substitutes:
                        return
                    settle()
                    pe.wait_ge(s["state"], b)
                    for p in range(NP):
                        for r in range(2):
                            mm = pe.matmul(bank[:, (SOLVE, JOIN)[r], p * D:(p + 1) * D], kb_t[done][1][half(r), p, :],
                                           state[half(r), p, :], start=True, stop=True)
                    mm.then_inc(s["carried_sum"], 1)

                def first_outputs(start, stop):
                    if not substitutes:
                        return
                    if start == 0:
                        settle()
                        pe.wait_ge(s["qk_even"], middle[2][0])
                        pe.wait_ge(s["qk_odd"], middle[2][0])
                        pe.wait_ge(s["out_t"], c - 2)
                    for h in range(start, stop):
                        p, r = divmod(h, 2)
                        mm = pe.matmul(bank[half(r), OUT, p * 128:(p + 1) * 128], u_new[0][:, h, :],
                                       qk[done][0][:, r, p, :], start=True, stop=True)
                    if stop == NH:
                        mm.then_inc(s["out_sum"], 1)

                def second_outputs():
                    if not finishes:
                        return
                    settle()
                    pe.wait_ge(s["qk_even"], final[2][1])
                    pe.wait_ge(s["qk_odd"], final[2][1])
                    pe.wait_ge(s[f"solved{NB - 1}"], final[2][1])
                    pe.wait_ge(s["out_t"], final[2][0])
                    for h in range(NH):
                        p, r = divmod(h, 2)
                        dst = bank[half(r), OUT, p * 128:(p + 1) * 128]
                        pe.matmul(dst, u_new[1][:, h, :], qk[par][1][:, r, p, :], start=True, stop=False)
                        mm = pe.matmul(dst, state[half(r), p, :], q_t[par][1][half(r), p, :],
                                       start=False, stop=True)
                    mm.then_inc(s["out_sum"], 1)

                def project_out():
                    if not finishes:
                        return
                    pe.wait_ge(s["out_t"], final[2][1])
                    for p in range(NP):
                        mm = pe.matmul(bank[:, PROJECT, 0:L], w_out[:, p, :], out_t[:, p, :],
                                       start=p == 0, stop=p == NP - 1)
                    mm.then_inc(s["projected"], 1)

                project("k", 0, PROJ_K[0], "qk_even", c)
                solve(final, 1, 2)
                project("k", 1, PROJ_K[1], "qk_copied", c)
                join(final, 1, 3)
                project("beta", 0, BETA, "q_t", c)
                project("beta", 1, BETA, "q_t", c)
                project("q", 0, PROJ_Q[0], "qk_even", c)
                solve(final, 1, 3)
                project("q", 1, PROJ_Q[1], "qk_copied", c)
                second_outputs()
                project_out()
                turn("kb", 0, kb[0], TURN_KB[0], "kb", "beta_exp", b + 1)
                turn("k", 0, k_rows[par][0], TURN_K[0], "rows_k", "shift_k", c + 1)
                turn("kb", 1, kb[1], TURN_KB[1], "kb", "shift_q", c + 1)
                turn("k", 1, k_rows[par][1], TURN_K[1], "rows_k", "shift_k", c + 2)
                sum_a(0)
                sum_a(1)
                solve(middle, 0, 0)
                turn("q", 0, q_rows[0], TURN_Q[0], "rows_q", "shift_q", c + 2)
                join(middle, 0, 1)
                project("v", 0, PROJ_V[0], "a_t", c + 1)
                solve(middle, 0, 1)
                project("v", 1, PROJ_V[1], "a_t", c + 1)
                join(middle, 0, 2)
                turn("q", 1, q_rows[1], TURN_Q[1], "rows_q", "a_t", c + 2)
                solve(middle, 0, 2)
                sum_qk(0, 0)
                join(middle, 0, 3)
                sum_qk(0, 1)
                solve(middle, 0, 3)
                sum_qk(1, 0)
                next_state()
                first_outputs(0, NH // 4)
                carry()
                first_outputs(NH // 4, NH // 2)
                solve(middle, 1, 0)
                first_outputs(NH // 2, NH)
                join(middle, 1, 1)
                sum_qk(1, 1)
                solve(middle, 1, 1)
                join(middle, 1, 2)

            stages(pe, stage)

        @block.scalar
        def _(act):
            load_exp_ln(act)

            def stage(b, par, prepares, substitutes, finishes):
                c = b * 2

                def exp(name, u, rows):
                    if prepares:
                        act.wait_ge(s["shift_" + name], c + u + 1)
                        act.activation(rows[0:C], rows[0:C], ACT.Exp).then_inc(s["exp_" + name], 1)

                def turned(name, u, bk, dst):
                    if prepares:
                        act.wait_ge(s["turn_" + name], c + u + 1)
                        act.activation(dst[:, :, :], pairs(bank[:, bk, :]), ACT.Copy).then_inc(s[name + "_t"], 1)

                def copy_a(u):
                    if prepares:
                        act.wait_ge(s["a_sum"], c + u + 1)
                        act.activation(a_t[par][:, u].rearrange("j r p i -> j r (p i)"),
                                       bank[:, SUM_A[u]:SUM_A[u] + 2, :], ACT.Copy).then_inc(s["a_t"], 1)

                def copy_qk(u):
                    if prepares:
                        act.wait_ge(s["qk_sum"], c + u + 1)
                        act.activation(qk[par][u][:, 1], pairs(bank[:, SUM_QK[u][1], :]), ACT.Copy)\
                            .then_inc(s["qk_copied"], 1)

                def solved(batch, u, g):
                    wanted, upto = batch
                    if wanted:
                        act.wait_ge(s[f"solve_sum{g}"], upto[u])
                        act.activation(u_new[u][rows_of(g)], heads(bank[rows_of(g), SOLVE, :]), ACT.Copy)\
                            .then_inc(s[f"solved{g}"], 1)

                def outputs(u, batches):
                    act.wait_ge(s["out_sum"], batches * 2 + u + 1)
                    act.wait_ge(s["projected"], batches)
                    act.activation(out_t[:, :, u * C:(u + 1) * C], pairs(bank[:, OUT, :])[:, :, 0:C],
                                   ACT.Copy).then_inc(s["out_t"], 1)

                middle = (substitutes, (c - 1, c))
                final = (finishes, (c - 3, c - 2))
                solved(final, 1, 2)
                if prepares:
                    act.wait_ge(s["proj_beta"], c + 2)
                    act.activation(beta[:, :, :, 0], bank[0:C, BETA, 0:LANES * NH].rearrange("p (u h) -> p u h", u=LANES),
                                   ACT.Exp, scale=-1.0).then_inc(s["beta_exp"], 1)
                exp("k", 0, k_rows[par][0])
                solved(final, 1, 3)
                exp("k", 1, k_rows[par][1])
                if finishes:
                    outputs(1, b - 2)
                exp("q", 0, q_rows[0])
                exp("q", 1, q_rows[1])
                turned("kb", 0, TURN_KB[0], kb_t[par][0])
                turned("k", 0, TURN_K[0], k_t[0])
                turned("kb", 1, TURN_KB[1], kb_t[par][1])
                turned("k", 1, TURN_K[1], k_t[1])
                copy_a(0)
                copy_a(1)
                solved(middle, 0, 0)
                turned("q", 0, TURN_Q[0], q_t[par][0])
                solved(middle, 0, 1)
                turned("q", 1, TURN_Q[1], q_t[par][1])
                solved(middle, 0, 2)
                copy_qk(0)
                solved(middle, 0, 3)
                if substitutes:
                    act.wait_ge(s["state_sum"], b)
                    act.activation(state[:, :, :], bank[:, SOLVE, 0:NP * D].rearrange("p (n d) -> p n d", n=NP),
                                   ACT.Copy).then_inc(s["state"], 1)
                solved(middle, 1, 0)
                if substitutes:
                    outputs(0, b - 1)
                solved(middle, 1, 1)
                copy_qk(1)

            stages(act, stage)

        @block.vector
        def _(dve):
            dve.wait_ge(loaded, n_loaded)
            dve.wait_ge(cleared, 1)
            wide = lambda ap: ap.to_broadcast([C, NH, D])

            def stage(b, par, prepares, substitutes, finishes):
                c = b * 2
                done = par ^ 1
                bank_of = {"k": PROJ_K, "q": PROJ_Q}
                rows = {"k": k_rows[par], "q": q_rows}

                def maximum(n, u):
                    if prepares:
                        dve.wait_ge(s["proj_" + n], c + u + 1)
                        dve.tensor_reduce(top[n][u][:, :, :], heads(bank[0:C, bank_of[n][u], :]), AX, ALU.max)\
                            .then_inc(s["top_" + n], 1)

                def shift(n, u):
                    if prepares:
                        dve.wait_ge(s["top_" + n], c + u + 1)
                        dve.tensor_tensor(rows[n][u][0:C], heads(bank[0:C, bank_of[n][u], :]),
                                          wide(top[n][u][:, :, :]), ALU.subtract).then_inc(s["shift_" + n], 1)

                def sums(n, u):
                    if prepares:
                        dve.wait_ge(s["exp_" + n], c + u + 1)
                        dve.tensor_reduce(total[n][u][:, :, :], rows[n][u][0:C], AX, ALU.add)\
                            .then_inc(s["total_" + n], 1)

                def inverse_sums(n, u):
                    if prepares:
                        dve.wait_ge(s["total_" + n], c + u + 1)
                        dve.reciprocal(total[n][u][:, :, :], total[n][u][:, :, :]).then_inc(s["recip_" + n], 1)

                def scale_kb(u):
                    if prepares:
                        dve.wait_ge(s["beta"], b + 1)
                        dve.wait_ge(s["recip_k"], c + u + 1)
                        dve.tensor_tensor(kb_scale[u][:, :, :], total["k"][u][:, :, :], beta[:, u], ALU.mult)\
                            .then_inc(s["kb_scale"], 1)

                def right_hand_side(u):
                    if prepares:
                        dve.wait_ge(s["proj_v"], c + u + 1)
                        dve.tensor_tensor(rhs[par][u][0:C], heads(bank[0:C, PROJ_V[u], :]), wide(beta[:, u]), ALU.mult)\
                            .then_inc(s["rhs"], 1)

                middle = (substitutes, done, (c - 1, c))
                final = (finishes, par, (c - 3, c - 2))

                def joined(batch, u, g):
                    wanted, parity, upto = batch
                    if wanted:
                        at = rhs[parity][u][rows_of(g)]
                        dve.wait_ge(s[f"join_sum{g}"], upto[u])
                        dve.tensor_tensor(at, at, heads(bank[rows_of(g), JOIN, :]), ALU.subtract)\
                            .then_inc(s[f"joined{g}"], 1)

                def mask_qk(u):
                    if prepares:
                        dve.wait_ge(s["qk_sum"], c + u + 1)
                        dve.tensor_tensor(qk[par][u][:, 0], pairs(bank[:, SUM_QK[u][0], :]),
                                          lower.to_broadcast([128, NP, 128]), ALU.mult).then_inc(s["qk_even"], 1)

                def invert(batch, start, stop):
                    for j in range(start, stop):
                        shape = [2 * LANES_OF, j // 2 + 1, BLOCK - 1 - j]
                        if j == 0:
                            dve.wait_ge(s["a_in"], batch * 32 + 32)
                            dve.wait_ge(s["unit"], batch + 1)
                        else:
                            dve.wait_ge(inverted[j - 1], batch + 1)
                        below = lane_x[:, 0:shape[1], j + 1:BLOCK]
                        p = lane_p[:, 0:shape[1], 0:shape[2]]
                        dve.tensor_tensor(p, lane_a[:, j:j + 1, j + 1:BLOCK].to_broadcast(shape),
                                          lane_x[:, 0:shape[1], j:j + 1].to_broadcast(shape), ALU.mult)\
                            .then_inc(product[j], 1)
                        dve.wait_ge(product[j], batch + 1)
                        dve.tensor_tensor(below, below, p, ALU.subtract).then_inc(inverted[j], 1)

                def begin(start, stop):
                    if prepares:
                        invert(b, start, stop)

                def go_on(start, stop):
                    if substitutes:
                        invert(b - 1, start, stop)

                maximum("k", 0)
                shift("k", 0)
                joined(final, 1, 3)
                maximum("k", 1)
                shift("k", 1)
                go_on(25, 26)
                if prepares:
                    dve.wait_ge(s["beta_exp"], b + 1)
                    dve.tensor_scalar(beta[:, :, :, :], beta[:, :, :, :], 1.0, None, ALU.add)\
                        .then_inc(s["beta_one"], 1)
                sums("k", 0)
                if prepares:
                    dve.wait_ge(s["beta_one"], b + 1)
                    dve.reciprocal(beta[:, :, :, :], beta[:, :, :, :]).then_inc(s["beta"], 1)
                inverse_sums("k", 0)
                sums("k", 1)
                scale_kb(0)
                inverse_sums("k", 1)
                go_on(26, 27)
                scale_kb(1)
                maximum("q", 0)
                go_on(27, 28)
                shift("q", 0)
                maximum("q", 1)
                go_on(28, 29)
                shift("q", 1)
                go_on(29, BLOCK - 1)
                sums("q", 0)
                sums("q", 1)
                inverse_sums("q", 0)
                inverse_sums("q", 1)
                if finishes:
                    r_at = k.r[:, cols(b - 2, L)]
                    dve.wait_ge(s["projected"], b - 1)
                    dve.tensor_tensor(r_at, bank[:, PROJECT, 0:L], r_at, ALU.add).then_inc(s["added"], 1)
                joined(middle, 0, 1)
                right_hand_side(0)
                joined(middle, 0, 2)
                right_hand_side(1)
                begin(0, 2)
                begin(2, 6)
                joined(middle, 0, 3)
                mask_qk(0)
                begin(6, 16)
                if substitutes:
                    v = rhs[done][1][:, :, :].rearrange("p (n r) d -> p r n d", r=2)
                    dve.wait_ge(s["carried_sum"], b)
                    dve.tensor_tensor(v, v, bank[:, 0:2, 0:NP * D].rearrange("p r (n d) -> p r n d", n=NP),
                                      ALU.subtract).then_inc(s["carried"], 1)
                begin(16, 18)
                joined(middle, 1, 1)
                begin(18, 21)
                mask_qk(1)
                begin(21, 23)
                joined(middle, 1, 2)
                begin(23, 25)

            stages(dve, stage)
            if layer == 1:
                dve.wait_ge(s["added"], B)
                dve.tensor_tensor(k.h[:, :], k.h[:, :], k.r[:, :], ALU.add)


MASK_COLS = 128 + 16 * 32


def delta_masks():
    m = np.zeros((128, MASK_COLS), np.float32)
    m[:, 0:128] = np.arange(128)[:, None] <= np.arange(128)[None, :]
    for odd in range(2):
        m[64 * odd:64 * odd + 64, 128:] = np.eye(32, dtype=np.float32)[odd::2].reshape(-1)
    return m



def experts1(k):
    with ExitStack() as weights:
        (gate_w,), gate_loaded = k.ahead(weights, "route1", {"w": ([H, E], "gate_w")})
        tiles = k.ahead(weights, "ex1", {
            "w1": ([H, E, H], "w1"), "w2": ([H, E, H], "w2"), "sw1": ([H, H], "sw1"),
            "sw2": ([H, H], "sw2"), "b2": ([E, H], "b2"), "vec": ([H, E + 2], "ffn1_vec")})
        block_norm(k)
        router(k, "route1", gate_w, None, gate_loaded, scores=True)
        run_experts1(k, *tiles)


def run_experts1(k, weights, loaded):
    nc = k.nc
    with ExitStack() as ctx:
        def sb(name, shape, dt=F32):
            return ctx.enter_context(nc.sbuf_tensor(f"ex1_{name}", shape, dt))

        def sem(name):
            return k.semaphore(ctx, f"ex1_{name}")

        w1, w2, sw1, sw2, b2, vec = weights
        relu = [sb(f"relu{n}", [H, W2]) for n in range(2)]
        weighted = [sb(f"weighted{n}", [H, W2]) for n in range(2)]
        shared = sb("shared", [H, W2])
        psum = lambda n: ctx.enter_context(nc.psum_tensor(f"ex1_{n}", [128, 512], F32))
        hidden, weight = [psum("hidden0"), psum("hidden1")], [psum("weight0"), psum("weight1")]
        hidden_shared, total = psum("hidden_shared"), psum("total")
        s = {n: sem(n) for n in ("hidden", "spread", "relu", "weighted", "summed", "shared_in",
                                 "shared", "total", "added")}
        block = ctx.enter_context(nc.Block())

        @block.tensor
        def _(pe):
            pe.wait_ge(loaded, 16 * 6)
            with pe.Fori(0, NT) as t:
                done = t * E
                x = k.xn[:, cols(t, W2)]

                def second(e):
                    pe.wait_ge(s["weighted"], done + e + 1)
                    pe.matmul(total[:, 0:W2], w2[:, e, :], weighted[e % 2][:, :], start=False,
                              stop=False).then_inc(s["summed"], 1)

                pe.wait_ge(s["shared"], t)
                pe.matmul(hidden_shared[:, 0:W2], sw1[:, :], x, start=True, stop=True)\
                    .then_inc(s["shared_in"], 1)
                for e in range(E):
                    if e >= 2:
                        pe.wait_ge(s["relu"], done + e - 1)
                        pe.wait_ge(s["weighted"], done + e - 1)
                    elif e == 0:
                        pe.wait_ge(s["weighted"], done)
                    pe.matmul(hidden[e % 2][:, 0:W2], w1[:, e, :], x, start=True, stop=True)\
                        .then_inc(s["hidden"], 1)
                    pe.matmul(weight[e % 2][:, 0:W2], k.select[:, e:e + 1].to_broadcast([128, 128]),
                              k.wt_parts[:, cols(t, W2)], start=True, stop=True).then_inc(s["spread"], 1)
                    if e == 0:
                        pe.wait_ge(s["added"], t)
                        pe.matmul(total[:, 0:W2], b2[:, :], k.wt[:, cols(t, W2)], start=True, stop=False)
                    else:
                        second(e - 1)
                second(E - 1)
                pe.wait_ge(s["shared"], t + 1)
                pe.matmul(total[:, 0:W2], sw2[:, :], shared[:, :], start=False, stop=True)\
                    .then_inc(s["total"], 1)

        @block.scalar
        def _(act):
            act.wait_ge(loaded, 16 * 6)
            with act.Fori(0, NT) as t:
                done = t * E
                act.wait_ge(s["shared_in"], t + 1)
                act.wait_ge(s["total"], t)
                act.activation(shared[:, :], hidden_shared[:, 0:W2], ACT.Relu, bias=vec[:, E:E + 1])\
                    .then_inc(s["shared"], 1)
                for e in range(E):
                    act.wait_ge(s["hidden"], done + e + 1)
                    if e >= 2:
                        act.wait_ge(s["weighted"], done + e - 1)
                    act.activation(relu[e % 2][:, :], hidden[e % 2][:, 0:W2], ACT.Relu,
                                   bias=vec[:, e:e + 1]).then_inc(s["relu"], 1)

        @block.vector
        def _(dve):
            dve.wait_ge(loaded, 16 * 6)
            with dve.Fori(0, NT) as t:
                done = t * E
                for e in range(E):
                    dve.wait_ge(s["relu"], done + e + 1)
                    dve.wait_ge(s["spread"], done + e + 1)
                    if e >= 2:
                        dve.wait_ge(s["summed"], done + e - 1)
                    dve.tensor_tensor(weighted[e % 2][:, :], relu[e % 2][:, :], weight[e % 2][:, 0:W2],
                                      ALU.mult).then_inc(s["weighted"], 1)
                dve.wait_ge(s["total"], t + 1)
                dve.scalar_tensor_tensor(k.h[:, cols(t, W2)], total[:, 0:W2], vec[:, E + 1:E + 2],
                                         k.h[:, cols(t, W2)], ALU.add, ALU.add).then_inc(s["added"], 1)



def store(k):
    nc = k.nc
    with ExitStack() as ctx:
        stored = k.semaphore(ctx, "stored")
        block = ctx.enter_context(nc.Block())

        @block.sync
        def _(sp):
            sp.dma_start(k.out, k.h[:, :]).then_inc(stored, 16)
            sp.wait_ge(stored, 16)


PHASES = [setup, token_mixer, attention0, experts0, attention1, experts1, store]


def build(nc, ins, out, phases=None):
    k = Kit(nc, ins, out)
    with ExitStack() as ctx:
        k.h = ctx.enter_context(nc.sbuf_tensor("h", [H, T], F32))
        k.xn = ctx.enter_context(nc.sbuf_tensor("xn", [H, T], F32))
        k.wt = ctx.enter_context(nc.sbuf_tensor("wt", [E, T], F32))
        k.wt_parts = ctx.enter_context(nc.sbuf_tensor("wt_parts", [128, T], BF16))
        k.select = ctx.enter_context(nc.sbuf_tensor("select", [128, 32], BF16))
        k.const = ctx.enter_context(nc.sbuf_tensor("const", [128, CONST_COLS], F32))
        k.ident = k.const[:, 0:128]
        k.centre = k.const[:, 128:256]
        k.average = k.const[:, 256:384]
        k.eps = k.const[:, 384:385]
        for phase in phases or PHASES:
            phase(k)
        k.end_phase(k.lasting)


CONST_COLS = 385 + 32 + 8


def constants():
    c = np.zeros((128, CONST_COLS), np.float32)
    c[:, 0:128] = np.eye(128)
    c[:, 128:256] = np.eye(128) - 1.0 / H
    c[:, 256:384] = 1.0 / H
    c[:, 384] = EPS
    for r in range(32):
        for part in PARTS:
            c[part + r, 385 + r] = 1.0
    c[:, 417:425] = np.arange(E)
    return c


def columns(*vectors):
    out = np.zeros((128, len(vectors)), np.float32)
    for n, v in enumerate(vectors):
        out[:len(v), n] = v
    return out


def layout(p):
    t = lambda a: np.ascontiguousarray(a)
    a = {"const": constants()}
    a["x"] = t(p["x"].transpose(2, 0, 1).reshape(H, B * S))
    a["w_compress"] = t(p["L0_tok_w_compress"][:, :, 0].T)
    a["w_main"] = np.zeros((BN, 3, H), np.float32)
    a["w_main"][:, :, :BN] = p["L0_tok_w_main"].transpose(1, 2, 0)
    a["w_expand"] = t(p["L0_tok_w_expand"][:, :, 0].T)
    a["tok_up"] = t(p["L0_tok_w_ff1"].T)
    a["tok_down"] = t(p["L0_tok_w_ff2"].T)
    a["tok_vec"] = columns(*(p["L0_tok_" + n] for n in (
        "b_compress", "b_main", "b_ff1", "b_expand", "b_ff2", "g_conv_norm", "b_conv_norm",
        "g_ff_norm", "b_ff_norm")))
    a["mk"] = t(p["L0_attn_mk_w"].T)
    a["mv"] = t(p["L0_attn_mv_w"])
    a["ea_vec"] = columns(p["L0_attn_ln_g"], p["L0_attn_ln_b"])
    halves = lambda m: t(m.reshape((2, H) + m.shape[1:]).swapaxes(0, 1))
    a["in_proj_x"] = halves(p["L0_attn_in_proj_w"][:DI])
    a["in_proj_z"] = t(p["L0_attn_in_proj_w"][DI:].T.reshape(H, 2, H))
    a["conv_w"] = halves(p["L0_attn_conv_w"])
    x_proj = halves(p["L0_attn_x_proj_w"].T)
    a["x_proj_dt"] = t(x_proj[:, :, :DR])
    a["x_proj_bc"] = np.zeros((H, 2, 128), np.float32)
    for at in PARTS:
        a["x_proj_bc"][:, :, at:at + 2 * DS] = x_proj[:, :, DR:]
    a["dt_proj"] = t(p["L0_attn_dt_proj_w"].T.reshape(DR, 2, H))
    a["out_proj"] = halves(p["L0_attn_out_proj_w"].T)
    a["mamba_vec"] = halves(np.stack([p["L0_attn_" + n] for n in ("conv_b", "dt_proj_b", "D")], 1))
    a["a_log"] = halves(p["L0_attn_A_log"])
    a["router_w"] = t(p["L0_ffn_router_w"])
    a["router_b"] = t(np.broadcast_to(p["L0_ffn_router_b"], (C, E)))
    a["gate_up"] = t(p["L0_ffn_gate_up_proj"].transpose(1, 0, 2))
    a["gate_up_bias"] = t(p["L0_ffn_gate_up_proj_bias"].reshape(E, 4, H).transpose(2, 0, 1))
    a["down"] = t(p["L0_ffn_down_proj"].reshape(E, 2, H, H).transpose(2, 0, 1, 3))
    a["down_bias"] = t(p["L0_ffn_down_proj_bias"])
    a["masks"] = delta_masks()
    a["ip_w"] = t(p["L1_attn_ip_w"].T)
    a["ip_vec"] = columns(p["L1_attn_ip_b"], p["L1_attn_fw_ln_g"][0], p["L1_attn_fw_ln_b"][0])
    a["ff_w1"] = t(p["L1_attn_ff_w1"].T.reshape(H, FF // H, H))
    a["ff_w2"] = t(p["L1_attn_ff_w2"].T.reshape(FF // H, H, H).transpose(1, 0, 2))
    a["ff_vec"] = columns(p["L1_attn_ff_ln_g"], p["L1_attn_ff_ln_b"], p["L1_attn_fw_ln_g"][1],
                          p["L1_attn_fw_ln_b"][1], p["L1_attn_ff_b2"],
                          *p["L1_attn_ff_b1"].reshape(FF // H, H))
    for n in range(2):
        slow = p["L1_attn_fw_slow_w"][n].reshape(NH, 3 * D + 1, H)
        parts = [slow[:, at:at + m].reshape(NH * m, H) for at, m in ((0, D), (D, D), (2 * D, D), (3 * D, 1))]
        a[f"slow_w{n}"] = t(np.concatenate(parts).T)
        a[f"fw_out{n}"] = t(p["L1_attn_fw_out_w"][n].T.reshape(NH // 2, 2 * D, H).transpose(1, 0, 2))
    a["gate_w"] = t(p["L1_ffn_gate_w"].T)
    a["w1"] = t(p["L1_ffn_w1"].transpose(1, 0, 2))
    a["w2"] = t(p["L1_ffn_w2"].transpose(1, 0, 2))
    a["sw1"] = t(p["L1_ffn_sw1"])
    a["sw2"] = t(p["L1_ffn_sw2"])
    a["b2"] = t(p["L1_ffn_b2"])
    a["ffn1_vec"] = t(np.concatenate([p["L1_ffn_b1"].T, columns(p["L1_ffn_sb1"], p["L1_ffn_sb2"])], 1))
    return a


def kernel(**inputs):
    import concourse.bacc as bacc
    from concourse.bass_utils import run_bass_kernel_spmd

    arrays = layout({n: np.asarray(a) for n, a in inputs.items()})
    nc = bacc.Bacc("TRN2", target_bir_lowering=False, num_devices=1)
    ins = {n: nc.dram_tensor(f"in_{n}", a.shape, mybir.dt.from_np(a.dtype), kind="ExternalInput").ap()
           for n, a in arrays.items()}
    out = nc.dram_tensor("out", (H, T), F32, kind="ExternalOutput").ap()
    build(nc, ins, out)
    r = run_bass_kernel_spmd(nc, [{f"in_{n}": a for n, a in arrays.items()}], core_ids=[0])
    return np.ascontiguousarray(r.results[0]["out"].reshape(H, B, L).transpose(1, 2, 0))
```
